# Optimizing a Trainium2 kernel written in Bass

```python
import numpy as np
import jax
import jax.numpy as jnp

def _softmax(x, axis=-1):
    return jax.nn.softmax(x, axis=axis)

def _gelu(x):
    return jax.nn.gelu(x, approximate=True)

def _silu(x):
    return jax.nn.silu(x)

def _sigmoid(x):
    return jax.nn.sigmoid(x)

def _layernorm(x, axis=-1, eps=1e-05):
    m = jnp.mean(x, axis=axis, keepdims=True)
    v = jnp.var(x, axis=axis, keepdims=True)
    return (x - m) / jnp.sqrt(v + eps)

def _scatter_add(tgt, idx, src, axis=0):
    return tgt.at[idx].add(src)

def _segment_sum(src, seg, n):
    return jax.ops.segment_sum(src, seg, n)
kernel_name = 'mk_xattn_ffn_d2_seqx_r8_24089a'

def setup_inputs(seed: int=0):
    np.random.seed(seed)
    _w = jnp.asarray

    def _rec_inputs():
        import jax
        import jax.numpy as jnp
        _rk = jax.random.key(seed)
        x = 7.22e-05 + 1 * jax.random.normal(jax.random.fold_in(_rk, 1), (1, 1024, 128), jnp.float32)
        _lenS = 1024 - jax.random.randint(jax.random.fold_in(_rk, 7), (1,), 0, max(1, 1024 // 4) + 1, jnp.int32)
        _lenS2 = 6404 - jax.random.randint(jax.random.fold_in(_rk, 8), (1,), 0, max(1, 6404 // 4) + 1, jnp.int32)
        _ctx_1024P = jax.random.normal(jax.random.fold_in(_rk, 11), (1, 16, 128), jnp.float32)
        _ctx_1024c = jax.random.dirichlet(jax.random.fold_in(_rk, 511), 0.3 * jnp.ones((16,), jnp.float32), (1, 6404))
        _ctx_1024t = jnp.einsum('bsk,bkd->bsd', _ctx_1024c, _ctx_1024P)
        _ctx_1024t = _ctx_1024t * jax.lax.rsqrt(jnp.mean(jnp.square(_ctx_1024t)) + 1e-12) * 0.953939
        ctx_1024 = 4.13588e-05 + 0.999923 * (_ctx_1024t + 0.3 * jax.random.normal(jax.random.fold_in(_rk, 611), (1, 6404, 128), jnp.float32))
        return (x, ctx_1024)
    x, ctx_1024 = _rec_inputs()

    def _L0_xattn_setup():
        import jax, jax.numpy as jnp
        import numpy as np
        EMBED = 128
        HEADS = 16
        HEAD_DIM = EMBED // HEADS
        key = jax.random.key(seed)
        ks = jax.random.split(key, 11)
        B, S, D = (4, 256, EMBED)
        scale = 1.0 / np.sqrt(D)
        inp = {'query': jax.random.normal(ks[0], (B, S, D), dtype=jnp.float32), 'key': jax.random.normal(ks[1], (B, S, D), dtype=jnp.float32), 'value': jax.random.normal(ks[2], (B, S, D), dtype=jnp.float32), 'Wq': jax.random.normal(ks[3], (D, D), dtype=jnp.float32) * scale, 'bq': jnp.zeros((D,), dtype=jnp.float32), 'Wk': jax.random.normal(ks[4], (D, D), dtype=jnp.float32) * scale, 'bk': jnp.zeros((D,), dtype=jnp.float32), 'Wv': jax.random.normal(ks[5], (D, D), dtype=jnp.float32) * scale, 'bv': jnp.zeros((D,), dtype=jnp.float32), 'Wo': jax.random.normal(ks[6], (D, D), dtype=jnp.float32) * scale, 'bo': jnp.zeros((D,), dtype=jnp.float32)}
        return inp
    _L0_xattn_all = _L0_xattn_setup()
    _L0_xattn_in = {k: v for k, v in _L0_xattn_all.items() if k in ('Wq', 'bq', 'Wk', 'bk', 'Wv', 'bv', 'Wo', 'bo')}
    del _L0_xattn_all

    def _L0_ffn_setup():
        import jax, jax.numpy as jnp
        import numpy as np
        TOP_K = 2
        key = jax.random.key(seed)
        k1, k2, k3, k4 = jax.random.split(key, 4)
        B_, S, D = (4, 1024, 128)
        E, R = (8, 16)
        x = jax.random.normal(k1, (B_, S, D), dtype=jnp.float32)
        Wg = jax.random.normal(k2, (D, E), dtype=jnp.float32) * 0.02
        A = jax.random.normal(k3, (E, D, R), dtype=jnp.float32) * 0.02
        Bm = jax.random.normal(k4, (E, R, D), dtype=jnp.float32) * 0.02
        return {'x': x, 'Wg': Wg, 'A': A, 'B': Bm}
    _L0_ffn_all = _L0_ffn_setup()
    _L0_ffn_in = {k: v for k, v in _L0_ffn_all.items() if k in ('Wg', 'A', 'B')}
    del _L0_ffn_all

    def _L1_xattn_setup():
        import jax, jax.numpy as jnp
        import numpy as np
        DIM = 128
        HEADS = 16
        DIM_HEAD = 64
        FF_MULT = 4
        CTX_DIM = 128
        INNER = HEADS * DIM_HEAD
        FF_INNER = DIM * FF_MULT
        FUSED = INNER + 2 * DIM_HEAD + 2 * FF_INNER
        SCALE = DIM_HEAD ** (-0.5)

        def layer_norm(x, gamma, eps=1e-05):
            mu = jnp.mean(x, axis=-1, keepdims=True)
            var = jnp.var(x, axis=-1, keepdims=True)
            return (x - mu) * jax.lax.rsqrt(var + eps) * gamma

        def swiglu(x):
            a, gate = jnp.split(x, 2, axis=-1)
            return jax.nn.silu(gate) * a

        def parallel_block(x, gamma, W_fused, W_attn_out, W_ff_out):
            B, N, D = x.shape
            h = layer_norm(x, gamma)
            fused = h @ W_fused
            q = fused[..., :INNER]
            k = fused[..., INNER:INNER + DIM_HEAD]
            v = fused[..., INNER + DIM_HEAD:INNER + 2 * DIM_HEAD]
            ff = fused[..., INNER + 2 * DIM_HEAD:]
            q = q.reshape(B, N, HEADS, DIM_HEAD).transpose(0, 2, 1, 3) * SCALE
            sim = jnp.einsum('bhid,bjd->bhij', q, k)
            causal = jnp.triu(jnp.ones((N, N), dtype=bool), k=1)
            neg = -jnp.finfo(sim.dtype).max
            sim = jnp.where(causal, neg, sim)
            sim = sim - jax.lax.stop_gradient(jnp.max(sim, axis=-1, keepdims=True))
            attn = jax.nn.softmax(sim, axis=-1)
            out = jnp.einsum('bhij,bjd->bhid', attn, v)
            out = out.transpose(0, 2, 1, 3).reshape(B, N, INNER)
            return out @ W_attn_out + swiglu(ff) @ W_ff_out

        def cross_attention(x, context, gamma, ctx_gamma, W_q, W_kv, W_out):
            B, N, D = x.shape
            xq = layer_norm(x, gamma)
            c = layer_norm(context, ctx_gamma)
            q = (xq @ W_q).reshape(B, N, HEADS, DIM_HEAD).transpose(0, 2, 1, 3) * SCALE
            kv = c @ W_kv
            k, v = (kv[..., :DIM_HEAD], kv[..., DIM_HEAD:])
            sim = jnp.einsum('bhid,bjd->bhij', q, k)
            attn = jax.nn.softmax(sim, axis=-1)
            out = jnp.einsum('bhij,bjd->bhid', attn, v)
            out = out.transpose(0, 2, 1, 3).reshape(B, N, INNER)
            return out @ W_out
        key = jax.random.key(seed)
        ks = jax.random.split(key, 12)
        w = lambda k, shape: jax.random.normal(k, shape, dtype=jnp.float32) * 0.02
        return {'x': jax.random.normal(ks[0], (4, 128, DIM), dtype=jnp.float32), 'context': jax.random.normal(ks[1], (4, 64, CTX_DIM), dtype=jnp.float32), 'ptb_gamma': jnp.ones((DIM,), dtype=jnp.float32), 'W_fused': w(ks[2], (DIM, FUSED)), 'W_attn_out': w(ks[3], (INNER, DIM)), 'W_ff_out': w(ks[4], (FF_INNER, DIM)), 'ca_gamma': jnp.ones((DIM,), dtype=jnp.float32), 'ca_ctx_gamma': jnp.ones((CTX_DIM,), dtype=jnp.float32), 'W_q': w(ks[5], (DIM, INNER)), 'W_kv': w(ks[6], (CTX_DIM, 2 * DIM_HEAD)), 'W_out': w(ks[7], (INNER, DIM))}
    _L1_xattn_all = _L1_xattn_setup()
    _L1_xattn_in = {k: v for k, v in _L1_xattn_all.items() if k in ('ptb_gamma', 'W_fused', 'W_attn_out', 'W_ff_out', 'ca_gamma', 'ca_ctx_gamma', 'W_q', 'W_kv', 'W_out')}
    del _L1_xattn_all

    def _L1_ffn_setup():
        import jax, jax.numpy as jnp
        import numpy as np
        BLOCK = 32
        W_BITS = 4
        ACT_BITS = 16

        def act_qdq(x):
            qmax = 2.0 ** (ACT_BITS - 1) - 1.0
            scale = jnp.maximum(jnp.max(jnp.abs(x)) / qmax, 1e-12)
            return jnp.clip(jnp.round(x / scale), -qmax - 1.0, qmax) * scale

        def fixed_qdq_u16(x):
            scale = 1.0 / 65536.0
            return jnp.clip(jnp.round(x / scale), 0.0, 65535.0) * scale

        def lpbq_dequant(w):
            O, I = w.shape
            qmax = 2.0 ** (W_BITS - 1) - 1.0
            wb = w.reshape(O, I // BLOCK, BLOCK)
            s = jnp.maximum(jnp.max(jnp.abs(wb), axis=-1, keepdims=True) / qmax, 1e-12)
            wq = jnp.clip(jnp.round(wb / s), -qmax - 1.0, qmax) * s
            return wq.reshape(O, I)
        key = jax.random.key(seed)
        k1, k2, k3, k4 = jax.random.split(key, 4)
        B, S, H, I = (2, 512, 128, 384)
        x = jax.random.normal(k1, (B, S, H), jnp.float32)
        w_gate = jax.random.normal(k2, (I, H), jnp.float32) * 0.02
        w_up = jax.random.normal(k3, (I, H), jnp.float32) * 0.02
        w_down = jax.random.normal(k4, (H, I), jnp.float32) * 0.02
        return {'x': x, 'w_gate': w_gate, 'w_up': w_up, 'w_down': w_down}
    _L1_ffn_all = _L1_ffn_setup()
    _L1_ffn_in = {k: v for k, v in _L1_ffn_all.items() if k in ('w_gate', 'w_up', 'w_down')}
    del _L1_ffn_all
    return {'x': x, 'ctx_1024': ctx_1024, 'L0_xattn_Wq': _L0_xattn_in['Wq'], 'L0_xattn_bq': _L0_xattn_in['bq'], 'L0_xattn_Wk': _L0_xattn_in['Wk'], 'L0_xattn_bk': _L0_xattn_in['bk'], 'L0_xattn_Wv': _L0_xattn_in['Wv'], 'L0_xattn_bv': _L0_xattn_in['bv'], 'L0_xattn_Wo': _L0_xattn_in['Wo'], 'L0_xattn_bo': _L0_xattn_in['bo'], 'L0_ffn_Wg': _L0_ffn_in['Wg'], 'L0_ffn_A': _L0_ffn_in['A'], 'L0_ffn_B': _L0_ffn_in['B'], 'L1_xattn_ptb_gamma': _L1_xattn_in['ptb_gamma'], 'L1_xattn_W_fused': _L1_xattn_in['W_fused'], 'L1_xattn_W_attn_out': _L1_xattn_in['W_attn_out'], 'L1_xattn_W_ff_out': _L1_xattn_in['W_ff_out'], 'L1_xattn_ca_gamma': _L1_xattn_in['ca_gamma'], 'L1_xattn_ca_ctx_gamma': _L1_xattn_in['ca_ctx_gamma'], 'L1_xattn_W_q': _L1_xattn_in['W_q'], 'L1_xattn_W_kv': _L1_xattn_in['W_kv'], 'L1_xattn_W_out': _L1_xattn_in['W_out'], 'L1_ffn_w_gate': _L1_ffn_in['w_gate'], 'L1_ffn_w_up': _L1_ffn_in['w_up'], 'L1_ffn_w_down': _L1_ffn_in['w_down']}

def reference(x, ctx_1024, L0_xattn_Wq, L0_xattn_bq, L0_xattn_Wk, L0_xattn_bk, L0_xattn_Wv, L0_xattn_bv, L0_xattn_Wo, L0_xattn_bo, L0_ffn_Wg, L0_ffn_A, L0_ffn_B, L1_xattn_ptb_gamma, L1_xattn_W_fused, L1_xattn_W_attn_out, L1_xattn_W_ff_out, L1_xattn_ca_gamma, L1_xattn_ca_ctx_gamma, L1_xattn_W_q, L1_xattn_W_kv, L1_xattn_W_out, L1_ffn_w_gate, L1_ffn_w_up, L1_ffn_w_down):
    import jax
    import jax.numpy as jnp

    def _L0_xattn_ref(query, key, value, Wq, bq, Wk, bk, Wv, bv, Wo, bo):
        import jax, jax.numpy as jnp
        import numpy as np
        EMBED = 128
        HEADS = 16
        HEAD_DIM = EMBED // HEADS
        B, S, D = query.shape
        H, Hd = (HEADS, HEAD_DIM)

        def split_heads(x):
            return x.reshape(B, -1, H, Hd).transpose(0, 2, 1, 3)
        q = split_heads(query @ Wq.T + bq)
        k = split_heads(key @ Wk.T + bk)
        v = split_heads(value @ Wv.T + bv)
        attn = jnp.einsum('bhsd,bhtd->bhst', q, k) / jnp.sqrt(jnp.float32(Hd))
        attn = jax.nn.softmax(attn, axis=-1)
        out = jnp.einsum('bhst,bhtd->bhsd', attn, v)
        out = out.transpose(0, 2, 1, 3).reshape(B, -1, D)
        return out @ Wo.T + bo

    def _L0_ffn_ref(x, Wg, A, B):
        import jax, jax.numpy as jnp
        import numpy as np
        TOP_K = 2
        D = x.shape[-1]
        E = Wg.shape[-1]
        xs = x.reshape(-1, D)
        gate_logits = xs @ Wg
        topw, sel = jax.lax.top_k(gate_logits, TOP_K)
        topw = jax.nn.softmax(topw.astype(jnp.float32), axis=-1).astype(x.dtype)
        cw = jnp.sum(jax.nn.one_hot(sel, E, dtype=x.dtype) * topw[..., None], axis=1)
        h = jnp.einsum('td,edr->ter', xs, A)
        hw = h * cw[..., None]
        out = jnp.einsum('ter,erd->td', hw, B)
        return out.reshape(x.shape)

    def _L1_xattn_ref(x, context, ptb_gamma, W_fused, W_attn_out, W_ff_out, ca_gamma, ca_ctx_gamma, W_q, W_kv, W_out):
        import jax, jax.numpy as jnp
        import numpy as np
        DIM = 128
        HEADS = 16
        DIM_HEAD = 64
        FF_MULT = 4
        CTX_DIM = 128
        INNER = HEADS * DIM_HEAD
        FF_INNER = DIM * FF_MULT
        FUSED = INNER + 2 * DIM_HEAD + 2 * FF_INNER
        SCALE = DIM_HEAD ** (-0.5)

        def layer_norm(x, gamma, eps=1e-05):
            mu = jnp.mean(x, axis=-1, keepdims=True)
            var = jnp.var(x, axis=-1, keepdims=True)
            return (x - mu) * jax.lax.rsqrt(var + eps) * gamma

        def swiglu(x):
            a, gate = jnp.split(x, 2, axis=-1)
            return jax.nn.silu(gate) * a

        def parallel_block(x, gamma, W_fused, W_attn_out, W_ff_out):
            B, N, D = x.shape
            h = layer_norm(x, gamma)
            fused = h @ W_fused
            q = fused[..., :INNER]
            k = fused[..., INNER:INNER + DIM_HEAD]
            v = fused[..., INNER + DIM_HEAD:INNER + 2 * DIM_HEAD]
            ff = fused[..., INNER + 2 * DIM_HEAD:]
            q = q.reshape(B, N, HEADS, DIM_HEAD).transpose(0, 2, 1, 3) * SCALE
            sim = jnp.einsum('bhid,bjd->bhij', q, k)
            causal = jnp.triu(jnp.ones((N, N), dtype=bool), k=1)
            neg = -jnp.finfo(sim.dtype).max
            sim = jnp.where(causal, neg, sim)
            sim = sim - jax.lax.stop_gradient(jnp.max(sim, axis=-1, keepdims=True))
            attn = jax.nn.softmax(sim, axis=-1)
            out = jnp.einsum('bhij,bjd->bhid', attn, v)
            out = out.transpose(0, 2, 1, 3).reshape(B, N, INNER)
            return out @ W_attn_out + swiglu(ff) @ W_ff_out

        def cross_attention(x, context, gamma, ctx_gamma, W_q, W_kv, W_out):
            B, N, D = x.shape
            xq = layer_norm(x, gamma)
            c = layer_norm(context, ctx_gamma)
            q = (xq @ W_q).reshape(B, N, HEADS, DIM_HEAD).transpose(0, 2, 1, 3) * SCALE
            kv = c @ W_kv
            k, v = (kv[..., :DIM_HEAD], kv[..., DIM_HEAD:])
            sim = jnp.einsum('bhid,bjd->bhij', q, k)
            attn = jax.nn.softmax(sim, axis=-1)
            out = jnp.einsum('bhij,bjd->bhid', attn, v)
            out = out.transpose(0, 2, 1, 3).reshape(B, N, INNER)
            return out @ W_out
        y = x + parallel_block(x, ptb_gamma, W_fused, W_attn_out, W_ff_out)
        return cross_attention(y, context, ca_gamma, ca_ctx_gamma, W_q, W_kv, W_out)

    def _L1_ffn_ref(x, w_gate, w_up, w_down):
        import jax, jax.numpy as jnp
        import numpy as np
        BLOCK = 32
        W_BITS = 4
        ACT_BITS = 16

        def act_qdq(x):
            qmax = 2.0 ** (ACT_BITS - 1) - 1.0
            scale = jnp.maximum(jnp.max(jnp.abs(x)) / qmax, 1e-12)
            return jnp.clip(jnp.round(x / scale), -qmax - 1.0, qmax) * scale

        def fixed_qdq_u16(x):
            scale = 1.0 / 65536.0
            return jnp.clip(jnp.round(x / scale), 0.0, 65535.0) * scale

        def lpbq_dequant(w):
            O, I = w.shape
            qmax = 2.0 ** (W_BITS - 1) - 1.0
            wb = w.reshape(O, I // BLOCK, BLOCK)
            s = jnp.maximum(jnp.max(jnp.abs(wb), axis=-1, keepdims=True) / qmax, 1e-12)
            wq = jnp.clip(jnp.round(wb / s), -qmax - 1.0, qmax) * s
            return wq.reshape(O, I)
        x = act_qdq(x)
        up = act_qdq(x @ lpbq_dequant(w_up).T)
        gate = act_qdq(x @ lpbq_dequant(w_gate).T)
        sig = fixed_qdq_u16(jax.nn.sigmoid(gate))
        gate = act_qdq(gate * sig)
        o = act_qdq(gate * up)
        return o @ lpbq_dequant(w_down).T
    x = x + _L0_xattn_ref(_layernorm(x, axis=-1), ctx_1024, ctx_1024, L0_xattn_Wq, L0_xattn_bq, L0_xattn_Wk, L0_xattn_bk, L0_xattn_Wv, L0_xattn_bv, L0_xattn_Wo, L0_xattn_bo)
    x = x + _L0_ffn_ref(_layernorm(x, axis=-1), L0_ffn_Wg, L0_ffn_A, L0_ffn_B)
    x = x + _L1_xattn_ref(_layernorm(x, axis=-1), ctx_1024, L1_xattn_ptb_gamma, L1_xattn_W_fused, L1_xattn_W_attn_out, L1_xattn_W_ff_out, L1_xattn_ca_gamma, L1_xattn_ca_ctx_gamma, L1_xattn_W_q, L1_xattn_W_kv, L1_xattn_W_out)
    x = x + _L1_ffn_ref(_layernorm(x, axis=-1), L1_ffn_w_gate, L1_ffn_w_up, L1_ffn_w_down)
    return x

_drawn_inputs = setup_inputs


def setup_inputs(seed=0):
    import zlib

    import numpy as np

    out = dict(_drawn_inputs(seed))
    spreads = {'L0_xattn_bq': (0.0, 0.364),
     'L0_xattn_bk': (0.0, 0.8),
     'L0_xattn_bv': (0.0, 0.1),
     'L0_xattn_bo': (0.0, 0.1),
     'L1_xattn_ptb_gamma': (1.0, 0.6),
     'L1_xattn_ca_gamma': (1.0, 0.6),
     'L1_xattn_ca_ctx_gamma': (1.0, 0.6)}
    factors = {'L0_ffn_Wg': 5.781,
     'L0_ffn_A': 4.943,
     'L0_ffn_B': 4.932,
     'L1_xattn_W_fused': 8.0,
     'L1_xattn_W_attn_out': 8.0,
     'L1_xattn_W_ff_out': 8.0,
     'L1_xattn_W_q': 8.0,
     'L1_ffn_w_gate': 5.706,
     'L1_ffn_w_up': 5.44,
     'L1_ffn_w_down': 5.367}
    for name, (base, spread) in spreads.items():
        noise = np.random.default_rng([zlib.crc32(name.encode()), seed]).standard_normal(out[name].shape)
        drawn = base * np.exp(spread * noise) if base else spread * noise
        out[name] = jnp.asarray(drawn.astype(out[name].dtype))
    for name, factor in factors.items():
        out[name] = (out[name] * factor).astype(out[name].dtype)
    return out
```

```python
from contextlib import ExitStack

import numpy as np
import concourse.bass as bass
from concourse import mybir

F32 = mybir.dt.float32
F16 = mybir.dt.float16
BF16 = mybir.dt.bfloat16
ALU = mybir.AluOpType
ACT = mybir.ActivationFunctionType
AX = mybir.AxisListType
RMAX = bass.bass_isa.ReduceOp.max

P = 128
D = 128
T = 1024
NT = T // P
CTX = 6404
KT = -(-CTX // P)
CTXP = KT * P
HALF = 512
H = 16
HD0 = 8
HD1 = 64
G0 = H // 4
E, R = 8, 16
FFI = 512
QI = 384
BLK = 32
EPS = 1e-5
PAD_SCORE = -30000.0
MASKED = -1e30
ROUND = 1.5 * 2.0 ** 23
QMAX = 32767.0
NCH = -(-CTX // HALF)
CW = [min(HALF, CTX - c * HALF) for c in range(NCH)]
PCH = -(-CTXP // HALF)
PW = [min(HALF, CTXP - c * HALF) for c in range(PCH)]
ROW_SHIFT0, ROW_PAD0 = 24, 27
ROW_SHIFT1, ROW_PAD1 = 64, 67
CHUNKS0 = [range(0, 4), range(4, 9), range(9, 13)]
CHUNKS_S = [(t, c0, min(HALF, P * (t + 1) - c0)) for t in range(NT) for c0 in range(0, P * (t + 1), HALF)]
STEPS_S = [range(0, 2), range(2, 4), range(4, 6), range(6, 7), range(7, 8), range(8, 9), range(9, 11), range(11, 12)]
CHUNKS1 = [range(0, 3), range(3, 5), range(5, 7), range(7, 9), range(9, 11), range(11, 13)]
CHUNKS1_LAST = [range(0, 3), range(3, 7), range(7, 10), range(10, 13), (), ()]


class Chain:

    def __init__(self, eng, sem, base=0, per=None):
        self.eng, self.sem, self.base, self.n, self.per = eng, sem, base, 0, per

    def __call__(self, ins):
        self.n += 1
        ins.then_inc(self.sem, 1)
        self.eng.wait_ge(self.sem, self.base + self.n)

    def check(self):
        assert self.n == self.per, self.n


def build(nc, a, out):
    with ExitStack() as ctx:
        def sb(name, shape, dt=F32):
            return ctx.enter_context(nc.sbuf_tensor(name, shape, dt))

        def ps(name, shape):
            return ctx.enter_context(nc.psum_tensor(name, shape, F32))

        sems = {}

        def sem(name):
            if name not in sems:
                sems[name] = ctx.enter_context(nc.semaphore(name))
            return sems[name]

        arena_a = sb("arena_a", [P, G0 * CTXP // 2])
        arena_b = sb("arena_b", [P, H * T // 2])
        arena_c = sb("arena_c", [P, CTXP])
        arena_d = sb("arena_d", [P, 7680])
        arena_e = sb("arena_e", [P, H * HALF])
        probs = sb("probs", [P, 3, 2 * HALF])

        def view(arena, at, shape, dt=F32):
            n = int(np.prod(shape))
            words = n if dt == F32 else n // 2
            v = arena[:, at:at + words]
            if dt != F32:
                v = v.bitcast(dt)
            if len(shape) == 2:
                v = v.rearrange("p (a b) -> p a b", a=shape[0])
            if len(shape) == 3:
                v = v.rearrange("p (a b c) -> p a b c", a=shape[0], b=shape[1])
            return v

        k0 = view(arena_a, 0, [G0 * CTXP], F16)
        q0 = view(arena_b, 0, [H * T], F16)
        ctx_t = view(arena_c, 0, [CTXP])
        v0 = view(arena_d, 0, [KT, H * 9])
        o0 = view(arena_e, 0, [G0, T])
        wq0 = view(arena_e, 4096, [H, P])
        wk0 = view(arena_e, 6144, [G0, P])
        wv0 = view(arena_e, 6656, [P])
        wo0 = view(arena_e, 6784, [G0, P])
        wg0 = view(arena_e, 7296, [E])
        moe_a = view(arena_e, 7304, [P])
        moe_b = view(arena_e, 7432, [P])
        rows0 = view(arena_e, 7560, [2 * P])

        c_nat = view(arena_e, 0, [KT, D])
        c_t = view(arena_d, 0, [CTXP])
        k1 = view(arena_c, 0, [CTXP], F16)
        k2 = view(arena_c, CTXP // 2, [CTXP], F16)
        v1 = view(arena_a, H * T // 2, [KT, HD1])
        wkv_c = view(arena_e, 6528, [3 * HD1])

        q2 = view(arena_a, 0, [H * T], F16)
        q1 = view(arena_b, 0, [H * T], F16)
        o1 = view(arena_e, 0, [H, HALF])
        wq1 = view(arena_e, 0, [H, P])
        wkv_s = view(arena_e, 2048, [3 * HD1])
        wff = view(arena_e, 2240, [2 * FFI])
        wffo = view(arena_e, 3264, [FFI // P, D])
        gated = view(arena_e, 3776, [FFI // P, T])
        k1s = view(arena_d, 0, [T], F16)
        k2s = view(arena_d, T // 2, [T], F16)
        v1s = view(arena_d, T, [NT, HD1])
        wproj = view(arena_d, 1536, [H, 2 * D])
        acc_v = view(arena_d, 5632, [2 * HALF])
        acc_g = view(arena_d, 6656, [2 * HALF])
        accs = view(arena_d, 5632, [2, 2 * HALF])
        probs_3 = view(arena_a, H * T // 2 + KT * HD1, [2 * HALF])

        qw = view(arena_a, 0, [3, 3, D])
        qwq = view(arena_a, 1152, [3, 3, D])
        qwt = view(arena_a, 2304, [3, 3, D])
        up = view(arena_b, 0, [3, T])
        gate = view(arena_b, 3072, [3, T])
        sig = view(arena_c, 0, [3, T])
        tmp = view(arena_c, 3072, [3, T])

        x = sb("x", [P, NT, D])
        xn = sb("xn", [P, NT, D])
        xt = sb("xt", [P, T])
        ident = sb("ident", [P, P])
        ident16 = sb("ident16", [P, P], F16)
        identb = sb("identb", [P, P], BF16)
        mask_kq = sb("mask_kq", [P, P], BF16)
        mask_qk = sb("mask_qk", [P, P], BF16)
        zeros16 = sb("zeros16", [P, P], F16)
        sel_sum = sb("sel_sum", [P, P])
        ones = sb("ones", [P, P])
        cols = sb("cols", [P, 34])
        shift_rows = sb("shift_rows", [P, 4 * P], F16)
        v_stage = sb("v_stage", [P, 3, HD1])
        mpart = sb("mpart", [P, 16])
        mx = sb("mx", [P, 16])
        mrest = sb("mrest", [P, 2, 16])
        recip = sb("recip", [P, HALF])
        stats = probs[:, 2, 0:6 * KT].rearrange("p (t s) -> p t s", s=6)
        mv = probs[:, 2, 320:320 + 2 * KT].rearrange("p (t s) -> p t s", s=2)
        sdev = probs[:, 2, 430:430 + KT]
        rstd = probs[:, 2, 490:490 + KT]
        hi_tmp = [probs[:, 0, 256 * i:256 * i + 256].bitcast(F16) for i in range(2)]
        hm_tmp = [probs[:, 0, 512 + 256 * i:768 + 256 * i].bitcast(F16) for i in range(2)]
        hn = probs[:, 0, :].rearrange("p (t d) -> p t d", t=NT)
        y_tmp = [probs[:, 1, 512 * i:512 * i + 512] for i in range(2)]

        kb0 = [cols[:, g:g + 1] for g in range(4)]
        qb0 = [cols[:, 4 + h:5 + h] for h in range(H)]
        C_QS, C_KLO, C_QLO, C_PAD0, C_ONE1, C_PAD1, C_GP, C_GC, C_GX = (20, 21, 22, 23, 24, 25, 27, 28, 29)

        def col(i, lo=0, hi=P):
            return cols[lo:hi, i:i + 1]

        ps_s = ps("ps_s", [P, 2, 2 * HALF])
        ps_o = ps("ps_o", [P, HALF])
        ps_m = ps("ps_m", [P, 2 * HALF])
        ps_t = ps("ps_t", [P, HALF])
        banks = [ps_s[:, i // 2, (i % 2) * HALF:(i % 2 + 1) * HALF] for i in range(4)]

        ps_flat = ps_s[:, :, :].rearrange("p a b -> p (a b)")

        def p_slot(t):
            return probs_3 if t % 4 == 3 else probs[:, t % 4, :]

        def mslot(c):
            return ps_m[:, (c % 2) * HALF:(c % 2 + 1) * HALF]

        def mslot3(c):
            return ps_t[:, :] if c % 3 == 2 else ps_m[:, 0:HALF] if c % 3 == 0 and c < NCH - 1 else ps_m[:, HALF:]

        ds = bass.ds

        block = ctx.enter_context(nc.Block())

        @block.sync
        def _(sp):
            def load(dst, src, name, after=()):
                for s, v in after:
                    sp.wait_ge(sem(s), v)
                sp.dma_start(dst, src).then_inc(sem(name), 16)

            load(x[:, :, :], a["x"].rearrange("(t p) d -> p t d", p=P), "x_in")
            load(cols[:, :], a["cols"], "const_in")
            load(ident[:, :], a["ident"], "const_in")
            load(ones[:, :], a["ones"], "const_in")
            load(ident16[:, :], a["ident16"], "const_in")
            load(probs[:, 0, 0:2 * P], a["masks"], "masks_in")
            load(sel_sum[:, :], a["sel_sum"], "const_in")
            load(wk0, a["wk0"], "w0_in")
            load(wv0, a["wv0"], "w0_in")
            load(wq0, a["wq0"], "w0_in")
            load(wo0, a["wo0"], "w0_in")
            load(wg0, a["wg0"], "w0_in")
            load(moe_a, a["moe_a"], "w0_in")
            load(moe_b, a["moe_b"], "w0_in")
            load(rows0[0:1], a["rows0"], "w0_in")
            for i in range(4):
                lo, hi = i * CTXP // 4, (i + 1) * CTXP // 4
                load(ctx_t[:, lo:hi], a["ctx_t"][:, lo:hi], "ctx_in")
            load(c_nat, a["ctx"].rearrange("(t p) d -> p t d", p=P), "ctx1_in", [("moe_out", NT)])
            load(wkv_c, a["wkv_c"], "ctx1_in")
            w1 = [("k1_split", PCH), ("v1_evac", 7)]
            load(wq1, a["wq_s"], "w1_in", w1)
            load(wkv_s, a["wkv_s"], "w1_in")
            load(wff, a["wff"], "w1_in")
            load(wffo, a["wffo"], "w1_in")
            load(wproj, a["wo_s"], "w1_in")
            load(wq1, a["wq_c"], "w2_in", [("sp_mm", 1)])
            load(wproj, a["wo_c"], "w2_in")
            load(qw, a["qw"], "qw_in", [("cp_mm", 1)])
            for t in range(NT):
                sp.wait_ge(sem("y_out"), t + 1)
                sp.dma_start(out[t * P:(t + 1) * P, :], x[:, t, :]).then_inc(sem("stored"), 16)
            sp.wait_ge(sem("stored"), 16 * NT)

        @block.tensor
        def _(pe):
            def mm(o, l, r, start=True, stop=True):
                return pe.matmul(o, l, r, start=start, stop=stop, skip_group_check=True)

            def ln_transposes(name, src, nt):
                pe.wait_ge(sem(name + "_xn"), 1)
                for i in range(0, nt, 4):
                    if i >= 16:
                        pe.wait_ge(sem(name + "_t"), i // 4 - 3)
                    for t in range(i, min(i + 4, nt)):
                        last = pe.transpose(banks[i // 4 % 4][:, (t % 4) * P:(t % 4 + 1) * P], src[:, t, :], ident[:, :])
                    last.then_inc(sem(name + "_mm"), 1)

            pe.sem_inc(sem("o0_mm"), 3)
            pe.sem_inc(sem("os_mm"), 4)
            pe.sem_inc(sem("o1_mm"), 3)
            pe.sem_inc(sem("s_sums"), 2)
            pe.sem_inc(sem("c_sums"), 1)
            pe.wait_ge(sem("const_in"), 16 * 5)
            pe.wait_ge(sem("zeros"), 2)
            pe.wait_ge(sem("w0_in"), 16 * 8)
            pe.wait_ge(sem("ctx_in"), 16 * 4)
            with pe.Fori(0, PCH - 1) as c:
                for g in range(G0):
                    pe.wait_ge(sem("k0_split"), 4 * c + g + 1)
                    mm(banks[g], wk0[:, g, :], ctx_t[:, ds(c * HALF, HALF)]).then_inc(sem("k0_mm"), 1)
            for g in range(G0):
                pe.wait_ge(sem("k0_split"), 4 * (PCH - 1) + g + 1)
                mm(banks[g][:, 0:PW[-1]], wk0[:, g, :], ctx_t[:, HALF * (PCH - 1):CTXP]).then_inc(sem("k0_mm"), 1)
            for i in range(PCH):
                if i < 4:
                    pe.wait_ge(sem("k0_split"), 4 + 4 * (PCH - 1) + i + 1)
                else:
                    pe.wait_ge(sem("v0_evac"), i - 3)
                for t in range(4 * i, min(4 * i + 4, KT)):
                    o = banks[i % 4][:, (t % 4) * P:(t % 4 + 1) * P]
                    mm(o, ctx_t[:, t * P:(t + 1) * P], wv0, stop=False)
                    last = mm(o, ones[0:1, :], rows0[0:1, 0:P], start=False)
                last.then_inc(sem("v0_mm"), 1)
            pe.wait_ge(sem("v0_evac"), PCH)
            ln_transposes("ln_a0", xn, NT)
            pe.wait_ge(sem("ln_a0_t"), 2)
            for i in range(2 * H):
                if i >= 4:
                    pe.wait_ge(sem("q0_split"), i - 3)
                mm(banks[i % 4], wq0[:, i // 2, :], xt[:, (i % 2) * HALF:(i % 2 + 1) * HALF]).then_inc(sem("q0_mm"), 1)
            pe.wait_ge(sem("q0_split"), 2 * H)

            def q0_at(b):
                return (b // 2) * (4 * T) + (b % 2) * HALF

            def max_chunk0(b, n, c):
                m = 208 * b + 13 * n + c
                pe.wait_ge(sem("m0_red"), m + 2 if c in (1, NCH - 1) else m + 1)
                mm(mslot3(c)[:, 0:CW[c]], q0[:, ds(q0_at(b) + (n // 4) * T + (n % 4) * P, P)],
                   k0[:, ds((b // 2) * CTXP + c * HALF, CW[c])]).then_inc(sem("m0_mm"), 1)

            def shift0(b):
                pe.wait_ge(sem("m0_parts"), b + 1)
                for t in range(4):
                    last = mm(ps_t[:, t * P:(t + 1) * P], shift_rows[:, t * P:(t + 1) * P], ident16[:, :])
                last.then_inc(sem("m0_turned"), 1)

            def scores0(b, kt, hp):
                i = 102 * b + 2 * kt + hp
                pe.wait_ge(sem("p0_exp"), i + 1)
                for j in range(2):
                    last = mm(ps_s[:, hp, j * HALF:(j + 1) * HALF], k0[:, ds((b // 2) * CTXP + kt * P, P)],
                              q0[:, ds(q0_at(b) + (2 * hp + j) * T, HALF)])
                last.then_inc(sem("s0_mm"), 1)

            def pv0(b, kt, u, stop):
                pe.wait_ge(sem("v0_staged"), 51 * b + kt + 1)
                pe.wait_ge(sem("p0_exp"), 102 * b + 2 * kt + 4)
                for j in range(4):
                    last = mm(ps_o[32 * j:32 * j + 9, :], v_stage[:, u, 9 * j:9 * j + 9],
                              probs[:, (2 * u + j // 2) % 3, (j % 2) * HALF:(j % 2 + 1) * HALF], False, stop)
                last.then_inc(sem("o0_mm"), 1)

            def first_scores0(b, hp):
                pe.wait_ge(sem("q0_shifted"), 4 * b + 2 * hp + 2)
                scores0(b, 0, hp)

            def block0(b, more):
                def group(n, first, last):
                    for u in range(3):
                        kt = 3 * n + u
                        ch = list(CHUNKS0[u]) if more and not last else []
                        for hp in range(2):
                            if not (last and u == 2):
                                scores0(b, kt + 1, hp)
                            elif more:
                                first_scores0(b + 1, hp)
                            for c in ch[0:2] if hp == 0 else ch[2:-1]:
                                max_chunk0(b + 1, n, c)
                        if first and u == 0:
                            pe.wait_ge(sem("o0_evac"), b + 1)
                            mm(ps_o[:, :], zeros16[:, :], q0[:, 0:HALF], True, False)
                        pv0(b, kt, u, last and u == 2)
                        for c in ch[-1:]:
                            max_chunk0(b + 1, n, c)
                        if last and more and u == 0:
                            shift0(b + 1)

                group(0, True, False)
                with pe.Fori(1, 16) as n:
                    group(n, False, False)
                group(16, False, True)

            pe.wait_ge(sem("k0_pad"), 1)
            with pe.Fori(0, 16) as n:
                for c in range(NCH):
                    max_chunk0(0, n, c)
            shift0(0)
            first_scores0(0, 0)
            first_scores0(0, 1)
            with pe.Fori(0, 7) as b:
                block0(b, True)
            block0(7, False)

            pe.wait_ge(sem("o0_evac"), 9)
            for i in range(8):
                if i >= 4:
                    pe.wait_ge(sem("o0_norm"), i - 3)
                mm(banks[i % 4], sel_sum[:, :], o0[:, i // 2, (i % 2) * HALF:(i % 2 + 1) * HALF]).then_inc(sem("sum0_mm"), 1)
            pe.wait_ge(sem("o0_norm"), 8)
            for t in range(NT):
                o = banks[t // 4][:, (t % 4) * P:(t % 4 + 1) * P]
                for g in range(G0):
                    mm(o, o0[:, g, t * P:(t + 1) * P], wo0[:, g, :], g == 0, False)
                last = mm(o, ones[0:1, :], rows0[0:1, P:2 * P], False)
            last.then_inc(sem("proj0_mm"), 1)

            pe.wait_ge(sem("x1"), 1)
            ln_transposes("ln_f0", xn, NT)
            pe.wait_ge(sem("ln_f0_t"), 2)
            for t in range(NT):
                mm(ps_t[:, t * E:(t + 1) * E], xt[:, t * P:(t + 1) * P], wg0)
            for t in range(NT):
                last = mm(banks[t // 4][:, (t % 4) * P:(t % 4 + 1) * P], xt[:, t * P:(t + 1) * P], moe_a)
            last.then_inc(sem("moe_mm"), 1)
            pe.wait_ge(sem("moe_hw"), 1)
            for t in range(NT):
                last = pe.transpose(banks[2 + t // 4][:, (t % 4) * P:(t % 4 + 1) * P], xn[:, t, :], ident[:, :])
            last.then_inc(sem("moe_tr"), 1)
            pe.wait_ge(sem("moe_ht"), 1)
            for t in range(NT):
                mm(banks[t // 4][:, (t % 4) * P:(t % 4 + 1) * P], xt[:, t * P:(t + 1) * P], moe_b).then_inc(sem("moe_out"), 1)

            pe.wait_ge(sem("x2"), 1)
            ln_transposes("ln_cx", c_nat, KT)
            pe.wait_ge(sem("ln_cx_t"), PCH)
            for i in range(PCH):
                if i >= 4:
                    pe.wait_ge(sem("k1_split"), i - 3)
                mm(banks[i % 4][:, 0:PW[i]], wkv_c[:, 0:P], c_t[:, i * HALF:i * HALF + PW[i]]).then_inc(sem("k1_mm"), 1)
            for i in range(7):
                if i < 4:
                    pe.wait_ge(sem("k1_split"), PCH)
                else:
                    pe.wait_ge(sem("v1_evac"), i - 3)
                for t in range(8 * i, min(8 * i + 8, KT)):
                    last = mm(banks[i % 4][:, (t % 8) * HD1:(t % 8 + 1) * HD1], c_t[:, t * P:(t + 1) * P], wkv_c[:, P:P + HD1])
                last.then_inc(sem("v1_mm"), 1)
            pe.wait_ge(sem("v1_evac"), 7)

            ln_transposes("ln_pb", hn, NT)
            pe.wait_ge(sem("ln_pb_t"), 2)
            pe.wait_ge(sem("w1_in"), 16 * 5)
            for i in range(8):
                if i >= 2:
                    pe.wait_ge(sem("ff_done"), i - 1)
                r, hf = i // 2, i % 2
                mm(banks[2 * (i % 2)], wff[:, r * P:(r + 1) * P], xt[:, hf * HALF:(hf + 1) * HALF])
                mm(banks[2 * (i % 2) + 1], wff[:, FFI + r * P:FFI + (r + 1) * P], xt[:, hf * HALF:(hf + 1) * HALF])\
                    .then_inc(sem("ff_mm"), 1)
            pe.wait_ge(sem("ff_done"), 8)
            for t in range(NT):
                for r in range(FFI // P):
                    last = mm(banks[t // 4][:, (t % 4) * P:(t % 4 + 1) * P], gated[:, r, t * P:(t + 1) * P], wffo[:, r, :],
                              r == 0, r == FFI // P - 1)
            last.then_inc(sem("ffo_mm"), 1)
            pe.wait_ge(sem("y_ff"), 1)
            for hf in range(2):
                mm(banks[hf], wkv_s[:, 0:P], xt[:, hf * HALF:(hf + 1) * HALF]).then_inc(sem("k1s_mm"), 1)
            for t in range(NT):
                last = mm(banks[2][:, t * HD1:(t + 1) * HD1], xt[:, t * P:(t + 1) * P], wkv_s[:, P:P + HD1])
            last.then_inc(sem("v1s_mm"), 1)
            pe.wait_ge(sem("k1s_split"), 2)
            pe.wait_ge(sem("v1s_evac"), 1)

            def queries1(name):
                for i in range(2 * H):
                    if i >= 4:
                        pe.wait_ge(sem(name + "_split"), i - 3)
                    mm(banks[i % 4], wq1[:, i // 2, :], xt[:, (i % 2) * HALF:(i % 2 + 1) * HALF]).then_inc(sem(name + "_mm"), 1)
                pe.wait_ge(sem(name + "_split"), 2 * H)

            queries1("qs")

            def max_chunk_s(h, n):
                t, c0, w = CHUNKS_S[n]
                pe.wait_ge(sem("sm_red"), 12 * h + n + 1)
                diagonal = c0 + w == P * (t + 1)
                last = mm(mslot(n)[:, 0:w], q1[:, ds(h * T + t * P, P)], k1s[:, c0:c0 + w], True, not diagonal)
                if diagonal:
                    last = mm(mslot(n)[:, w - P:w], identb[:, :], mask_qk[:, :], False, True)
                last.then_inc(sem("sm_mm"), 1)

            def shift1(k, h):
                pe.wait_ge(sem(k + "_parts"), h + 1)
                for t in range(NT):
                    at = 64 + 32 * (t // 4)
                    last = mm(ps_t[at:at + 32, (t % 4) * P:(t % 4 + 1) * P], shift_rows[:, t * 32:t * 32 + 32], ident16[:, :])
                last.then_inc(sem(k + "_turned"), 1)

            def scores_s(h, t):
                pe.wait_ge(sem("ps_exp"), 8 * h + t + 1)
                sl = ps_s[:, t % 2, :]
                parts = [(P * t, HALF), (HALF, T)] if t < 4 else [(P * t, T)]
                for lo, hi in parts:
                    mm(sl[:, lo:hi], k1s[:, t * P:(t + 1) * P], q1[:, ds(h * T + lo, hi - lo)], True, False)
                for lo, hi in parts:
                    mm(sl[:, lo:hi], k2s[:, t * P:(t + 1) * P], q2[:, ds(h * T + lo, hi - lo)], False, False)
                mm(sl[:, t * P:(t + 1) * P], identb[:, :], mask_kq[:, :], False, True).then_inc(sem("ss_mm"), 1)

            def pv_s(h, t):
                pe.wait_ge(sem("ps_exp"), 8 * h + t + 3)
                pr = p_slot(t).rearrange("p (i f c) -> p f i c", f=2, c=P)
                for f in range(2):
                    i = (t + 1 - f) // 2
                    if i < 4:
                        last = mm(ps_o[64 * f:64 * f + 64, i * P:HALF], v1s[:, t, :], pr[:, f, i:4], t == 0, t == 6 + f)
                last.then_inc(sem("os_mm"), 1)

            def sums_s(h, odd):
                pe.wait_ge(sem("s_add"), 8 * h + 8 + 4)
                for f in range(2):
                    last = mm(ps_t[64 * f:64 * f + 64, :], ones[:, 0:64],
                              accs[:, odd, :].rearrange("p (i f c) -> p f i c", f=2, c=P)[:, f], True, True)
                last.then_inc(sem("s_sums"), 1)

            def head_s(h, odd, first=False, maxima=True, more=True):
                for t in range(NT):
                    if t + 1 < NT:
                        scores_s(h, t + 1)
                    elif more:
                        pe.wait_ge(sem("s_shifted"), h + 2)
                        scores_s(h + 1, 0)
                    if maxima:
                        for n in STEPS_S[t]:
                            max_chunk_s(h + 2, n)
                    if t == 0:
                        pe.wait_ge(sem("s_evac"), h + 1)
                    pv_s(h, t)
                    if t == 0 and more:
                        pe.wait_ge(sem("s_shifted"), h + 1)
                        if not first:
                            pe.wait_ge(sem("s_recip"), 2 * h)
                        shift1("s", h + 1)
                    if t == 2 and not first:
                        pe.wait_ge(sem("s_shifted"), h + 2 if more else h + 1)
                        pe.wait_ge(sem("s_recip"), 2 * h)
                        sums_s(h - 1, 1 - odd)

            pe.wait_ge(sem("k2s_const"), 2)
            pe.wait_ge(sem("q2_zero"), 1)
            for h in range(2):
                for n in range(12):
                    max_chunk_s(h, n)
                if h == 0:
                    shift1("s", 0)
            pe.wait_ge(sem("s_shifted"), 1)
            scores_s(0, 0)
            head_s(0, 0, first=True)
            with pe.Fori(0, (H - 4) // 2) as n:
                head_s(2 * n + 1, 1)
                head_s(2 * n + 2, 0)
            head_s(H - 3, 1)
            head_s(H - 2, 0, maxima=False)
            head_s(H - 1, 1, maxima=False, more=False)
            pe.wait_ge(sem("s_recip"), 2 * H)
            sums_s(H - 1, 1)

            def project1(name, done):
                pe.wait_ge(sem(done), 16 + 1)
                for i in range(4):
                    for h in range(H):
                        last = mm(banks[i // 2][:, (i % 2) * 2 * P:(i % 2 + 1) * 2 * P], o1[:, h, i * P:(i + 1) * P],
                                  wproj[:, h, :], h == 0, h == H - 1)
                last.then_inc(sem(name), 1)

            project1("sp_mm", "s_o")

            ln_transposes("ln_ca", hn, NT)
            pe.wait_ge(sem("ln_ca_t"), 2)
            pe.wait_ge(sem("w2_in"), 16 * 2)
            queries1("qc")

            def max_chunk1(h, r, c):
                m = 104 * h + 13 * r + c
                pe.wait_ge(sem("m1_red"), m + 2 if c == 0 else m + 1)
                mm(mslot(c)[:, 0:CW[c]], q1[:, ds(h * T + r * P, P)], k1[:, c * HALF:c * HALF + CW[c]]).then_inc(sem("m1_mm"), 1)

            def scores1(h, kt):
                i = 51 * h + kt
                pe.wait_ge(sem("p1_exp"), i + 1)
                for n, (k, q) in enumerate(((k1, q1), (k2, q2))):
                    for hf in range(2):
                        last = mm(ps_flat[:, ds(((h + kt) % 2) * (2 * HALF) + hf * HALF, HALF)], k[:, ds(kt * P, P)],
                                  q[:, ds(h * T + hf * HALF, HALF)], n == 0, n == 1)
                last.then_inc(sem("s1_mm"), 1)

            def pv1(h, kt, slot, start, stop):
                i = 51 * h + kt
                pe.wait_ge(sem("v1_staged"), i + 1)
                pe.wait_ge(sem("p1_exp"), i + 3)
                for hf in range(2):
                    last = mm(ps_o[64 * hf:64 * hf + 64, :], v_stage[:, slot, :],
                              probs[:, slot, hf * HALF:(hf + 1) * HALF], start, stop)
                last.then_inc(sem("o1_mm"), 1)

            def sums_c(h):
                pe.wait_ge(sem("c_add_v"), 18 * h + 18 + 2)
                pe.wait_ge(sem("c_add_g"), 33 * h + 33 + 2)
                for i, acc in enumerate((acc_v, acc_g)):
                    for hf in range(2):
                        last = mm(ps_t[64 * hf:64 * hf + 64, :], ones[:, 0:64], acc[:, hf * HALF:(hf + 1) * HALF], i == 0, i == 1)
                last.then_inc(sem("c_sums"), 1)

            def head_c(h, first=False, more=True):
                for u in range(3):
                    scores1(h, u + 1)
                    if u == 0:
                        if not first:
                            sums_c(h - 1)
                        pe.wait_ge(sem("c_evac"), h + 1)
                    pv1(h, u, u, u == 0, False)

                def group(r, last):
                    for u in range(6):
                        kt = 3 + 6 * r + u
                        ch = list((CHUNKS1_LAST if last else CHUNKS1)[u]) if more else []
                        for c in ch[0:1]:
                            max_chunk1(h + 1, r, c)
                        if not (last and u == 5):
                            scores1(h, kt + 1)
                        for c in ch[1:]:
                            max_chunk1(h + 1, r, c)
                        pv1(h, kt, u % 3, False, last and u == 5)
                        if last and more and u == 4:
                            if not first:
                                pe.wait_ge(sem("c_recip"), 2 * h)
                            shift1("c", h + 1)

                with pe.Fori(0, 7) as r:
                    group(r, False)
                group(7, True)
                if more:
                    pe.wait_ge(sem("c_shifted"), h + 2)
                    scores1(h + 1, 0)

            with pe.Fori(0, NT) as r:
                for c in range(NCH):
                    max_chunk1(0, r, c)
            shift1("c", 0)
            pe.wait_ge(sem("c_shifted"), 1)
            scores1(0, 0)
            head_c(0, first=True)
            with pe.Fori(1, H - 1) as h:
                head_c(h)
            head_c(H - 1, more=False)
            pe.wait_ge(sem("c_recip"), 2 * (H - 1))
            sums_c(H - 1)
            project1("cp_mm", "c_o")

            pe.wait_ge(sem("qw_deq"), 1)
            for i in range(9):
                last = pe.transpose(ps_m[:, i * P:(i + 1) * P] if i < 8 else ps_t[:, 0:P], qwq[:, i // 3, i % 3, :], ident[:, :])
            last.then_inc(sem("qw_mm"), 1)
            ln_transposes("ln_f1", xn, NT)
            pe.wait_ge(sem("qx"), 1)
            pe.wait_ge(sem("qw_t"), 1)
            for w in range(2):
                for i in range(6):
                    n = 6 * w + i
                    if n >= 4:
                        pe.wait_ge(sem("ug_evac"), n - 3)
                    mm(banks[n % 4], qwt[:, w, i // 2, :], xt[:, (i % 2) * HALF:(i % 2 + 1) * HALF]).then_inc(sem("ug_mm"), 1)
            pe.wait_ge(sem("ug_evac"), 12)
            pe.wait_ge(sem("o_q"), 1)
            for t in range(NT):
                for c in range(3):
                    last = mm(banks[t // 4][:, (t % 4) * P:(t % 4 + 1) * P], gate[:, c, t * P:(t + 1) * P], qwt[:, 2, c, :],
                              c == 0, c == 2)
                last.then_inc(sem("down_mm"), 1)

        @block.vector
        def _(dve):
            link = Chain(dve, sem("dve_link"))
            dve.sem_inc(sem("k0_split"), 4)
            dve.sem_inc(sem("m0_red"), 3)
            dve.sem_inc(sem("m1_red"), 2)
            dve.sem_inc(sem("m0_unit"), 1)
            dve.sem_inc(sem("m1_unit"), 1)
            dve.sem_inc(sem("sm_red"), 2)
            dve.sem_inc(sem("s_recip"), 2)
            dve.sem_inc(sem("c_add_v"), 2)
            dve.sem_inc(sem("c_o"), 1)

            def flat(t3):
                return t3.rearrange("p a b -> p (a b)")

            def layernorm(name, src, dst, nt):
                for t in range(nt):
                    last = dve.bn_stats(stats[:, t, :], src[:, t, :])
                link(last)
                for t in range(nt):
                    last = dve.bn_aggr(mv[:, t, :], stats[:, t, :])
                link(last)
                dve.tensor_scalar(sdev[:, 0:nt], mv[:, 0:nt, 1], EPS, None, ALU.add).then_inc(sem(name + "_var"), 1)
                dve.wait_ge(sem(name + "_sd"), 1)
                link(dve.reciprocal(rstd[:, 0:nt], sdev[:, 0:nt]))
                for t in range(nt):
                    last = dve.tensor_scalar(dst[:, t, :], src[:, t, :], mv[:, t, 0:1], rstd[:, t:t + 1], ALU.subtract, ALU.mult)
                last.then_inc(sem(name + "_xn"), 1)

            dve.wait_ge(sem("x_in"), 16)
            dve.wait_ge(sem("const_in"), 16 * 5)
            layernorm("ln_a0", x, xn, NT)
            dve.wait_ge(sem("masks_in"), 16)
            dve.tensor_copy(identb[:, :], ident[:, :])
            dve.tensor_copy(mask_kq[:, :], probs[:, 0, 0:P])
            link(dve.tensor_copy(mask_qk[:, :], probs[:, 0, P:2 * P]))
            dve.sem_inc(sem("masks"), 1)

            def split_k0(i, g, dst, w):
                dve.wait_ge(sem("k0_hi"), i + 1)
                dve.tensor_scalar(hm_tmp[g % 2][:, 0:w], hi_tmp[g % 2][:, 0:w], col(C_KLO), None, ALU.mult)\
                    .then_inc(sem("k0_masked"), 1)
                dve.wait_ge(sem("k0_masked"), i + 1)
                dve.scalar_tensor_tensor(out=dst, in0=banks[g][:, 0:w], scalar=kb0[g], in1=hm_tmp[g % 2][:, 0:w],
                                         op0=ALU.add, op1=ALU.subtract).then_inc(sem("k0_split"), 1)

            with dve.Fori(0, PCH - 1) as c:
                for g in range(G0):
                    split_k0(4 * c + g, g, k0[:, ds(c * HALF + g * CTXP, HALF)], HALF)
            for g in range(G0):
                at = g * CTXP + (PCH - 1) * HALF
                split_k0(4 * (PCH - 1) + g, g, k0[:, at:at + PW[-1]], PW[-1])
            dve.wait_ge(sem("k0_split"), 4 * PCH + 4)
            for g in range(G0):
                last = dve.tensor_scalar(k0[:, g * CTXP + CTX:(g + 1) * CTXP], zeros16[:, 0:CTXP - CTX], col(C_PAD0), None, ALU.add)
            last.then_inc(sem("k0_pad"), 1)

            def q0_finish(i):
                dve.wait_ge(sem("q0_hi"), i + 1)
                link(dve.tensor_scalar(hm_tmp[i % 2], hi_tmp[i % 2], col(C_QLO), None, ALU.mult))
                dve.tensor_tensor(q0[:, i * HALF:(i + 1) * HALF], y_tmp[i % 2], hm_tmp[i % 2], ALU.subtract)\
                    .then_inc(sem("q0_split"), 1)

            for i in range(2 * H):
                dve.wait_ge(sem("q0_mm"), i + 1)
                if i >= 2:
                    dve.wait_ge(sem("q0_split"), i - 1)
                dve.tensor_scalar(y_tmp[i % 2], banks[i % 4], qb0[i // 2], col(C_QS), ALU.add, ALU.mult)\
                    .then_inc(sem("q0_y"), 1)
                if i >= 1:
                    q0_finish(i - 1)
            q0_finish(2 * H - 1)

            rows4 = shift_rows[:, :].rearrange("p (t j r) -> p j t r", t=4, j=4)
            rows8 = shift_rows[:, 0:8 * 32].rearrange("p (t r) -> p t r", r=32)

            def negated_parts(link_sem, base, ready, part, mxv, rest):
                ch = Chain(dve, sem(link_sem), base, 4)
                ch(dve.tensor_scalar(part(0), mxv, -1.0, None, ALU.mult))
                ch(dve.scalar_tensor_tensor(out=rest(0), in0=mxv, scalar=-1.0, in1=part(0), op0=ALU.mult, op1=ALU.subtract))
                ch(dve.tensor_copy(part(1), rest(0)))
                ch(dve.tensor_tensor(rest(1), rest(0), part(1), ALU.subtract))
                dve.tensor_copy(part(2), rest(1)).then_inc(sem(ready), 1)
                ch.check()

            def unit0(b, n):
                dve.wait_ge(sem("m0_unit"), 16 * b + n + 1)
                for c in range(NCH):
                    dve.wait_ge(sem("m0_mm"), 208 * b + 13 * n + c + 1)
                    dve.tensor_reduce(mpart[:, c:c + 1], mslot3(c)[:, 0:CW[c]], AX.X, ALU.max).then_inc(sem("m0_red"), 1)
                dve.wait_ge(sem("m0_red"), 208 * b + 13 * n + NCH + 3)
                dve.tensor_reduce(mx[:, ds(n, 1)], mpart[:, 0:NCH], AX.X, ALU.max).then_inc(sem("m0_unit"), 1)

            def shift_block0(b):
                dve.wait_ge(sem("m0_unit"), 16 * b + 16 + 1)
                negated_parts("m0_link", 4 * b, "m0_parts",
                              lambda k: rows4[:, :, :, ROW_SHIFT0 + k],
                              mx[:, :].rearrange("p (j t) -> p j t", j=4),
                              lambda k: mrest[:, k, :].rearrange("p (j t) -> p j t", j=4))
                dve.wait_ge(sem("m0_turned"), b + 1)
                for j in range(4):
                    q = q0[32 * j:32 * j + 32, ds((b // 2) * (4 * T) + (b % 2) * HALF + j * T, HALF)]
                    dve.tensor_tensor(q, ps_t[32 * j:32 * j + 32, :], q, ALU.add).then_inc(sem("q0_shifted"), 1)

            dve.wait_ge(sem("q0_split"), 2 * H)
            dve.wait_ge(sem("zeros"), 2)
            with dve.Fori(0, 8) as b:
                with dve.Fori(0, 16) as n:
                    unit0(b, n)
                shift_block0(b)

            for i in range(8):
                dve.wait_ge(sem("sum0_mm"), i + 1)
                link(dve.reciprocal(y_tmp[i % 2], banks[i % 4]))
                o = o0[:, i // 2, (i % 2) * HALF:(i % 2 + 1) * HALF]
                dve.tensor_tensor(o, o, y_tmp[i % 2], ALU.mult).then_inc(sem("o0_norm"), 1)
            dve.wait_ge(sem("proj0_mm"), 1)
            link(dve.tensor_tensor(flat(x[:, :, :]), ps_s[:, 0, :], flat(x[:, :, :]), ALU.add))
            dve.sem_inc(sem("x1"), 1)
            layernorm("ln_f0", x, xn, NT)

            dve.wait_ge(sem("moe_mm"), 1)
            lg = y_tmp[0][:, 0:64].rearrange("p (t e) -> p t e", e=E)
            ex = y_tmp[0][:, 64:128].rearrange("p (t e) -> p t e", e=E)
            rank = y_tmp[0][:, 128:192].rearrange("p (t e) -> p t e", e=E)
            m1 = y_tmp[0][:, 192:200]
            ssum = y_tmp[0][:, 200:208]
            ahead = y_tmp[1].rearrange("p (t e f) -> p t e f", e=E, f=E)
            link(dve.tensor_copy(flat(lg), ps_t[:, 0:NT * E]))
            link(dve.memset(y_tmp[1], 0.0))
            link(dve.tensor_reduce(m1, lg, AX.X, ALU.max))
            for f in range(E):
                one = lg[:, :, f:f + 1]
                if f + 1 < E:
                    last = dve.tensor_tensor(ahead[:, :, f + 1:E, f], one.broadcast_to([P, NT, E - f - 1]), lg[:, :, f + 1:E], ALU.is_ge)
                if f:
                    last = dve.tensor_tensor(ahead[:, :, 0:f, f], one.broadcast_to([P, NT, f]), lg[:, :, 0:f], ALU.is_gt)
            link(last)
            link(dve.tensor_reduce(rank, ahead, AX.X, ALU.add))
            link(dve.tensor_scalar(rank, rank, 1.5, None, ALU.is_lt))
            dve.tensor_tensor(ex, lg, m1.unsqueeze(2).broadcast_to([P, NT, E]), ALU.subtract).then_inc(sem("moe_d"), 1)
            dve.wait_ge(sem("moe_exp"), 1)
            link(dve.tensor_tensor(ex, ex, rank, ALU.mult))
            link(dve.tensor_reduce(ssum, ex, AX.X, ALU.add))
            link(dve.reciprocal(ssum, ssum))
            link(dve.tensor_tensor(ex, ex, ssum.unsqueeze(2).broadcast_to([P, NT, E]), ALU.mult))
            dve.tensor_tensor(flat(xn[:, :, :]).rearrange("p (a r) -> p a r", r=R), ps_s[:, 0, :].rearrange("p (a r) -> p a r", r=R),
                              flat(ex).unsqueeze(2).broadcast_to([P, NT * E, R]), ALU.mult).then_inc(sem("moe_hw"), 1)
            dve.wait_ge(sem("moe_out"), NT)
            link(dve.tensor_tensor(flat(x[:, :, :]), ps_s[:, 0, :], flat(x[:, :, :]), ALU.add))
            dve.sem_inc(sem("x2"), 1)

            dve.wait_ge(sem("ctx1_in"), 32)
            layernorm("ln_cx", c_nat, c_nat, KT)
            for i in range(PCH):
                dve.wait_ge(sem("k1_hi"), i + 1)
                s = slice(i * HALF, i * HALF + PW[i])
                dve.tensor_tensor(k2[0:64, s], banks[i % 4][0:64, 0:PW[i]], k1[0:64, s], ALU.subtract).then_inc(sem("k1_split"), 1)

            dve.wait_ge(sem("ln_cx_xn"), 1)
            layernorm("ln_a1", x, xn, NT)
            dve.wait_ge(sem("ln_a1_xn"), 1)
            layernorm("ln_pb", xn, hn, NT)

            dve.wait_ge(sem("ln_pb_t"), 2)
            for i in range(8):
                r, hf = i // 2, i % 2
                e = y_tmp[i % 2]
                g = gated[:, r, hf * HALF:(hf + 1) * HALF]
                dve.wait_ge(sem("ff_exp"), i + 1)
                link(dve.tensor_scalar(e, e, 1.0, None, ALU.add))
                link(dve.reciprocal(e, e))
                link(dve.tensor_tensor(e, banks[2 * (i % 2) + 1], e, ALU.mult))
                dve.tensor_tensor(g, banks[2 * (i % 2)], e, ALU.mult).then_inc(sem("ff_done"), 1)
            dve.wait_ge(sem("ffo_mm"), 1)
            dve.tensor_tensor(flat(xn[:, :, :]), ps_s[:, 0, :], flat(xn[:, :, :]), ALU.add).then_inc(sem("y_ff"), 1)
            for i in range(2):
                dve.wait_ge(sem("k1s_hi"), i + 1)
                s = slice(i * HALF, (i + 1) * HALF)
                dve.tensor_tensor(k2s[0:64, s], banks[i][0:64, :], k1s[0:64, s], ALU.subtract).then_inc(sem("k1s_split"), 1)

            def split_queries(name):
                for i in range(2 * H):
                    dve.wait_ge(sem(name + "_hi"), i + 1)
                    lo = q1[64:128, i * HALF:(i + 1) * HALF]
                    dve.scalar_tensor_tensor(out=lo, in0=banks[i % 4][64:128, :], scalar=HD1 ** -0.5, in1=lo,
                                             op0=ALU.mult, op1=ALU.subtract).then_inc(sem(name + "_split"), 1)

            split_queries("qs")

            def reduce_s(h, n):
                t, c0, w = CHUNKS_S[n]
                dve.wait_ge(sem("sm_mm"), 12 * h + n + 1)
                at = t if c0 == 0 else 4 + t
                dve.tensor_reduce(mx[:, at:at + 1], mslot(n)[:, 0:w], AX.X, ALU.max).then_inc(sem("sm_red"), 1)

            def parts_s(h):
                dve.wait_ge(sem("sm_red"), 12 * h + 12 + 2)
                dve.tensor_tensor(mx[:, 4:8], mx[:, 4:8], mx[:, 8:12], ALU.max).then_inc(sem("s_unit"), 1)
                dve.wait_ge(sem("s_unit"), h + 1)
                negated_parts("s_link", 4 * h, "s_parts", lambda p: rows8[:, :, p], mx[:, 0:NT], lambda p: mrest[:, p, 0:NT])

            def recip_s(h, i):
                dve.wait_ge(sem("s_sums"), h + 1 + 2)
                dve.wait_ge(sem("s_o"), h + 1)
                s = slice(i * HALF // 2, (i + 1) * HALF // 2)
                dve.reciprocal(recip[:, s], ps_t[:, s]).then_inc(sem("s_recip"), 1)

            def head_s(h, first=False, maxima=True):
                for n in range(12):
                    if n in (6, 7) and not first:
                        recip_s(h - 1, n - 6)
                    if maxima:
                        reduce_s(h + 2, n)
                if maxima:
                    dve.wait_ge(sem("s_turned"), h + 2)
                    parts_s(h + 2)

            dve.wait_ge(sem("shift_zero"), 2)
            for h in range(2):
                for n in range(12):
                    reduce_s(h, n)
                if h:
                    dve.wait_ge(sem("s_turned"), 1)
                parts_s(h)
            head_s(0, first=True)
            with dve.Fori(1, H - 2) as h:
                head_s(h)
            head_s(H - 2, maxima=False)
            head_s(H - 1, maxima=False)
            recip_s(H - 1, 0)
            recip_s(H - 1, 1)

            halves = xn[:, :, :].rearrange("p (i f) d -> p i f d", f=2)
            dve.wait_ge(sem("sp_mm"), 1)
            for i in range(4):
                last = dve.tensor_tensor(halves[:, i], ps_s[:, 0, i * 256:(i + 1) * 256].rearrange("p (f d) -> p f d", f=2),
                                         halves[:, i], ALU.add)
            link(last)

            layernorm("ln_ca", xn, hn, NT)
            split_queries("qc")

            def reduce1(h, r, c):
                if c == 0:
                    dve.wait_ge(sem("m1_unit"), 8 * h + r + 1)
                dve.wait_ge(sem("m1_mm"), 104 * h + 13 * r + c + 1)
                dve.tensor_reduce(mpart[:, c:c + 1], mslot(c)[:, 0:CW[c]], AX.X, ALU.max).then_inc(sem("m1_red"), 1)

            def unit1(h, r):
                dve.wait_ge(sem("m1_red"), 104 * h + 13 * r + NCH + 2)
                dve.tensor_reduce(mx[:, ds(r, 1)], mpart[:, 0:NCH], AX.X, ALU.max).then_inc(sem("m1_unit"), 1)

            def parts_c(h):
                dve.wait_ge(sem("m1_unit"), 8 * h + 8 + 1)
                negated_parts("c_link", 4 * h, "c_parts", lambda p: rows8[:, :, p], mx[:, 0:NT], lambda p: mrest[:, p, 0:NT])

            def add_v(h, n, slot=0):
                dve.wait_ge(sem("p1_exp"), 51 * h + 3 * n + 3 if slot == 0 else 51 * h + 50 + 3)
                dve.wait_ge(sem("c_add_v"), 18 * h + n + 2)
                dve.tensor_tensor(acc_v, acc_v, probs[:, slot, :], ALU.add).then_inc(sem("c_add_v"), 1)

            def normalise_c(h):
                dve.wait_ge(sem("c_sums"), h + 2)
                dve.wait_ge(sem("c_o"), h + 1)
                for i in range(2):
                    s = slice(i * HALF // 2, (i + 1) * HALF // 2)
                    dve.reciprocal(recip[:, s], ps_t[:, s]).then_inc(sem("c_recip"), 1)
                dve.wait_ge(sem("c_recip"), 2 * h + 2)
                dve.wait_ge(sem("c_evac"), h + 1 + 1)
                o = o1[:, ds(h, 1), :].rearrange("p a b -> p (a b)")
                dve.tensor_tensor(o, o, recip[:, :], ALU.mult).then_inc(sem("c_o"), 1)

            def head_c(h, first=False, more=True):
                dve.wait_ge(sem("p1_exp"), 51 * h + 3)
                dve.wait_ge(sem("c_sums"), h + 1)
                dve.tensor_copy(acc_v, probs[:, 0, :]).then_inc(sem("c_add_v"), 1)
                if not first:
                    normalise_c(h - 1)

                def group(r, last):
                    for u in range(6):
                        if more:
                            for c in (CHUNKS1_LAST if last else CHUNKS1)[u]:
                                reduce1(h + 1, r, c)
                            if u == (3 if last else 5):
                                unit1(h + 1, r)
                        if last and more and u == 3:
                            dve.wait_ge(sem("c_turned"), h + 1)
                            parts_c(h + 1)
                        if u % 3 == 0:
                            add_v(h, 1 + 2 * r + u // 3)
                    if last:
                        add_v(h, 17, 2)

                with dve.Fori(0, 7) as r:
                    group(r, False)
                group(7, True)

            with dve.Fori(0, NT) as r:
                for c in range(NCH):
                    reduce1(0, r, c)
                unit1(0, r)
            parts_c(0)
            head_c(0, first=True)
            with dve.Fori(1, H - 1) as h:
                head_c(h)
            head_c(H - 1, more=False)
            normalise_c(H - 1)

            halves = x[:, :, :].rearrange("p (f i) d -> p i f d", f=2)
            dve.wait_ge(sem("cp_mm"), 1)
            for i in range(4):
                last = dve.tensor_tensor(halves[:, i], ps_s[:, 0, i * 256:(i + 1) * 256].rearrange("p (f d) -> p f d", f=2),
                                         halves[:, i], ALU.add)
            link(last)

            dve.wait_ge(sem("qw_in"), 16)
            wb = qw.rearrange("p a b d -> p (a b d)").rearrange("p (n k) -> p n k", k=BLK)
            wqb = qwq.rearrange("p a b d -> p (a b d)").rearrange("p (n k) -> p n k", k=BLK)
            NB = 9 * D // BLK
            wscale, winv = y_tmp[0][:, 0:NB], y_tmp[0][:, 64:64 + NB]
            link(dve.tensor_reduce(wscale, wb, AX.X, ALU.max, apply_absolute_value=True))
            link(dve.tensor_scalar(wscale, wscale, 1.0 / 7.0, 1e-12, ALU.mult, ALU.max))
            link(dve.reciprocal(winv, wscale))
            link(dve.tensor_tensor(wqb, wb, winv.unsqueeze(2).broadcast_to([P, NB, BLK]), ALU.mult))
            link(dve.tensor_scalar(wqb, wqb, ROUND, ROUND, ALU.add, ALU.subtract))
            link(dve.tensor_scalar(wqb, wqb, 7.0, -8.0, ALU.min, ALU.max))
            dve.tensor_tensor(wqb, wqb, wscale.unsqueeze(2).broadcast_to([P, NB, BLK]), ALU.mult).then_inc(sem("qw_deq"), 1)
            layernorm("ln_f1", x, xn, NT)

            amax = [y_tmp[0][:, 128 + i:129 + i] for i in range(5)]
            gmax = [y_tmp[0][:, 136 + i:137 + i] for i in range(5)]
            scale = [y_tmp[0][:, 144 + i:145 + i] for i in range(5)]
            inv = [y_tmp[0][:, 152 + i:153 + i] for i in range(5)]

            def quantise(n, z, done=None):
                dve.tensor_reduce(amax[n], z, AX.X, ALU.max, apply_absolute_value=True).then_inc(sem("q_amax"), 1)
                dve.wait_ge(sem("q_gmax"), n + 1)
                link(dve.tensor_scalar(scale[n], gmax[n], 1.0 / QMAX, 1e-12, ALU.mult, ALU.max))
                link(dve.reciprocal(inv[n], scale[n]))
                link(dve.tensor_scalar(z, z, inv[n], ROUND, ALU.mult, ALU.add))
                link(dve.tensor_scalar(z, z, ROUND, QMAX, ALU.subtract, ALU.min))
                last = dve.tensor_scalar(z, z, -QMAX - 1.0, scale[n], ALU.max, ALU.mult)
                if done:
                    last.then_inc(sem(done), 1)
                else:
                    link(last)

            upf, gatef, sigf, tmpf = (flat(v) for v in (up, gate, sig, tmp))
            dve.wait_ge(sem("ln_f1_t"), 2)
            quantise(0, xt[:, :], "qx")
            dve.wait_ge(sem("ug_evac"), 6)
            quantise(1, gatef, "gate_q")
            dve.wait_ge(sem("ug_evac"), 12)
            quantise(2, upf)
            dve.wait_ge(sem("sig_exp"), 1)
            link(dve.tensor_scalar(sigf, sigf, 1.0, None, ALU.add))
            link(dve.reciprocal(sigf, sigf))
            link(dve.tensor_scalar(sigf, sigf, 65536.0, ROUND, ALU.mult, ALU.add))
            link(dve.tensor_scalar(sigf, sigf, ROUND, 0.0, ALU.subtract, ALU.max))
            link(dve.tensor_scalar(sigf, sigf, 65535.0, 1.0 / 65536.0, ALU.min, ALU.mult))
            link(dve.tensor_tensor(tmpf, gatef, sigf, ALU.mult))
            quantise(3, tmpf)
            link(dve.tensor_tensor(gatef, tmpf, upf, ALU.mult))
            quantise(4, gatef, "o_q")
            for t in range(NT):
                dve.wait_ge(sem("down_mm"), 4 * (t // 4) + 4)
                dve.tensor_tensor(x[:, t, :], banks[t // 4][:, (t % 4) * P:(t % 4 + 1) * P], x[:, t, :], ALU.add)\
                    .then_inc(sem("y_out"), 1)

        @block.scalar
        def _(act):
            act.sem_inc(sem("p0_exp"), 2)
            act.sem_inc(sem("ps_exp"), 2)
            act.sem_inc(sem("s_evac"), 1)
            act.sem_inc(sem("c_evac"), 1)
            act.sem_inc(sem("p1_exp"), 2)
            act.sem_inc(sem("o0_evac"), 1)

            def sqrt(name, nt):
                act.wait_ge(sem(name + "_var"), 1)
                act.activation(sdev[:, 0:nt], sdev[:, 0:nt], ACT.Sqrt).then_inc(sem(name + "_sd"), 1)

            def columns(name, dst, nt, gamma=None):
                for i in range(0, nt, 4):
                    n = min(4, nt - i) * P
                    act.wait_ge(sem(name + "_mm"), i // 4 + 1)
                    act.activation(dst[:, i * P:i * P + n], banks[i // 4 % 4][:, 0:n], ACT.Copy,
                                   scale=1.0 if gamma is None else gamma).then_inc(sem(name + "_t"), 1)

            act.wait_ge(sem("const_in"), 16 * 5)
            sqrt("ln_a0", NT)
            act.wait_ge(sem("ln_a0_xn"), 1)
            act.wait_ge(sem("masks"), 1)

            def hi_k0(i, g, w):
                act.wait_ge(sem("k0_mm"), i + 1)
                act.wait_ge(sem("k0_split"), i + 3)
                act.activation(hi_tmp[g % 2][:, 0:w], banks[g][:, 0:w], ACT.Identity, bias=kb0[g]).then_inc(sem("k0_hi"), 1)

            with act.Fori(0, PCH - 1) as c:
                for g in range(G0):
                    hi_k0(4 * c + g, g, HALF)
            for g in range(G0):
                hi_k0(4 * (PCH - 1) + g, g, PW[-1])
            act.wait_ge(sem("v0_ones"), 1)
            v0h = v0.rearrange("p t (h c) -> p t h c", c=9)
            for i in range(PCH):
                act.wait_ge(sem("v0_mm"), i + 1)
                n = min(4, KT - 4 * i)
                for t in range(n):
                    last = act.activation(v0h[:, 4 * i + t, :, 0:HD0],
                                          banks[i % 4][:, t * P:(t + 1) * P].rearrange("p (h c) -> p h c", c=HD0), ACT.Copy)
                last.then_inc(sem("v0_evac"), 1)
            columns("ln_a0", xt, NT)
            for i in range(2 * H):
                act.wait_ge(sem("q0_y"), i + 1)
                act.activation(hi_tmp[i % 2], y_tmp[i % 2], ACT.Copy).then_inc(sem("q0_hi"), 1)

            act.preload_act_table(ACT.Exp)
            act.wait_ge(sem("v0_evac"), PCH)

            def exp0(b, n, u):
                kt = 3 * n + u
                i = 51 * b + kt
                act.wait_ge(sem("o0_mm"), i + 1)
                act.activation(v_stage[:, u, 0:36], v0[:, ds(kt, 1), ds((b // 2) * 36, 36)].rearrange("p a b -> p (a b)"),
                               ACT.Copy).then_inc(sem("v0_staged"), 1)
                for hp in range(2):
                    act.wait_ge(sem("s0_mm"), 2 * i + hp + 1)
                    act.wait_ge(sem("o0_mm"), i + 2 + hp)
                    act.activation(probs[:, (2 * u + hp) % 3, :], ps_s[:, hp, :], ACT.Exp).then_inc(sem("p0_exp"), 1)

            def block0(b, more):
                exp0(b, 0, 1)
                exp0(b, 0, 2)
                with act.Fori(1, KT // 3) as n:
                    for u in range(3):
                        exp0(b, n, u)
                if more:
                    exp0(b + 1, 0, 0)
                act.wait_ge(sem("o0_mm"), 51 * b + 51 + 3)
                act.activation(o0[:, ds(b // 2, 1), ds((b % 2) * HALF, HALF)].rearrange("p a b -> p (a b)"), ps_o[:, :], ACT.Copy)\
                    .then_inc(sem("o0_evac"), 1)

            exp0(0, 0, 0)
            with act.Fori(0, 7) as b:
                block0(b, True)
            block0(7, False)

            sqrt("ln_f0", NT)
            columns("ln_f0", xt, NT)
            ex = y_tmp[0][:, 64:128]
            act.wait_ge(sem("moe_d"), 1)
            act.activation(ex, ex, ACT.Exp).then_inc(sem("moe_exp"), 1)
            act.wait_ge(sem("moe_tr"), 1)
            act.activation(xt[:, :], ps_s[:, 1, :], ACT.Copy).then_inc(sem("moe_ht"), 1)

            sqrt("ln_cx", KT)
            columns("ln_cx", c_t, KT, col(C_GC))
            act.wait_ge(sem("k2_const"), 3)
            for i in range(PCH):
                act.wait_ge(sem("k1_mm"), i + 1)
                act.activation(k1[:, i * HALF:i * HALF + PW[i]], banks[i % 4][:, 0:PW[i]], ACT.Copy).then_inc(sem("k1_hi"), 1)
            for i in range(7):
                act.wait_ge(sem("v1_mm"), i + 1)
                n = min(8, KT - 8 * i)
                act.activation(v1[:, 8 * i:8 * i + n, :].rearrange("p a b -> p (a b)"), banks[i % 4][:, 0:n * HD1], ACT.Copy)\
                    .then_inc(sem("v1_evac"), 1)
            sqrt("ln_a1", NT)
            sqrt("ln_pb", NT)
            columns("ln_pb", xt, NT, col(C_GP))

            for i in range(8):
                act.wait_ge(sem("ff_mm"), i + 1)
                if i >= 2:
                    act.wait_ge(sem("ff_done"), i - 1)
                act.activation(y_tmp[i % 2], banks[2 * (i % 2) + 1], ACT.Exp, scale=-1.0).then_inc(sem("ff_exp"), 1)
            for i in range(2):
                act.wait_ge(sem("k1s_mm"), i + 1)
                act.activation(k1s[:, i * HALF:(i + 1) * HALF], banks[i], ACT.Copy).then_inc(sem("k1s_hi"), 1)
            act.wait_ge(sem("v1s_mm"), 1)
            act.activation(v1s.rearrange("p a b -> p (a b)"), banks[2], ACT.Copy).then_inc(sem("v1s_evac"), 1)

            def hi_queries(name):
                for i in range(2 * H):
                    act.wait_ge(sem(name + "_mm"), i + 1)
                    s = slice(i * HALF, (i + 1) * HALF)
                    act.activation(q2[0:64, s], banks[i % 4][0:64, :], ACT.Copy, scale=HD1 ** -0.5)
                    act.activation(q1[:, s], banks[i % 4], ACT.Copy, scale=HD1 ** -0.5).then_inc(sem(name + "_hi"), 1)

            hi_queries("qs")

            def exp_s(h, t):
                i = 8 * h + t
                act.wait_ge(sem("ss_mm"), i + 1)
                act.wait_ge(sem("os_mm"), i + 1)
                act.wait_ge(sem("s_add"), i + 1)
                act.activation(p_slot(t)[:, P * t:T], ps_s[:, t % 2, P * t:T], ACT.Exp).then_inc(sem("ps_exp"), 1)

            def shift_copies(k, h):
                act.wait_ge(sem(k + "_turned"), h + 1)
                act.activation(q2[64:96, ds(h * T, HALF)], ps_t[64:96, :], ACT.Copy)
                act.activation(q2[64:96, ds(h * T + HALF, HALF)], ps_t[96:128, :], ACT.Copy).then_inc(sem(k + "_shifted"), 1)

            def head_s(h, more=True):
                for t in range(1, NT):
                    exp_s(h, t)
                    if t == 1 and more:
                        shift_copies("s", h + 1)
                if more:
                    exp_s(h + 1, 0)
                act.wait_ge(sem("os_mm"), 8 * h + 8 + 4)
                act.activation(o1[:, ds(h, 1), :].rearrange("p a b -> p (a b)"), ps_o[:, :], ACT.Copy).then_inc(sem("s_evac"), 1)

            act.preload_act_table(ACT.Exp)
            shift_copies("s", 0)
            exp_s(0, 0)
            with act.Fori(0, H - 1) as h:
                head_s(h)
            head_s(H - 1, more=False)

            sqrt("ln_ca", NT)
            columns("ln_ca", xt, NT, col(C_GX))
            hi_queries("qc")

            act.preload_act_table(ACT.Exp)

            def exp_c(h, n, u, first=False):
                i = 51 * h + 3 * n + u
                act.wait_ge(sem("o1_mm"), i + 1)
                act.activation(v_stage[:, u, :], v1[:, ds(3 * n + u, 1), :].rearrange("p a b -> p (a b)"), ACT.Copy)\
                    .then_inc(sem("v1_staged"), 1)
                act.wait_ge(sem("s1_mm"), i + 1)
                if u == 0 or first and u == 2:
                    act.wait_ge(sem("c_add_v"), 18 * h + n + 2)
                else:
                    act.wait_ge(sem("c_add_g"), 33 * h + (2 if first else 2 * n + u))
                act.activation(probs[:, u, :], ps_flat[:, ds(((h + n + u) % 2) * (2 * HALF), 2 * HALF)], ACT.Exp)\
                    .then_inc(sem("p1_exp"), 1)

            def head_c(h, more=True):
                for u in range(3):
                    exp_c(h, 0, u, first=True)
                with act.Fori(1, KT // 3) as n:
                    for u in range(3):
                        exp_c(h, n, u)
                if more:
                    shift_copies("c", h + 1)
                act.wait_ge(sem("o1_mm"), 51 * h + 51 + 3)
                act.activation(o1[:, ds(h, 1), :].rearrange("p a b -> p (a b)"), ps_o[:, :], ACT.Copy).then_inc(sem("c_evac"), 1)

            shift_copies("c", 0)
            with act.Fori(0, H - 1) as h:
                head_c(h)
            head_c(H - 1, more=False)

            act.wait_ge(sem("qw_mm"), 1)
            act.activation(qwt.rearrange("p a b d -> p (a b d)")[:, 0:8 * P], ps_m[:, :], ACT.Copy)
            act.activation(qwt[:, 2, 2, :], ps_t[:, 0:P], ACT.Copy).then_inc(sem("qw_t"), 1)
            sqrt("ln_f1", NT)
            columns("ln_f1", xt, NT)
            for n in range(12):
                i = n % 6
                dst = (gate, up)[n // 6]
                act.wait_ge(sem("ug_mm"), n + 1)
                act.activation(dst[:, i // 2, (i % 2) * HALF:(i % 2 + 1) * HALF], banks[n % 4], ACT.Copy).then_inc(sem("ug_evac"), 1)
            act.wait_ge(sem("gate_q"), 1)
            act.activation(sig.rearrange("p a b -> p (a b)"), gate.rearrange("p a b -> p (a b)"), ACT.Exp, scale=-1.0)\
                .then_inc(sem("sig_exp"), 1)

        @block.gpsimd
        def _(pool):
            pool.sem_inc(sem("c_add_g"), 2)
            pool.sem_inc(sem("s_add"), 4)
            pool.sem_inc(sem("s_o"), 1)
            pool.memset(zeros16[:, :], 0.0).then_inc(sem("zeros"), 1)
            pool.wait_ge(sem("zeros"), 1)
            pool.memset(shift_rows[:, :], 0.0).then_inc(sem("zeros"), 1)
            pool.wait_ge(sem("zeros"), 2)
            pool.memset(v0.rearrange("p a b -> p (a b)"), 1.0).then_inc(sem("v0_ones"), 1)
            pool.wait_ge(sem("v0_ones"), 1)

            pool.wait_ge(sem("const_in"), 16 * 5)
            pool.wait_ge(sem("v0_mm"), PCH)
            pool.memset(k2[64:128, :], 0.0).then_inc(sem("k2_const"), 1)
            pool.wait_ge(sem("k2_const"), 1)
            pool.tensor_scalar(k2[64:128, 0:CTX], k2[64:128, 0:CTX], col(C_ONE1, 64, 128), None, ALU.add)\
                .then_inc(sem("k2_const"), 1)
            pool.wait_ge(sem("k2_const"), 2)
            pool.tensor_scalar(k2[64:128, CTX:CTXP], k2[64:128, CTX:CTXP], col(C_PAD1, 64, 128), None, ALU.add)\
                .then_inc(sem("k2_const"), 1)
            pool.wait_ge(sem("k2_const"), 3)
            pool.wait_ge(sem("m0_turned"), 8)
            pool.memset(shift_rows[:, :], 0.0).then_inc(sem("shift_zero"), 1)
            pool.wait_ge(sem("shift_zero"), 1)
            pool.memset(shift_rows[:, 0:8 * 32].rearrange("p (t r) -> p t r", r=32)[:, :, 3], 1.0).then_inc(sem("shift_zero"), 1)
            pool.wait_ge(sem("shift_zero"), 2)
            pool.wait_ge(sem("o0_mm"), 51 * 8 + 3)
            pool.memset(q2[96:128, :], 0.0).then_inc(sem("q2_zero"), 1)
            pool.wait_ge(sem("q2_zero"), 1)
            pool.wait_ge(sem("k1_mm"), PCH)
            pool.wait_ge(sem("v1_mm"), 7)
            pool.memset(k2s[64:128, :], 0.0).then_inc(sem("k2s_const"), 1)
            pool.wait_ge(sem("k2s_const"), 1)
            pool.tensor_scalar(k2s[64:128, :], k2s[64:128, :], col(C_ONE1, 64, 128), None, ALU.add).then_inc(sem("k2s_const"), 1)
            pool.wait_ge(sem("k2s_const"), 2)

            pool.wait_ge(sem("ff_done"), 8)
            pool.memset(probs[:, 1, 0:P], 0.0).then_inc(sem("p1_zero"), 1)
            pool.wait_ge(sem("p1_zero"), 1)

            def normalise_s(h):
                pool.wait_ge(sem("s_recip"), 2 * h + 2 + 2)
                pool.wait_ge(sem("s_evac"), h + 1 + 1)
                o = o1[:, ds(h, 1), :].rearrange("p a b -> p (a b)")
                pool.tensor_tensor(o, o, recip[:, :], ALU.mult).then_inc(sem("s_o"), 1)
                pool.wait_ge(sem("s_o"), h + 1 + 1)

            def head_s(h, first=False):
                acc = accs[:, ds(h % 2, 1), :].rearrange("p a b -> p (a b)")
                pool.wait_ge(sem("ps_exp"), 8 * h + 1 + 3)
                pool.wait_ge(sem("s_sums"), h + 1)
                pool.tensor_tensor(acc, probs[:, 0, :], probs[:, 1, :], ALU.add).then_inc(sem("s_add"), 2)
                for t in range(2, NT):
                    pool.wait_ge(sem("ps_exp"), 8 * h + t + 3)
                    pool.wait_ge(sem("s_add"), 8 * h + t + 4)
                    part = accs[:, ds(h % 2, 1), P * t:T].rearrange("p a b -> p (a b)")
                    pool.tensor_tensor(part, part, p_slot(t)[:, P * t:T], ALU.add).then_inc(sem("s_add"), 1)
                    if t == 5 and not first:
                        pool.wait_ge(sem("s_add"), 8 * h + t + 1 + 4)
                        normalise_s(h - 1)

            head_s(0, first=True)
            with pool.Fori(1, H) as h:
                head_s(h)
            normalise_s(H - 1)

            def add_g(h, n, u):
                pool.wait_ge(sem("p1_exp"), 51 * h + 3 * n + u + 3)
                pool.wait_ge(sem("c_add_g"), 33 * h + 2 * n + u - 1 + 2)
                pool.tensor_tensor(acc_g, acc_g, probs[:, u, :], ALU.add).then_inc(sem("c_add_g"), 1)

            with pool.Fori(0, H) as h:
                pool.wait_ge(sem("p1_exp"), 51 * h + 2 + 3)
                pool.wait_ge(sem("c_sums"), h + 1)
                pool.tensor_tensor(acc_g, probs[:, 1, :], probs[:, 2, :], ALU.add).then_inc(sem("c_add_g"), 2)
                with pool.Fori(1, KT // 3 - 1) as n:
                    add_g(h, n, 1)
                    add_g(h, n, 2)
                add_g(h, KT // 3 - 1, 1)

            for n in range(5):
                pool.wait_ge(sem("q_amax"), n + 1)
                pool.partition_all_reduce(y_tmp[0][:, 136 + n:137 + n], y_tmp[0][:, 128 + n:129 + n], P, RMAX)\
                    .then_inc(sem("q_gmax"), 1)


def laid_out(i):
    f = {k: np.ascontiguousarray(v) for k, v in i.items()}
    z = lambda *s: np.zeros(s, np.float32)
    o = {"x": f["x"].reshape(T, D)}
    ctx_rows = z(CTXP, D)
    ctx_rows[:CTX] = f["ctx_1024"][0]
    o["ctx"] = ctx_rows
    o["ctx_t"] = np.ascontiguousarray(ctx_rows.T)
    cols = z(P, 34)
    wk, wq, wo = z(P, G0, P), z(P, H, P), z(P, G0, P)
    wkt, wqt, wot = f["L0_xattn_Wk"].T, f["L0_xattn_Wq"].T, f["L0_xattn_Wo"].T
    for h in range(H):
        g, j = divmod(h, 4)
        s = slice(h * HD0, (h + 1) * HD0)
        for r in range(3):
            d = slice(32 * j + 8 * r, 32 * j + 8 * r + 8)
            wk[:, g, d] = wkt[:, s]
            wq[:, h, d] = wqt[:, s]
            cols[d, g] = f["L0_xattn_bk"][s]
            cols[d, 4 + h] = f["L0_xattn_bq"][s]
        cols[32 * j + ROW_SHIFT0:32 * j + ROW_SHIFT0 + 3, g] = 1
        cols[32 * j + ROW_PAD0, 4 + h] = 1
        wo[32 * j:32 * j + 8, g, :] = wot[s]
    r = np.arange(P) % 32
    cols[:, 20] = np.where(r < ROW_SHIFT0, np.float32(1 / np.sqrt(HD0)), 1)
    cols[:, 21] = (r >= 16) & (r < 24)
    cols[:, 22] = (r >= 8) & (r < 16)
    cols[:, 23] = np.where(r == ROW_PAD0, PAD_SCORE, 0)
    cols[ROW_SHIFT1:ROW_SHIFT1 + 3, 24] = 1
    cols[ROW_PAD1, 25] = PAD_SCORE
    cols[ROW_PAD1, 26] = 1
    cols[:, 27] = f["L1_xattn_ptb_gamma"]
    cols[:, 28] = f["L1_xattn_ca_ctx_gamma"]
    cols[:, 29] = f["L1_xattn_ca_gamma"]
    o["cols"] = cols
    o["wk0"], o["wq0"], o["wo0"] = wk, wq, wo
    o["wv0"] = np.ascontiguousarray(f["L0_xattn_Wv"].T)
    o["rows0"] = np.concatenate([f["L0_xattn_bv"], f["L0_xattn_bo"]])[None]
    o["wg0"] = f["L0_ffn_Wg"]
    o["moe_a"] = np.ascontiguousarray(f["L0_ffn_A"].transpose(1, 0, 2).reshape(D, E * R))
    o["moe_b"] = f["L0_ffn_B"].reshape(E * R, D)
    sel = z(P, P)
    for j in range(4):
        sel[32 * j + 8, 32 * j:32 * j + 32] = 1
    o["sel_sum"] = sel
    o["ident"] = np.eye(P, dtype=np.float32)
    o["ones"] = np.ones((P, P), np.float32)
    o["ident16"] = np.eye(P, dtype=np.float16)
    k, q = np.arange(P)[:, None], np.arange(P)[None]
    o["masks"] = np.concatenate([np.where(k > q, MASKED, 0), np.where(k < q, MASKED, 0)], 1).astype(np.float32)

    wf = f["L1_xattn_W_fused"]
    inner = H * HD1

    def twice(w):
        w = w.reshape(D, H, 1, HD1)
        return np.ascontiguousarray(np.broadcast_to(w, (D, H, 2, HD1)).reshape(D, H, P))

    def kkv(w):
        return np.concatenate([w[:, :HD1], w[:, :HD1], w[:, HD1:]], 1)

    def halves(w):
        m = z(P, H, 2 * D)
        for h in range(H):
            m[0:HD1, h, 0:D] = w[h * HD1:(h + 1) * HD1]
            m[HD1:P, h, D:] = w[h * HD1:(h + 1) * HD1]
        return m

    o["wq_s"] = twice(wf[:, :inner])
    o["wkv_s"] = kkv(wf[:, inner:inner + 2 * HD1])
    o["wff"] = np.ascontiguousarray(wf[:, inner + 2 * HD1:])
    o["wffo"] = np.ascontiguousarray(f["L1_xattn_W_ff_out"].reshape(FFI // P, P, D).transpose(1, 0, 2))
    o["wo_s"] = halves(f["L1_xattn_W_attn_out"])
    o["wq_c"] = twice(f["L1_xattn_W_q"])
    o["wkv_c"] = kkv(f["L1_xattn_W_kv"])
    o["wo_c"] = halves(f["L1_xattn_W_out"])
    rows = lambda w: w.reshape(3, P, D).transpose(1, 0, 2)
    o["qw"] = np.ascontiguousarray(np.stack([rows(f["L1_ffn_w_gate"]), rows(f["L1_ffn_w_up"]),
                                             f["L1_ffn_w_down"].reshape(D, 3, P)], 1))
    return {k: np.ascontiguousarray(v) for k, v in o.items()}


def kernel(**inputs):
    import concourse.bacc as bacc
    from concourse.bass_utils import run_bass_kernel_spmd

    arrays = laid_out(inputs)
    nc = bacc.Bacc("TRN2", target_bir_lowering=False, num_devices=1)
    args = {k: nc.dram_tensor("in_" + k, v.shape, mybir.dt.from_np(v.dtype), kind="ExternalInput").ap()
            for k, v in arrays.items()}
    out = nc.dram_tensor("out_x", (T, D), F32, kind="ExternalOutput").ap()
    build(nc, args, out)
    r = run_bass_kernel_spmd(nc, [{"in_" + k: v for k, v in arrays.items()}], core_ids=[0])
    return r.results[0]["out_x"].reshape(1, T, D)
```

```python
from contextlib import ExitStack

import numpy as np
import concourse.bass as bass
from concourse import mybir

F32 = mybir.dt.float32
F16 = mybir.dt.float16
BF16 = mybir.dt.bfloat16
ALU = mybir.AluOpType
ACT = mybir.ActivationFunctionType
AX = mybir.AxisListType
RMAX = bass.bass_isa.ReduceOp.max

P = 128
D = 128
T = 1024
NT = T // P
CTX = 6404
KT = -(-CTX // P)
CTXP = KT * P
HALF = 512
H = 16
HD0 = 8
HD1 = 64
G0 = H // 4
E, R = 8, 16
FFI = 512
QI = 384
BLK = 32
EPS = 1e-5
PAD_SCORE = -30000.0
MASKED = -1e30
ROUND = 1.5 * 2.0 ** 23
QMAX = 32767.0
NCH = -(-CTX // HALF)
CW = [min(HALF, CTX - c * HALF) for c in range(NCH)]
PCH = -(-CTXP // HALF)
PW = [min(HALF, CTXP - c * HALF) for c in range(PCH)]
ROW_SHIFT0, ROW_PAD0 = 24, 27
ROW_SHIFT1, ROW_PAD1 = 64, 67
CHUNKS0 = [range(0, 4), range(4, 9), range(9, 13)]
FIRST0 = [("k", 0, c) for c in range(PCH)] + [("q", h, f) for h in range(4) for f in range(2)]
_QS = [("q", h, f) for h in range(4, H) for f in range(2)]
OTHER0 = [item for c in range(PCH) for item in [("k", g, c) for g in range(1, G0)] + _QS[2 * c:2 * c + 2] + [("v", c, 0)]]
ITEMS0 = FIRST0 + OTHER0
NSPLIT = sum(kind != "v" for kind, _, _ in ITEMS0)
CHUNKS_S = [(t, c0, min(HALF, P * (t + 1) - c0)) for t in range(NT) for c0 in range(0, P * (t + 1), HALF)]
STEPS_S = [range(0, 2), range(2, 4), range(4, 6), range(6, 7), range(7, 8), range(8, 9), range(9, 11), range(11, 12)]
CHUNKS1 = [range(0, 3), range(3, 5), range(5, 7), range(7, 9), range(9, 11), range(11, 13)]
CHUNKS1_LAST = [range(0, 3), range(3, 7), range(7, 10), range(10, 13), (), ()]


class Chain:

    def __init__(self, eng, sem, base=0, per=None):
        self.eng, self.sem, self.base, self.n, self.per = eng, sem, base, 0, per

    def __call__(self, ins):
        self.n += 1
        ins.then_inc(self.sem, 1)
        self.eng.wait_ge(self.sem, self.base + self.n)

    def check(self):
        assert self.n == self.per, self.n


def build(nc, a, out):
    with ExitStack() as ctx:
        def sb(name, shape, dt=F32):
            return ctx.enter_context(nc.sbuf_tensor(name, shape, dt))

        def ps(name, shape):
            return ctx.enter_context(nc.psum_tensor(name, shape, F32))

        sems = {}

        def sem(name):
            if name not in sems:
                sems[name] = ctx.enter_context(nc.semaphore(name))
            return sems[name]

        arena_a = sb("arena_a", [P, G0 * CTXP // 2])
        arena_b = sb("arena_b", [P, H * T // 2])
        arena_c = sb("arena_c", [P, CTXP])
        arena_d = sb("arena_d", [P, 7680])
        arena_e = sb("arena_e", [P, H * HALF])
        probs = sb("probs", [P, 3, 2 * HALF])

        def view(arena, at, shape, dt=F32):
            n = int(np.prod(shape))
            words = n if dt == F32 else n // 2
            v = arena[:, at:at + words]
            if dt != F32:
                v = v.bitcast(dt)
            if len(shape) == 2:
                v = v.rearrange("p (a b) -> p a b", a=shape[0])
            if len(shape) == 3:
                v = v.rearrange("p (a b c) -> p a b c", a=shape[0], b=shape[1])
            return v

        k0 = view(arena_a, 0, [G0 * CTXP], F16)
        q0 = view(arena_b, 0, [H * T], F16)
        ctx_t = view(arena_c, 0, [CTXP])
        v0 = view(arena_d, 0, [KT, H * 9])
        o0 = view(arena_e, 0, [G0, T])
        wq0 = view(arena_e, 4096, [H, P])
        wk0 = view(arena_e, 6144, [G0, P])
        wv0 = view(arena_e, 6656, [P])
        wo0 = view(arena_e, 6784, [G0, P])
        wg0 = view(arena_e, 7296, [E])
        moe_a = view(arena_e, 7304, [P])
        moe_b = view(arena_e, 7432, [P])
        rows0 = view(arena_e, 7560, [2 * P])

        c_nat = view(arena_e, 0, [KT, D])
        c_t = view(arena_d, 0, [CTXP])
        k1 = view(arena_c, 0, [CTXP], F16)
        k2 = view(arena_c, CTXP // 2, [CTXP], F16)
        v1 = view(arena_a, H * T // 2, [KT, HD1])
        wkv_c = view(arena_e, 6528, [3 * HD1])

        q2 = view(arena_a, 0, [H * T], F16)
        q1 = view(arena_b, 0, [H * T], F16)
        o1 = view(arena_e, 0, [H, HALF])
        wq1 = view(arena_e, 0, [H, P])
        wkv_s = view(arena_e, 2048, [3 * HD1])
        wff = view(arena_e, 2240, [2 * FFI])
        wffo = view(arena_e, 3264, [FFI // P, D])
        gated = view(arena_e, 3776, [FFI // P, T])
        k1s = view(arena_d, 0, [T], F16)
        k2s = view(arena_d, T // 2, [T], F16)
        v1s = view(arena_d, T, [NT, HD1])
        wproj = view(arena_d, 1536, [H, 2 * D])
        acc_v = view(arena_d, 5632, [2 * HALF])
        acc_g = view(arena_d, 6656, [2 * HALF])
        accs = view(arena_d, 5632, [2, 2 * HALF])
        probs_3 = view(arena_a, H * T // 2 + KT * HD1, [2 * HALF])

        qw = view(arena_a, 0, [3, 3, D])
        qwq = view(arena_a, 1152, [3, 3, D])
        qwt = view(arena_a, 2304, [3, 3, D])
        up = view(arena_b, 0, [3, T])
        gate = view(arena_b, 3072, [3, T])
        sig = view(arena_c, 0, [3, T])
        tmp = view(arena_c, 3072, [3, T])

        x = sb("x", [P, NT, D])
        xn = sb("xn", [P, NT, D])
        xt = sb("xt", [P, T])
        ident = sb("ident", [P, P])
        ident16 = sb("ident16", [P, P], F16)
        identb = sb("identb", [P, P], BF16)
        mask_kq = sb("mask_kq", [P, P], BF16)
        mask_qk = sb("mask_qk", [P, P], BF16)
        zeros16 = sb("zeros16", [P, P], F16)
        sel_sum = sb("sel_sum", [P, P])
        ones = sb("ones", [P, P])
        cols = sb("cols", [P, 34])
        shift_rows = sb("shift_rows", [P, 4 * P], F16)
        v_stage = sb("v_stage", [P, 3, HD1])
        mpart = sb("mpart", [P, 16])
        mx = sb("mx", [P, 16])
        mrest = sb("mrest", [P, 2, 16])
        recip = sb("recip", [P, HALF])
        qb0s = sb("qb0s", [P, H])
        stats = probs[:, 2, 0:6 * KT].rearrange("p (t s) -> p t s", s=6)
        mv = probs[:, 2, 320:320 + 2 * KT].rearrange("p (t s) -> p t s", s=2)
        sdev = probs[:, 2, 430:430 + KT]
        rstd = probs[:, 2, 490:490 + KT]
        hm_tmp = [probs[:, 0, 512 + 256 * i:768 + 256 * i].bitcast(F16) for i in range(2)]
        hn = probs[:, 0, :].rearrange("p (t d) -> p t d", t=NT)
        y_tmp = [probs[:, 1, 512 * i:512 * i + 512] for i in range(2)]

        kb0 = [cols[:, g:g + 1] for g in range(4)]
        qb0 = [cols[:, 4 + h:5 + h] for h in range(H)]
        C_QS, C_KLO, C_QLO, C_PAD0, C_ONE1, C_PAD1, C_GP, C_GC, C_GX = (20, 21, 22, 23, 24, 25, 27, 28, 29)

        def col(i, lo=0, hi=P):
            return cols[lo:hi, i:i + 1]

        ps_s = ps("ps_s", [P, 2, 2 * HALF])
        ps_o = ps("ps_o", [P, HALF])
        ps_m = ps("ps_m", [P, 2 * HALF])
        ps_t = ps("ps_t", [P, HALF])
        banks = [ps_s[:, i // 2, (i % 2) * HALF:(i % 2 + 1) * HALF] for i in range(4)]

        ps_flat = ps_s[:, :, :].rearrange("p a b -> p (a b)")

        def p_slot(t):
            return probs_3 if t % 4 == 3 else probs[:, t % 4, :]

        def mslot(c):
            return ps_m[:, (c % 2) * HALF:(c % 2 + 1) * HALF]

        def mslot3(c):
            return ps_t[:, :] if c % 3 == 2 else ps_m[:, 0:HALF] if c % 3 == 0 and c < NCH - 1 else ps_m[:, HALF:]

        ds = bass.ds

        def subtract_hi(eng, n, j):
            kind, i, c = ITEMS0[n]
            if kind == "k":
                at, w = i * CTXP + c * HALF, PW[c]
                dst = k0[:, at:at + w]
            else:
                at, w = i * T + c * HALF, HALF
                dst = q0[:, at:at + w]
            return eng.tensor_tensor(dst, y_tmp[j % 2][:, 0:w], hm_tmp[j % 2][:, 0:w], ALU.subtract)

        block = ctx.enter_context(nc.Block())

        @block.sync
        def _(sp):
            def load(dst, src, name, after=()):
                for s, v in after:
                    sp.wait_ge(sem(s), v)
                sp.dma_start(dst, src).then_inc(sem(name), 16)

            load(x[:, :, :], a["x"].rearrange("(t p) d -> p t d", p=P), "x_in")
            load(cols[:, :], a["cols"], "const_in")
            load(ident[:, :], a["ident"], "const_in")
            load(ones[:, :], a["ones"], "const_in")
            load(ident16[:, :], a["ident16"], "const_in")
            load(probs[:, 0, 0:2 * P], a["masks"], "masks_in")
            load(sel_sum[:, :], a["sel_sum"], "const_in")
            load(wk0, a["wk0"], "w0_in")
            load(wv0, a["wv0"], "w0_in")
            load(wq0, a["wq0"], "w0_in")
            load(wo0, a["wo0"], "w0_in")
            load(wg0, a["wg0"], "w0_in")
            load(moe_a, a["moe_a"], "w0_in")
            load(moe_b, a["moe_b"], "w0_in")
            load(rows0[0:1], a["rows0"], "w0_in")
            for i in range(4):
                lo, hi = i * CTXP // 4, (i + 1) * CTXP // 4
                load(ctx_t[:, lo:hi], a["ctx_t"][:, lo:hi], "ctx_in")
            load(c_nat, a["ctx"].rearrange("(t p) d -> p t d", p=P), "ctx1_in", [("moe_out", NT)])
            load(wkv_c, a["wkv_c"], "ctx1_in")
            w1 = [("k1_split", PCH), ("v1_evac", 7)]
            load(wq1, a["wq_s"], "w1_in", w1)
            load(wkv_s, a["wkv_s"], "w1_in")
            load(wff, a["wff"], "w1_in")
            load(wffo, a["wffo"], "w1_in")
            load(wproj, a["wo_s"], "w1_in")
            load(wq1, a["wq_c"], "w2_in", [("sp_mm", 1)])
            load(wproj, a["wo_c"], "w2_in")
            load(qw, a["qw"], "qw_in", [("cp_mm", 1)])
            for t in range(NT):
                sp.wait_ge(sem("y_out"), t + 1)
                sp.dma_start(out[t * P:(t + 1) * P, :], x[:, t, :]).then_inc(sem("stored"), 16)
            sp.wait_ge(sem("stored"), 16 * NT)

        @block.tensor
        def _(pe):
            def mm(o, l, r, start=True, stop=True):
                return pe.matmul(o, l, r, start=start, stop=stop, skip_group_check=True)

            def ln_transposes(name, src, nt):
                pe.wait_ge(sem(name + "_xn"), 1)
                for i in range(0, nt, 4):
                    if i >= 16:
                        pe.wait_ge(sem(name + "_t"), i // 4 - 3)
                    for t in range(i, min(i + 4, nt)):
                        last = pe.transpose(banks[i // 4 % 4][:, (t % 4) * P:(t % 4 + 1) * P], src[:, t, :], ident[:, :])
                    last.then_inc(sem(name + "_mm"), 1)

            pe.sem_inc(sem("o0_mm"), 3)
            pe.sem_inc(sem("os_mm"), 4)
            pe.sem_inc(sem("o1_mm"), 3)
            pe.sem_inc(sem("s_sums"), 2)
            pe.sem_inc(sem("c_sums"), 1)
            pe.wait_ge(sem("const_in"), 16 * 5)
            pe.wait_ge(sem("zeros"), 2)
            pe.wait_ge(sem("w0_in"), 16 * 8)
            ln_transposes("ln_a0", xn, NT)
            pe.wait_ge(sem("ctx_in"), 16 * 4)
            pe.wait_ge(sem("ln_a0_t"), 2)

            def operand0(n):
                kind, i, j = ITEMS0[n]
                if n >= 4:
                    pe.wait_ge(sem("item_read"), n - 3)
                bank = banks[n % 4]
                if kind == "k":
                    last = mm(bank[:, 0:PW[j]], wk0[:, i, :], ctx_t[:, j * HALF:j * HALF + PW[j]])
                elif kind == "q":
                    last = mm(bank, wq0[:, i, :], xt[:, j * HALF:(j + 1) * HALF])
                else:
                    for t in range(4 * i, min(4 * i + 4, KT)):
                        o = bank[:, (t % 4) * P:(t % 4 + 1) * P]
                        mm(o, ctx_t[:, t * P:(t + 1) * P], wv0, stop=False)
                        last = mm(o, ones[0:1, :], rows0[0:1, 0:P], start=False)
                last.then_inc(sem("item_mm"), 1)

            for n in range(len(FIRST0)):
                operand0(n)

            def q0_at(b):
                return (b // 2) * (4 * T) + (b % 2) * HALF

            def max_chunk0(b, n, c):
                m = 208 * b + 13 * n + c
                pe.wait_ge(sem("m0_red"), m + 2 if c in (1, NCH - 1) else m + 1)
                mm(mslot3(c)[:, 0:CW[c]], q0[:, ds(q0_at(b) + (n // 4) * T + (n % 4) * P, P)],
                   k0[:, ds((b // 2) * CTXP + c * HALF, CW[c])]).then_inc(sem("m0_mm"), 1)

            def shift0(b):
                pe.wait_ge(sem("m0_parts"), b + 1)
                for t in range(4):
                    last = mm(ps_t[:, t * P:(t + 1) * P], shift_rows[:, t * P:(t + 1) * P], ident16[:, :])
                last.then_inc(sem("m0_turned"), 1)

            def scores0(b, kt, hp):
                i = 102 * b + 2 * kt + hp
                pe.wait_ge(sem("p0_exp"), i + 1)
                for j in range(2):
                    last = mm(ps_s[:, hp, j * HALF:(j + 1) * HALF], k0[:, ds((b // 2) * CTXP + kt * P, P)],
                              q0[:, ds(q0_at(b) + (2 * hp + j) * T, HALF)])
                last.then_inc(sem("s0_mm"), 1)

            def pv0(b, kt, u, stop):
                pe.wait_ge(sem("v0_staged"), 51 * b + kt + 1)
                pe.wait_ge(sem("p0_exp"), 102 * b + 2 * kt + 4)
                for j in range(4):
                    last = mm(ps_o[32 * j:32 * j + 9, :], v_stage[:, u, 9 * j:9 * j + 9],
                              probs[:, (2 * u + j // 2) % 3, (j % 2) * HALF:(j % 2 + 1) * HALF], False, stop)
                last.then_inc(sem("o0_mm"), 1)

            def first_scores0(b, hp):
                pe.wait_ge(sem("q0_shifted"), 4 * b + 2 * hp + 2)
                scores0(b, 0, hp)

            def block0(b, more):
                def group(n, first, last):
                    for u in range(3):
                        kt = 3 * n + u
                        ch = list(CHUNKS0[u]) if more and not last else []
                        for hp in range(2):
                            if not (last and u == 2):
                                scores0(b, kt + 1, hp)
                            elif more:
                                first_scores0(b + 1, hp)
                            for c in ch[0:2] if hp == 0 else ch[2:-1]:
                                max_chunk0(b + 1, n, c)
                        if first and u == 0:
                            pe.wait_ge(sem("o0_evac"), b + 1)
                            mm(ps_o[:, :], zeros16[:, :], q0[:, 0:HALF], True, False)
                        pv0(b, kt, u, last and u == 2)
                        for c in ch[-1:]:
                            max_chunk0(b + 1, n, c)
                        if last and more and u == 0:
                            shift0(b + 1)

                group(0, True, False)
                with pe.Fori(1, 16) as n:
                    group(n, False, False)
                group(16, False, True)

            pe.wait_ge(sem("k0_pad"), 1)
            pe.wait_ge(sem("item_split"), len(FIRST0))
            made, chunks = len(FIRST0), 0
            for n in range(16):
                for c in range(NCH):
                    max_chunk0(0, n, c)
                    chunks += 1
                    if made < len(ITEMS0) and (made - len(FIRST0)) * 16 * NCH < chunks * len(OTHER0):
                        operand0(made)
                        made += 1
            assert made == len(ITEMS0)
            shift0(0)
            pe.wait_ge(sem("item_split"), NSPLIT)
            pe.wait_ge(sem("item_read"), len(ITEMS0))
            pe.wait_ge(sem("k0_pad_others"), G0 - 1)
            first_scores0(0, 0)
            first_scores0(0, 1)
            with pe.Fori(0, 7) as b:
                block0(b, True)
            block0(7, False)

            pe.wait_ge(sem("o0_evac"), 9)
            for i in range(8):
                if i >= 4:
                    pe.wait_ge(sem("o0_norm"), i - 3)
                mm(banks[i % 4], sel_sum[:, :], o0[:, i // 2, (i % 2) * HALF:(i % 2 + 1) * HALF]).then_inc(sem("sum0_mm"), 1)
            pe.wait_ge(sem("o0_norm"), 8)
            for t in range(NT):
                o = banks[t // 4][:, (t % 4) * P:(t % 4 + 1) * P]
                for g in range(G0):
                    mm(o, o0[:, g, t * P:(t + 1) * P], wo0[:, g, :], g == 0, False)
                last = mm(o, ones[0:1, :], rows0[0:1, P:2 * P], False)
            last.then_inc(sem("proj0_mm"), 1)

            pe.wait_ge(sem("x1"), 1)
            ln_transposes("ln_f0", xn, NT)
            pe.wait_ge(sem("ln_f0_t"), 2)
            for t in range(NT):
                mm(ps_t[:, t * E:(t + 1) * E], xt[:, t * P:(t + 1) * P], wg0)
            for t in range(NT):
                last = mm(banks[t // 4][:, (t % 4) * P:(t % 4 + 1) * P], xt[:, t * P:(t + 1) * P], moe_a)
            last.then_inc(sem("moe_mm"), 1)
            pe.wait_ge(sem("moe_hw"), 1)
            for t in range(NT):
                last = pe.transpose(banks[2 + t // 4][:, (t % 4) * P:(t % 4 + 1) * P], xn[:, t, :], ident[:, :])
            last.then_inc(sem("moe_tr"), 1)
            pe.wait_ge(sem("moe_ht"), 1)
            for t in range(NT):
                mm(banks[t // 4][:, (t % 4) * P:(t % 4 + 1) * P], xt[:, t * P:(t + 1) * P], moe_b).then_inc(sem("moe_out"), 1)

            pe.wait_ge(sem("x2"), 1)
            ln_transposes("ln_cx", c_nat, KT)
            pe.wait_ge(sem("ln_cx_t"), PCH)
            for i in range(PCH):
                if i >= 4:
                    pe.wait_ge(sem("k1_split"), i - 3)
                mm(banks[i % 4][:, 0:PW[i]], wkv_c[:, 0:P], c_t[:, i * HALF:i * HALF + PW[i]]).then_inc(sem("k1_mm"), 1)
            for i in range(7):
                if i < 4:
                    pe.wait_ge(sem("k1_split"), PCH)
                else:
                    pe.wait_ge(sem("v1_evac"), i - 3)
                for t in range(8 * i, min(8 * i + 8, KT)):
                    last = mm(banks[i % 4][:, (t % 8) * HD1:(t % 8 + 1) * HD1], c_t[:, t * P:(t + 1) * P], wkv_c[:, P:P + HD1])
                last.then_inc(sem("v1_mm"), 1)
            pe.wait_ge(sem("v1_evac"), 7)

            ln_transposes("ln_pb", hn, NT)
            pe.wait_ge(sem("ln_pb_t"), 2)
            pe.wait_ge(sem("w1_in"), 16 * 5)
            for i in range(8):
                if i >= 2:
                    pe.wait_ge(sem("ff_done"), i - 1)
                r, hf = i // 2, i % 2
                mm(banks[2 * (i % 2)], wff[:, r * P:(r + 1) * P], xt[:, hf * HALF:(hf + 1) * HALF])
                mm(banks[2 * (i % 2) + 1], wff[:, FFI + r * P:FFI + (r + 1) * P], xt[:, hf * HALF:(hf + 1) * HALF])\
                    .then_inc(sem("ff_mm"), 1)
            pe.wait_ge(sem("ff_done"), 8)
            for t in range(NT):
                for r in range(FFI // P):
                    last = mm(banks[t // 4][:, (t % 4) * P:(t % 4 + 1) * P], gated[:, r, t * P:(t + 1) * P], wffo[:, r, :],
                              r == 0, r == FFI // P - 1)
            last.then_inc(sem("ffo_mm"), 1)
            pe.wait_ge(sem("y_ff"), 1)
            for hf in range(2):
                mm(banks[hf], wkv_s[:, 0:P], xt[:, hf * HALF:(hf + 1) * HALF]).then_inc(sem("k1s_mm"), 1)
            for t in range(NT):
                last = mm(banks[2][:, t * HD1:(t + 1) * HD1], xt[:, t * P:(t + 1) * P], wkv_s[:, P:P + HD1])
            last.then_inc(sem("v1s_mm"), 1)
            pe.wait_ge(sem("k1s_split"), 2)
            pe.wait_ge(sem("v1s_evac"), 1)

            def query1(name, i, read):
                if i >= 4:
                    pe.wait_ge(sem(read), i - 3)
                mm(banks[i % 4], wq1[:, i // 2, :], xt[:, (i % 2) * HALF:(i % 2 + 1) * HALF]).then_inc(sem(name + "_mm"), 1)

            def max_chunk_s(h, n):
                t, c0, w = CHUNKS_S[n]
                pe.wait_ge(sem("sm_red"), 12 * h + n + 1)
                diagonal = c0 + w == P * (t + 1)
                last = mm(mslot(n)[:, 0:w], q1[:, ds(h * T + t * P, P)], k1s[:, c0:c0 + w], True, not diagonal)
                if diagonal:
                    last = mm(mslot(n)[:, w - P:w], identb[:, :], mask_qk[:, :], False, True)
                last.then_inc(sem("sm_mm"), 1)

            def shift1(k, h):
                pe.wait_ge(sem(k + "_parts"), h + 1)
                for t in range(NT):
                    at = 64 + 32 * (t // 4)
                    last = mm(ps_t[at:at + 32, (t % 4) * P:(t % 4 + 1) * P], shift_rows[:, t * 32:t * 32 + 32], ident16[:, :])
                last.then_inc(sem(k + "_turned"), 1)

            def scores_s(h, t):
                pe.wait_ge(sem("ps_exp"), 8 * h + t + 1)
                sl = ps_s[:, t % 2, :]
                parts = [(P * t, HALF), (HALF, T)] if t < 4 else [(P * t, T)]
                for lo, hi in parts:
                    mm(sl[:, lo:hi], k1s[:, t * P:(t + 1) * P], q1[:, ds(h * T + lo, hi - lo)], True, False)
                for lo, hi in parts:
                    mm(sl[:, lo:hi], k2s[:, t * P:(t + 1) * P], q2[:, ds(h * T + lo, hi - lo)], False, False)
                mm(sl[:, t * P:(t + 1) * P], identb[:, :], mask_kq[:, :], False, True).then_inc(sem("ss_mm"), 1)

            def pv_s(h, t):
                pe.wait_ge(sem("ps_exp"), 8 * h + t + 3)
                pr = p_slot(t).rearrange("p (i f c) -> p f i c", f=2, c=P)
                for f in range(2):
                    i = (t + 1 - f) // 2
                    if i < 4:
                        last = mm(ps_o[64 * f:64 * f + 64, i * P:HALF], v1s[:, t, :], pr[:, f, i:4], t == 0, t == 6 + f)
                last.then_inc(sem("os_mm"), 1)

            def sums_s(h, odd):
                pe.wait_ge(sem("s_add"), 8 * h + 8 + 4)
                for f in range(2):
                    last = mm(ps_t[64 * f:64 * f + 64, :], ones[:, 0:64],
                              accs[:, odd, :].rearrange("p (i f c) -> p f i c", f=2, c=P)[:, f], True, True)
                last.then_inc(sem("s_sums"), 1)

            def head_s(h, odd, first=False, maxima=True, more=True):
                for t in range(NT):
                    if t + 1 < NT:
                        scores_s(h, t + 1)
                    elif more:
                        pe.wait_ge(sem("s_shifted"), h + 2)
                        scores_s(h + 1, 0)
                    if maxima:
                        for n in STEPS_S[t]:
                            max_chunk_s(h + 2, n)
                    if t == 0:
                        pe.wait_ge(sem("s_evac"), h + 1)
                    pv_s(h, t)
                    if t == 0 and more:
                        pe.wait_ge(sem("s_shifted"), h + 1)
                        if not first:
                            pe.wait_ge(sem("s_recip"), 2 * h)
                        shift1("s", h + 1)
                    if t == 2 and not first:
                        pe.wait_ge(sem("s_shifted"), h + 2 if more else h + 1)
                        pe.wait_ge(sem("s_recip"), 2 * h)
                        sums_s(h - 1, 1 - odd)

            pe.wait_ge(sem("k2s_const"), 2)
            pe.wait_ge(sem("q2_zero"), 1)
            for i in range(4):
                query1("qs", i, "qs_split")
            for n in range(24):
                query1("qs", 4 + n, "qs_split")
                if n % 12 == 0:
                    pe.wait_ge(sem("qs_split"), 2 + n // 6)
                max_chunk_s(n // 12, n % 12)
                if n == 14:
                    shift1("s", 0)
            for i in range(28, 2 * H):
                query1("qs", i, "qs_split")
            pe.wait_ge(sem("qs_split"), 2 * H)
            pe.wait_ge(sem("s_shifted"), 1)
            scores_s(0, 0)
            head_s(0, 0, first=True)
            with pe.Fori(0, (H - 4) // 2) as n:
                head_s(2 * n + 1, 1)
                head_s(2 * n + 2, 0)
            head_s(H - 3, 1)
            head_s(H - 2, 0, maxima=False)
            head_s(H - 1, 1, maxima=False, more=False)
            pe.wait_ge(sem("s_recip"), 2 * H)
            sums_s(H - 1, 1)

            def project1(name, done):
                pe.wait_ge(sem(done), 16 + 1)
                for i in range(4):
                    for h in range(H):
                        last = mm(banks[i // 2][:, (i % 2) * 2 * P:(i % 2 + 1) * 2 * P], o1[:, h, i * P:(i + 1) * P],
                                  wproj[:, h, :], h == 0, h == H - 1)
                last.then_inc(sem(name), 1)

            project1("sp_mm", "s_o")

            ln_transposes("ln_ca", hn, NT)
            pe.wait_ge(sem("ln_ca_t"), 2)
            pe.wait_ge(sem("w2_in"), 16 * 2)
            def max_chunk1(h, r, c):
                m = 104 * h + 13 * r + c
                pe.wait_ge(sem("m1_red"), m + 2 if c in (1, NCH - 1) else m + 1)
                mm(mslot3(c)[:, 0:CW[c]], q1[:, ds(h * T + r * P, P)], k1[:, c * HALF:c * HALF + CW[c]]).then_inc(sem("m1_mm"), 1)

            def scores1(h, kt):
                i = 51 * h + kt
                pe.wait_ge(sem("p1_exp"), i + 1)
                for n, (k, q) in enumerate(((k1, q1), (k2, q2))):
                    for hf in range(2):
                        last = mm(ps_flat[:, ds(((h + kt) % 2) * (2 * HALF) + hf * HALF, HALF)], k[:, ds(kt * P, P)],
                                  q[:, ds(h * T + hf * HALF, HALF)], n == 0, n == 1)
                last.then_inc(sem("s1_mm"), 1)

            def pv1(h, kt, slot, start, stop):
                i = 51 * h + kt
                pe.wait_ge(sem("v1_staged"), i + 1)
                pe.wait_ge(sem("p1_exp"), i + 3)
                for hf in range(2):
                    last = mm(ps_o[64 * hf:64 * hf + 64, :], v_stage[:, slot, :],
                              probs[:, slot, hf * HALF:(hf + 1) * HALF], start, stop)
                last.then_inc(sem("o1_mm"), 1)

            def sums_c(h):
                pe.wait_ge(sem("c_add_v"), 18 * h + 18 + 2)
                pe.wait_ge(sem("c_add_g"), 33 * h + 33 + 2)
                for i, acc in enumerate((acc_v, acc_g)):
                    for hf in range(2):
                        last = mm(ps_t[64 * hf:64 * hf + 64, :], ones[:, 0:64], acc[:, hf * HALF:(hf + 1) * HALF], i == 0, i == 1)
                last.then_inc(sem("c_sums"), 1)

            def head_c(h, first=False, more=True):
                for u in range(3):
                    scores1(h, u + 1)
                    if u == 0:
                        if not first:
                            sums_c(h - 1)
                        pe.wait_ge(sem("c_evac"), h + 1)
                    if u == 2 and more and not first:
                        pe.wait_ge(sem("c_recip"), 2 * h)
                    pv1(h, u, u, u == 0, False)

                def group(r, last):
                    for u in range(6):
                        kt = 3 + 6 * r + u
                        ch = list((CHUNKS1_LAST if last else CHUNKS1)[u]) if more else []
                        for c in ch[0:1]:
                            max_chunk1(h + 1, r, c)
                        if not (last and u == 5):
                            scores1(h, kt + 1)
                        for c in ch[1:]:
                            max_chunk1(h + 1, r, c)
                        pv1(h, kt, u % 3, False, last and u == 5)
                        if last and more and u == 4:
                            shift1("c", h + 1)

                with pe.Fori(0, 7) as r:
                    group(r, False)
                group(7, True)
                if more:
                    pe.wait_ge(sem("c_shifted"), h + 2)
                    scores1(h + 1, 0)

            made = 0
            for n in range(NT * NCH):
                while made < 2 * H and made < 2 + n * 2 * H // (NT * NCH - 8):
                    query1("qc", made, "qc_read")
                    made += 1
                if n == 0:
                    pe.wait_ge(sem("qc_split"), 2)
                max_chunk1(0, n // NCH, n % NCH)
            assert made == 2 * H
            shift1("c", 0)
            pe.wait_ge(sem("qc_split"), 2 * H)
            pe.wait_ge(sem("c_shifted"), 1)
            scores1(0, 0)
            head_c(0, first=True)
            with pe.Fori(1, H - 1) as h:
                head_c(h)
            head_c(H - 1, more=False)
            pe.wait_ge(sem("c_recip"), 2 * (H - 1))
            sums_c(H - 1)
            project1("cp_mm", "c_o")

            pe.wait_ge(sem("qw_deq"), 1)
            for i in range(9):
                last = pe.transpose(ps_m[:, i * P:(i + 1) * P] if i < 8 else ps_t[:, 0:P], qwq[:, i // 3, i % 3, :], ident[:, :])
            last.then_inc(sem("qw_mm"), 1)
            ln_transposes("ln_f1", xn, NT)
            pe.wait_ge(sem("qx"), 1)
            pe.wait_ge(sem("qw_t"), 1)
            for w in range(2):
                for i in range(6):
                    n = 6 * w + i
                    if n >= 4:
                        pe.wait_ge(sem("ug_evac"), n - 3)
                    mm(banks[n % 4], qwt[:, w, i // 2, :], xt[:, (i % 2) * HALF:(i % 2 + 1) * HALF]).then_inc(sem("ug_mm"), 1)
            pe.wait_ge(sem("ug_evac"), 12)
            pe.wait_ge(sem("o_q"), 1)
            for t in range(NT):
                for c in range(3):
                    last = mm(banks[t // 4][:, (t % 4) * P:(t % 4 + 1) * P], gate[:, c, t * P:(t + 1) * P], qwt[:, 2, c, :],
                              c == 0, c == 2)
                last.then_inc(sem("down_mm"), 1)

        @block.vector
        def _(dve):
            link = Chain(dve, sem("dve_link"))
            dve.sem_inc(sem("m0_red"), 3)
            dve.sem_inc(sem("m1_red"), 3)
            dve.sem_inc(sem("m0_unit"), 1)
            dve.sem_inc(sem("m1_unit"), 1)
            dve.sem_inc(sem("sm_red"), 2)
            dve.sem_inc(sem("s_recip"), 2)
            dve.sem_inc(sem("c_add_v"), 2)
            dve.sem_inc(sem("c_o"), 1)

            def flat(t3):
                return t3.rearrange("p a b -> p (a b)")

            def layernorm(name, src, dst, nt):
                for t in range(nt):
                    last = dve.bn_stats(stats[:, t, :], src[:, t, :])
                link(last)
                for t in range(nt):
                    last = dve.bn_aggr(mv[:, t, :], stats[:, t, :])
                link(last)
                dve.tensor_scalar(sdev[:, 0:nt], mv[:, 0:nt, 1], EPS, None, ALU.add).then_inc(sem(name + "_var"), 1)
                dve.wait_ge(sem(name + "_sd"), 1)
                link(dve.reciprocal(rstd[:, 0:nt], sdev[:, 0:nt]))
                for t in range(nt):
                    last = dve.tensor_scalar(dst[:, t, :], src[:, t, :], mv[:, t, 0:1], rstd[:, t:t + 1], ALU.subtract, ALU.mult)
                last.then_inc(sem(name + "_xn"), 1)

            dve.wait_ge(sem("x_in"), 16)
            dve.wait_ge(sem("const_in"), 16 * 5)
            layernorm("ln_a0", x, xn, NT)
            dve.wait_ge(sem("masks_in"), 16)
            dve.tensor_copy(identb[:, :], ident[:, :])
            dve.tensor_copy(mask_kq[:, :], probs[:, 0, 0:P])
            link(dve.tensor_copy(mask_qk[:, :], probs[:, 0, P:2 * P]))
            dve.sem_inc(sem("masks"), 1)

            dve.wait_ge(sem("zeros"), 2)
            link(dve.tensor_scalar(qb0s[:, :], cols[:, 4:4 + H], col(C_QS), None, ALU.mult))
            dve.sem_inc(sem("qb0s"), 1)
            for n in range(len(FIRST0)):
                dve.wait_ge(sem("item_hi"), n + 1)
                subtract_hi(dve, n, n).then_inc(sem("item_split"), 1)
            dve.wait_ge(sem("item_split"), len(FIRST0))
            dve.tensor_scalar(k0[:, CTX:CTXP], zeros16[:, 0:CTXP - CTX], col(C_PAD0), None, ALU.add)\
                .then_inc(sem("k0_pad"), 1)

            rows4 = shift_rows[:, :].rearrange("p (t j r) -> p j t r", t=4, j=4)
            rows8 = shift_rows[:, 0:8 * 32].rearrange("p (t r) -> p t r", r=32)

            def negated_parts(link_sem, base, ready, part, mxv, rest):
                ch = Chain(dve, sem(link_sem), base, 4)
                ch(dve.tensor_scalar(part(0), mxv, -1.0, None, ALU.mult))
                ch(dve.scalar_tensor_tensor(out=rest(0), in0=mxv, scalar=-1.0, in1=part(0), op0=ALU.mult, op1=ALU.subtract))
                ch(dve.tensor_copy(part(1), rest(0)))
                ch(dve.tensor_tensor(rest(1), rest(0), part(1), ALU.subtract))
                dve.tensor_copy(part(2), rest(1)).then_inc(sem(ready), 1)
                ch.check()

            def unit0(b, n):
                dve.wait_ge(sem("m0_unit"), 16 * b + n + 1)
                for c in range(NCH):
                    dve.wait_ge(sem("m0_mm"), 208 * b + 13 * n + c + 1)
                    dve.tensor_reduce(mpart[:, c:c + 1], mslot3(c)[:, 0:CW[c]], AX.X, ALU.max).then_inc(sem("m0_red"), 1)
                dve.wait_ge(sem("m0_red"), 208 * b + 13 * n + NCH + 3)
                dve.tensor_reduce(mx[:, ds(n, 1)], mpart[:, 0:NCH], AX.X, ALU.max).then_inc(sem("m0_unit"), 1)

            def shift_block0(b):
                dve.wait_ge(sem("m0_unit"), 16 * b + 16 + 1)
                negated_parts("m0_link", 4 * b, "m0_parts",
                              lambda k: rows4[:, :, :, ROW_SHIFT0 + k],
                              mx[:, :].rearrange("p (j t) -> p j t", j=4),
                              lambda k: mrest[:, k, :].rearrange("p (j t) -> p j t", j=4))
                dve.wait_ge(sem("m0_turned"), b + 1)
                for j in range(4):
                    q = q0[32 * j:32 * j + 32, ds((b // 2) * (4 * T) + (b % 2) * HALF + j * T, HALF)]
                    dve.tensor_tensor(q, ps_t[32 * j:32 * j + 32, :], q, ALU.add).then_inc(sem("q0_shifted"), 1)

            with dve.Fori(0, 8) as b:
                with dve.Fori(0, 16) as n:
                    unit0(b, n)
                shift_block0(b)

            for i in range(8):
                dve.wait_ge(sem("sum0_mm"), i + 1)
                link(dve.reciprocal(y_tmp[i % 2], banks[i % 4]))
                o = o0[:, i // 2, (i % 2) * HALF:(i % 2 + 1) * HALF]
                dve.tensor_tensor(o, o, y_tmp[i % 2], ALU.mult).then_inc(sem("o0_norm"), 1)
            dve.wait_ge(sem("proj0_mm"), 1)
            link(dve.tensor_tensor(flat(x[:, :, :]), ps_s[:, 0, :], flat(x[:, :, :]), ALU.add))
            dve.sem_inc(sem("x1"), 1)
            layernorm("ln_f0", x, xn, NT)

            dve.wait_ge(sem("moe_mm"), 1)
            lg = y_tmp[0][:, 0:64].rearrange("p (t e) -> p t e", e=E)
            ex = y_tmp[0][:, 64:128].rearrange("p (t e) -> p t e", e=E)
            rank = y_tmp[0][:, 128:192].rearrange("p (t e) -> p t e", e=E)
            m1 = y_tmp[0][:, 192:200]
            ssum = y_tmp[0][:, 200:208]
            ahead = y_tmp[1].rearrange("p (t e f) -> p t e f", e=E, f=E)
            link(dve.tensor_copy(flat(lg), ps_t[:, 0:NT * E]))
            link(dve.memset(y_tmp[1], 0.0))
            link(dve.tensor_reduce(m1, lg, AX.X, ALU.max))
            for f in range(E):
                one = lg[:, :, f:f + 1]
                if f + 1 < E:
                    last = dve.tensor_tensor(ahead[:, :, f + 1:E, f], one.broadcast_to([P, NT, E - f - 1]), lg[:, :, f + 1:E], ALU.is_ge)
                if f:
                    last = dve.tensor_tensor(ahead[:, :, 0:f, f], one.broadcast_to([P, NT, f]), lg[:, :, 0:f], ALU.is_gt)
            link(last)
            link(dve.tensor_reduce(rank, ahead, AX.X, ALU.add))
            link(dve.tensor_scalar(rank, rank, 1.5, None, ALU.is_lt))
            dve.tensor_tensor(ex, lg, m1.unsqueeze(2).broadcast_to([P, NT, E]), ALU.subtract).then_inc(sem("moe_d"), 1)
            dve.wait_ge(sem("moe_exp"), 1)
            link(dve.tensor_tensor(ex, ex, rank, ALU.mult))
            link(dve.tensor_reduce(ssum, ex, AX.X, ALU.add))
            link(dve.reciprocal(ssum, ssum))
            link(dve.tensor_tensor(ex, ex, ssum.unsqueeze(2).broadcast_to([P, NT, E]), ALU.mult))
            dve.tensor_tensor(flat(xn[:, :, :]).rearrange("p (a r) -> p a r", r=R), ps_s[:, 0, :].rearrange("p (a r) -> p a r", r=R),
                              flat(ex).unsqueeze(2).broadcast_to([P, NT * E, R]), ALU.mult).then_inc(sem("moe_hw"), 1)
            dve.wait_ge(sem("moe_out"), NT)
            link(dve.tensor_tensor(flat(x[:, :, :]), ps_s[:, 0, :], flat(x[:, :, :]), ALU.add))
            dve.sem_inc(sem("x2"), 1)

            dve.wait_ge(sem("ctx1_in"), 32)
            layernorm("ln_cx", c_nat, c_nat, KT)
            for i in range(PCH):
                dve.wait_ge(sem("k1_hi"), i + 1)
                s = slice(i * HALF, i * HALF + PW[i])
                dve.tensor_tensor(k2[0:64, s], banks[i % 4][0:64, 0:PW[i]], k1[0:64, s], ALU.subtract).then_inc(sem("k1_split"), 1)

            dve.wait_ge(sem("ln_cx_xn"), 1)
            layernorm("ln_a1", x, xn, NT)
            dve.wait_ge(sem("ln_a1_xn"), 1)
            layernorm("ln_pb", xn, hn, NT)

            dve.wait_ge(sem("ln_pb_t"), 2)
            for i in range(8):
                r, hf = i // 2, i % 2
                e = y_tmp[i % 2]
                g = gated[:, r, hf * HALF:(hf + 1) * HALF]
                dve.wait_ge(sem("ff_silu"), i + 1)
                dve.tensor_tensor(g, banks[2 * (i % 2)], e, ALU.mult).then_inc(sem("ff_done"), 1)
            dve.wait_ge(sem("ffo_mm"), 1)
            dve.tensor_tensor(flat(xn[:, :, :]), ps_s[:, 0, :], flat(xn[:, :, :]), ALU.add).then_inc(sem("y_ff"), 1)
            for i in range(2):
                dve.wait_ge(sem("k1s_hi"), i + 1)
                s = slice(i * HALF, (i + 1) * HALF)
                dve.tensor_tensor(k2s[0:64, s], banks[i][0:64, :], k1s[0:64, s], ALU.subtract).then_inc(sem("k1s_split"), 1)

            def split_query(i):
                dve.wait_ge(sem("qs_hi"), i + 1)
                lo = q1[64:128, i * HALF:(i + 1) * HALF]
                dve.scalar_tensor_tensor(out=lo, in0=banks[i % 4][64:128, :], scalar=HD1 ** -0.5, in1=lo,
                                         op0=ALU.mult, op1=ALU.subtract).then_inc(sem("qs_split"), 1)

            def reduce_s(h, n):
                t, c0, w = CHUNKS_S[n]
                dve.wait_ge(sem("sm_mm"), 12 * h + n + 1)
                at = t if c0 == 0 else 4 + t
                dve.tensor_reduce(mx[:, at:at + 1], mslot(n)[:, 0:w], AX.X, ALU.max).then_inc(sem("sm_red"), 1)

            def parts_s(h):
                dve.wait_ge(sem("sm_red"), 12 * h + 12 + 2)
                dve.tensor_tensor(mx[:, 4:8], mx[:, 4:8], mx[:, 8:12], ALU.max).then_inc(sem("s_unit"), 1)
                dve.wait_ge(sem("s_unit"), h + 1)
                negated_parts("s_link", 4 * h, "s_parts", lambda p: rows8[:, :, p], mx[:, 0:NT], lambda p: mrest[:, p, 0:NT])

            def recip_s(h, i):
                dve.wait_ge(sem("s_sums"), h + 1 + 2)
                dve.wait_ge(sem("s_o"), h + 1)
                s = slice(i * HALF // 2, (i + 1) * HALF // 2)
                dve.reciprocal(recip[:, s], ps_t[:, s]).then_inc(sem("s_recip"), 1)

            def head_s(h, first=False, maxima=True):
                for n in range(12):
                    if n in (6, 7) and not first:
                        recip_s(h - 1, n - 6)
                    if maxima:
                        reduce_s(h + 2, n)
                if maxima:
                    dve.wait_ge(sem("s_turned"), h + 2)
                    parts_s(h + 2)

            dve.wait_ge(sem("shift_zero"), 2)
            for i in range(4):
                split_query(i)
            for n in range(24):
                split_query(4 + n)
                reduce_s(n // 12, n % 12)
                if n == 11:
                    parts_s(0)
            dve.wait_ge(sem("s_turned"), 1)
            parts_s(1)
            for i in range(28, 2 * H):
                split_query(i)
            head_s(0, first=True)
            with dve.Fori(1, H - 2) as h:
                head_s(h)
            head_s(H - 2, maxima=False)
            head_s(H - 1, maxima=False)
            recip_s(H - 1, 0)
            recip_s(H - 1, 1)

            halves = xn[:, :, :].rearrange("p (i f) d -> p i f d", f=2)
            dve.wait_ge(sem("sp_mm"), 1)
            for i in range(4):
                last = dve.tensor_tensor(halves[:, i], ps_s[:, 0, i * 256:(i + 1) * 256].rearrange("p (f d) -> p f d", f=2),
                                         halves[:, i], ALU.add)
            link(last)

            layernorm("ln_ca", xn, hn, NT)
            def reduce1(h, r, c):
                if c == 0:
                    dve.wait_ge(sem("m1_unit"), 8 * h + r + 1)
                dve.wait_ge(sem("m1_mm"), 104 * h + 13 * r + c + 1)
                dve.tensor_reduce(mpart[:, c:c + 1], mslot3(c)[:, 0:CW[c]], AX.X, ALU.max).then_inc(sem("m1_red"), 1)

            def unit1(h, r):
                dve.wait_ge(sem("m1_red"), 104 * h + 13 * r + NCH + 3)
                dve.tensor_reduce(mx[:, ds(r, 1)], mpart[:, 0:NCH], AX.X, ALU.max).then_inc(sem("m1_unit"), 1)

            def parts_c(h):
                dve.wait_ge(sem("m1_unit"), 8 * h + 8 + 1)
                negated_parts("c_link", 4 * h, "c_parts", lambda p: rows8[:, :, p], mx[:, 0:NT], lambda p: mrest[:, p, 0:NT])

            def add_v(h, n, slot=0):
                dve.wait_ge(sem("p1_exp"), 51 * h + 3 * n + 3 if slot == 0 else 51 * h + 50 + 3)
                dve.wait_ge(sem("c_add_v"), 18 * h + n + 2)
                dve.tensor_tensor(acc_v, acc_v, probs[:, slot, :], ALU.add).then_inc(sem("c_add_v"), 1)

            def normalise_c(h):
                dve.wait_ge(sem("c_sums"), h + 2)
                dve.wait_ge(sem("c_o"), h + 1)
                for i in range(2):
                    s = slice(i * HALF // 2, (i + 1) * HALF // 2)
                    dve.reciprocal(recip[:, s], ps_t[:, s]).then_inc(sem("c_recip"), 1)
                dve.wait_ge(sem("c_recip"), 2 * h + 2)
                dve.wait_ge(sem("c_evac"), h + 1 + 1)
                o = o1[:, ds(h, 1), :].rearrange("p a b -> p (a b)")
                dve.tensor_tensor(o, o, recip[:, :], ALU.mult).then_inc(sem("c_o"), 1)

            def head_c(h, first=False, more=True):
                dve.wait_ge(sem("p1_exp"), 51 * h + 3)
                dve.wait_ge(sem("c_sums"), h + 1)
                dve.tensor_copy(acc_v, probs[:, 0, :]).then_inc(sem("c_add_v"), 1)
                if not first:
                    normalise_c(h - 1)

                def group(r, last):
                    for u in range(6):
                        if more:
                            for c in (CHUNKS1_LAST if last else CHUNKS1)[u]:
                                reduce1(h + 1, r, c)
                            if u == (3 if last else 5):
                                unit1(h + 1, r)
                        if last and more and u == 3:
                            dve.wait_ge(sem("c_turned"), h + 1)
                            parts_c(h + 1)
                        if u % 3 == 0:
                            add_v(h, 1 + 2 * r + u // 3)
                    if last:
                        add_v(h, 17, 2)

                with dve.Fori(0, 7) as r:
                    group(r, False)
                group(7, True)

            with dve.Fori(0, NT) as r:
                for c in range(NCH):
                    reduce1(0, r, c)
                unit1(0, r)
            parts_c(0)
            head_c(0, first=True)
            with dve.Fori(1, H - 1) as h:
                head_c(h)
            head_c(H - 1, more=False)
            normalise_c(H - 1)

            halves = x[:, :, :].rearrange("p (f i) d -> p i f d", f=2)
            dve.wait_ge(sem("cp_mm"), 1)
            for i in range(4):
                last = dve.tensor_tensor(halves[:, i], ps_s[:, 0, i * 256:(i + 1) * 256].rearrange("p (f d) -> p f d", f=2),
                                         halves[:, i], ALU.add)
            link(last)

            dve.wait_ge(sem("qw_in"), 16)
            wb = qw.rearrange("p a b d -> p (a b d)").rearrange("p (n k) -> p n k", k=BLK)
            wqb = qwq.rearrange("p a b d -> p (a b d)").rearrange("p (n k) -> p n k", k=BLK)
            NB = 9 * D // BLK
            wscale, winv = y_tmp[0][:, 0:NB], y_tmp[0][:, 64:64 + NB]
            link(dve.tensor_reduce(wscale, wb, AX.X, ALU.max, apply_absolute_value=True))
            link(dve.tensor_scalar(wscale, wscale, 1.0 / 7.0, 1e-12, ALU.mult, ALU.max))
            link(dve.reciprocal(winv, wscale))
            link(dve.tensor_tensor(wqb, wb, winv.unsqueeze(2).broadcast_to([P, NB, BLK]), ALU.mult))
            link(dve.tensor_scalar(wqb, wqb, ROUND, ROUND, ALU.add, ALU.subtract))
            link(dve.tensor_scalar(wqb, wqb, 7.0, -8.0, ALU.min, ALU.max))
            dve.tensor_tensor(wqb, wqb, wscale.unsqueeze(2).broadcast_to([P, NB, BLK]), ALU.mult).then_inc(sem("qw_deq"), 1)
            layernorm("ln_f1", x, xn, NT)

            amax = [y_tmp[0][:, 128 + i:129 + i] for i in range(5)]
            gmax = [y_tmp[0][:, 136 + i:137 + i] for i in range(5)]
            scale = [y_tmp[0][:, 144 + i:145 + i] for i in range(5)]
            inv = [y_tmp[0][:, 152 + i:153 + i] for i in range(5)]

            def quantise(n, z, done=None):
                dve.tensor_reduce(amax[n], z, AX.X, ALU.max, apply_absolute_value=True).then_inc(sem("q_amax"), 1)
                dve.wait_ge(sem("q_gmax"), n + 1)
                link(dve.tensor_scalar(scale[n], gmax[n], 1.0 / QMAX, 1e-12, ALU.mult, ALU.max))
                link(dve.reciprocal(inv[n], scale[n]))
                link(dve.tensor_scalar(z, z, inv[n], ROUND, ALU.mult, ALU.add))
                link(dve.tensor_scalar(z, z, ROUND, QMAX, ALU.subtract, ALU.min))
                last = dve.tensor_scalar(z, z, -QMAX - 1.0, scale[n], ALU.max, ALU.mult)
                if done:
                    last.then_inc(sem(done), 1)
                else:
                    link(last)

            upf, gatef, sigf, tmpf = (flat(v) for v in (up, gate, sig, tmp))
            dve.wait_ge(sem("ln_f1_t"), 2)
            quantise(0, xt[:, :], "qx")
            dve.wait_ge(sem("ug_evac"), 6)
            quantise(1, gatef, "gate_q")
            dve.wait_ge(sem("ug_evac"), 12)
            quantise(2, upf)
            dve.wait_ge(sem("sigmoid"), 1)
            link(dve.tensor_scalar(sigf, sigf, 65536.0, ROUND, ALU.mult, ALU.add))
            link(dve.tensor_scalar(sigf, sigf, ROUND, 0.0, ALU.subtract, ALU.max))
            link(dve.tensor_scalar(sigf, sigf, 65535.0, 1.0 / 65536.0, ALU.min, ALU.mult))
            link(dve.tensor_tensor(tmpf, gatef, sigf, ALU.mult))
            quantise(3, tmpf)
            link(dve.tensor_tensor(gatef, tmpf, upf, ALU.mult))
            quantise(4, gatef, "o_q")
            for t in range(NT):
                dve.wait_ge(sem("down_mm"), 4 * (t // 4) + 4)
                dve.tensor_tensor(x[:, t, :], banks[t // 4][:, (t % 4) * P:(t % 4 + 1) * P], x[:, t, :], ALU.add)\
                    .then_inc(sem("y_out"), 1)

        @block.scalar
        def _(act):
            act.sem_inc(sem("p0_exp"), 2)
            act.sem_inc(sem("ps_exp"), 2)
            act.sem_inc(sem("s_evac"), 1)
            act.sem_inc(sem("c_evac"), 1)
            act.sem_inc(sem("p1_exp"), 2)
            act.sem_inc(sem("o0_evac"), 1)

            def sqrt(name, nt):
                act.wait_ge(sem(name + "_var"), 1)
                act.activation(sdev[:, 0:nt], sdev[:, 0:nt], ACT.Sqrt).then_inc(sem(name + "_sd"), 1)

            def columns(name, dst, nt, gamma=None):
                for i in range(0, nt, 4):
                    n = min(4, nt - i) * P
                    act.wait_ge(sem(name + "_mm"), i // 4 + 1)
                    act.activation(dst[:, i * P:i * P + n], banks[i // 4 % 4][:, 0:n], ACT.Copy,
                                   scale=1.0 if gamma is None else gamma).then_inc(sem(name + "_t"), 1)

            act.wait_ge(sem("const_in"), 16 * 5)
            sqrt("ln_a0", NT)
            act.wait_ge(sem("masks"), 1)
            act.wait_ge(sem("qb0s"), 1)
            act.wait_ge(sem("v0_ones"), 1)
            columns("ln_a0", xt, NT)
            v0h = v0.rearrange("p t (h c) -> p t h c", c=9)
            j = 0
            for n, (kind, i, c) in enumerate(ITEMS0):
                act.wait_ge(sem("item_mm"), n + 1)
                bank = banks[n % 4]
                if kind == "v":
                    for t in range(4 * i, min(4 * i + 4, KT)):
                        last = act.activation(v0h[:, t, :, 0:HD0],
                                              bank[:, (t % 4) * P:(t % 4 + 1) * P].rearrange("p (h c) -> p h c", c=HD0), ACT.Copy)
                    last.then_inc(sem("item_read"), 1)
                    continue
                if j >= 2:
                    act.wait_ge(sem("item_split"), j - 1)
                w = PW[c] if kind == "k" else HALF
                y = y_tmp[j % 2][:, 0:w]
                if kind == "k":
                    act.activation(y, bank[:, 0:w], ACT.Identity, bias=kb0[i]).then_inc(sem("item_read"), 1)
                else:
                    act.activation(y, bank, ACT.Identity, bias=qb0s[:, i:i + 1], scale=col(C_QS)).then_inc(sem("item_read"), 1)
                act.wait_ge(sem("item_read"), n + 1)
                act.activation(hm_tmp[j % 2][:, 0:w], y, ACT.Copy, scale=col(C_KLO if kind == "k" else C_QLO))\
                    .then_inc(sem("item_hi"), 1)
                j += 1

            act.preload_act_table(ACT.Exp)
            act.wait_ge(sem("item_read"), len(ITEMS0))
            act.wait_ge(sem("item_split"), NSPLIT)

            def exp0(b, n, u):
                kt = 3 * n + u
                i = 51 * b + kt
                act.wait_ge(sem("o0_mm"), i + 1)
                act.activation(v_stage[:, u, 0:36], v0[:, ds(kt, 1), ds((b // 2) * 36, 36)].rearrange("p a b -> p (a b)"),
                               ACT.Copy).then_inc(sem("v0_staged"), 1)
                for hp in range(2):
                    act.wait_ge(sem("s0_mm"), 2 * i + hp + 1)
                    act.wait_ge(sem("o0_mm"), i + 2 + hp)
                    act.activation(probs[:, (2 * u + hp) % 3, :], ps_s[:, hp, :], ACT.Exp).then_inc(sem("p0_exp"), 1)

            def block0(b, more):
                exp0(b, 0, 1)
                exp0(b, 0, 2)
                with act.Fori(1, KT // 3) as n:
                    for u in range(3):
                        exp0(b, n, u)
                if more:
                    exp0(b + 1, 0, 0)
                act.wait_ge(sem("o0_mm"), 51 * b + 51 + 3)
                act.activation(o0[:, ds(b // 2, 1), ds((b % 2) * HALF, HALF)].rearrange("p a b -> p (a b)"), ps_o[:, :], ACT.Copy)\
                    .then_inc(sem("o0_evac"), 1)

            exp0(0, 0, 0)
            with act.Fori(0, 7) as b:
                block0(b, True)
            block0(7, False)

            sqrt("ln_f0", NT)
            columns("ln_f0", xt, NT)
            ex = y_tmp[0][:, 64:128]
            act.wait_ge(sem("moe_d"), 1)
            act.activation(ex, ex, ACT.Exp).then_inc(sem("moe_exp"), 1)
            act.wait_ge(sem("moe_tr"), 1)
            act.activation(xt[:, :], ps_s[:, 1, :], ACT.Copy).then_inc(sem("moe_ht"), 1)

            sqrt("ln_cx", KT)
            columns("ln_cx", c_t, KT, col(C_GC))
            act.wait_ge(sem("k2_const"), 3)
            for i in range(PCH):
                act.wait_ge(sem("k1_mm"), i + 1)
                act.activation(k1[:, i * HALF:i * HALF + PW[i]], banks[i % 4][:, 0:PW[i]], ACT.Copy).then_inc(sem("k1_hi"), 1)
            for i in range(7):
                act.wait_ge(sem("v1_mm"), i + 1)
                n = min(8, KT - 8 * i)
                act.activation(v1[:, 8 * i:8 * i + n, :].rearrange("p a b -> p (a b)"), banks[i % 4][:, 0:n * HD1], ACT.Copy)\
                    .then_inc(sem("v1_evac"), 1)
            sqrt("ln_a1", NT)
            sqrt("ln_pb", NT)
            columns("ln_pb", xt, NT, col(C_GP))

            for i in range(8):
                act.wait_ge(sem("ff_mm"), i + 1)
                if i >= 2:
                    act.wait_ge(sem("ff_done"), i - 1)
                act.activation(y_tmp[i % 2], banks[2 * (i % 2) + 1], ACT.Silu).then_inc(sem("ff_silu"), 1)
            for i in range(2):
                act.wait_ge(sem("k1s_mm"), i + 1)
                act.activation(k1s[:, i * HALF:(i + 1) * HALF], banks[i], ACT.Copy).then_inc(sem("k1s_hi"), 1)
            act.wait_ge(sem("v1s_mm"), 1)
            act.activation(v1s.rearrange("p a b -> p (a b)"), banks[2], ACT.Copy).then_inc(sem("v1s_evac"), 1)

            def exp_s(h, t):
                i = 8 * h + t
                act.wait_ge(sem("ss_mm"), i + 1)
                act.wait_ge(sem("os_mm"), i + 1)
                act.wait_ge(sem("s_add"), i + 1)
                act.activation(p_slot(t)[:, P * t:T], ps_s[:, t % 2, P * t:T], ACT.Exp).then_inc(sem("ps_exp"), 1)

            def shift_copies(k, h):
                act.wait_ge(sem(k + "_turned"), h + 1)
                act.activation(q2[64:96, ds(h * T, HALF)], ps_t[64:96, :], ACT.Copy)
                act.activation(q2[64:96, ds(h * T + HALF, HALF)], ps_t[96:128, :], ACT.Copy).then_inc(sem(k + "_shifted"), 1)

            def head_s(h, more=True):
                for t in range(1, NT):
                    exp_s(h, t)
                    if t == 1 and more:
                        shift_copies("s", h + 1)
                if more:
                    exp_s(h + 1, 0)
                act.wait_ge(sem("os_mm"), 8 * h + 8 + 4)
                act.activation(o1[:, ds(h, 1), :].rearrange("p a b -> p (a b)"), ps_o[:, :], ACT.Copy).then_inc(sem("s_evac"), 1)

            for i in range(2 * H):
                act.wait_ge(sem("qs_mm"), i + 1)
                s = slice(i * HALF, (i + 1) * HALF)
                act.activation(q2[0:64, s], banks[i % 4][0:64, :], ACT.Copy, scale=HD1 ** -0.5)
                act.activation(q1[:, s], banks[i % 4], ACT.Copy, scale=HD1 ** -0.5).then_inc(sem("qs_hi"), 1)
                if i == 19:
                    shift_copies("s", 0)
            act.preload_act_table(ACT.Exp)
            exp_s(0, 0)
            with act.Fori(0, H - 1) as h:
                head_s(h)
            head_s(H - 1, more=False)

            sqrt("ln_ca", NT)
            columns("ln_ca", xt, NT, col(C_GX))
            for i in range(2 * H):
                act.wait_ge(sem("qc_mm"), i + 1)
                s = slice(i * HALF, (i + 1) * HALF)
                if i >= 2:
                    act.wait_ge(sem("qc_split"), i - 1)
                act.activation(y_tmp[i % 2], banks[i % 4], ACT.Copy, scale=HD1 ** -0.5).then_inc(sem("qc_read"), 1)
                act.wait_ge(sem("qc_read"), i + 1)
                act.activation(q2[0:64, s], y_tmp[i % 2][0:64, :], ACT.Copy)
                act.activation(q1[:, s], y_tmp[i % 2], ACT.Copy).then_inc(sem("qc_hi"), 1)

            act.preload_act_table(ACT.Exp)

            def exp_c(h, n, u, first=False):
                i = 51 * h + 3 * n + u
                act.wait_ge(sem("o1_mm"), i + 1)
                act.activation(v_stage[:, u, :], v1[:, ds(3 * n + u, 1), :].rearrange("p a b -> p (a b)"), ACT.Copy)\
                    .then_inc(sem("v1_staged"), 1)
                act.wait_ge(sem("s1_mm"), i + 1)
                if u == 0 or first and u == 2:
                    act.wait_ge(sem("c_add_v"), 18 * h + n + 2)
                else:
                    act.wait_ge(sem("c_add_g"), 33 * h + (2 if first else 2 * n + u))
                act.activation(probs[:, u, :], ps_flat[:, ds(((h + n + u) % 2) * (2 * HALF), 2 * HALF)], ACT.Exp)\
                    .then_inc(sem("p1_exp"), 1)

            def head_c(h, more=True):
                for u in range(3):
                    exp_c(h, 0, u, first=True)
                with act.Fori(1, KT // 3) as n:
                    for u in range(3):
                        exp_c(h, n, u)
                if more:
                    shift_copies("c", h + 1)
                act.wait_ge(sem("o1_mm"), 51 * h + 51 + 3)
                act.activation(o1[:, ds(h, 1), :].rearrange("p a b -> p (a b)"), ps_o[:, :], ACT.Copy).then_inc(sem("c_evac"), 1)

            act.wait_ge(sem("qc_split"), 2 * H)
            shift_copies("c", 0)
            with act.Fori(0, H - 1) as h:
                head_c(h)
            head_c(H - 1, more=False)

            act.wait_ge(sem("qw_mm"), 1)
            act.activation(qwt.rearrange("p a b d -> p (a b d)")[:, 0:8 * P], ps_m[:, :], ACT.Copy)
            act.activation(qwt[:, 2, 2, :], ps_t[:, 0:P], ACT.Copy).then_inc(sem("qw_t"), 1)
            sqrt("ln_f1", NT)
            columns("ln_f1", xt, NT)
            for n in range(12):
                i = n % 6
                dst = (gate, up)[n // 6]
                act.wait_ge(sem("ug_mm"), n + 1)
                act.activation(dst[:, i // 2, (i % 2) * HALF:(i % 2 + 1) * HALF], banks[n % 4], ACT.Copy).then_inc(sem("ug_evac"), 1)
            act.wait_ge(sem("gate_q"), 1)
            act.activation(sig.rearrange("p a b -> p (a b)"), gate.rearrange("p a b -> p (a b)"), ACT.Sigmoid)\
                .then_inc(sem("sigmoid"), 1)

        @block.gpsimd
        def _(pool):
            pool.sem_inc(sem("c_add_g"), 2)
            pool.sem_inc(sem("s_add"), 4)
            pool.sem_inc(sem("s_o"), 1)
            pool.memset(zeros16[:, :], 0.0).then_inc(sem("zeros"), 1)
            pool.wait_ge(sem("zeros"), 1)
            pool.memset(shift_rows[:, :], 0.0).then_inc(sem("zeros"), 1)
            pool.wait_ge(sem("zeros"), 2)
            pool.memset(v0.rearrange("p a b -> p (a b)"), 1.0).then_inc(sem("v0_ones"), 1)
            pool.wait_ge(sem("v0_ones"), 1)

            pool.wait_ge(sem("const_in"), 16 * 5)
            j = len(FIRST0)
            for n in range(len(FIRST0), len(ITEMS0)):
                if ITEMS0[n][0] != "v":
                    pool.wait_ge(sem("item_hi"), j + 1)
                    subtract_hi(pool, n, j).then_inc(sem("item_split"), 1)
                    j += 1
                    pool.wait_ge(sem("item_split"), j)
            for g in range(1, G0):
                pool.tensor_scalar(k0[:, g * CTXP + CTX:(g + 1) * CTXP], zeros16[:, 0:CTXP - CTX], col(C_PAD0), None, ALU.add)\
                    .then_inc(sem("k0_pad_others"), 1)
                pool.wait_ge(sem("k0_pad_others"), g)

            pool.wait_ge(sem("item_mm"), len(ITEMS0))
            pool.memset(k2[64:128, :], 0.0).then_inc(sem("k2_const"), 1)
            pool.wait_ge(sem("k2_const"), 1)
            pool.tensor_scalar(k2[64:128, 0:CTX], k2[64:128, 0:CTX], col(C_ONE1, 64, 128), None, ALU.add)\
                .then_inc(sem("k2_const"), 1)
            pool.wait_ge(sem("k2_const"), 2)
            pool.tensor_scalar(k2[64:128, CTX:CTXP], k2[64:128, CTX:CTXP], col(C_PAD1, 64, 128), None, ALU.add)\
                .then_inc(sem("k2_const"), 1)
            pool.wait_ge(sem("k2_const"), 3)
            pool.wait_ge(sem("m0_turned"), 8)
            pool.memset(shift_rows[:, :], 0.0).then_inc(sem("shift_zero"), 1)
            pool.wait_ge(sem("shift_zero"), 1)
            pool.memset(shift_rows[:, 0:8 * 32].rearrange("p (t r) -> p t r", r=32)[:, :, 3], 1.0).then_inc(sem("shift_zero"), 1)
            pool.wait_ge(sem("shift_zero"), 2)
            pool.wait_ge(sem("o0_mm"), 51 * 8 + 3)
            pool.memset(q2[96:128, :], 0.0).then_inc(sem("q2_zero"), 1)
            pool.wait_ge(sem("q2_zero"), 1)
            pool.wait_ge(sem("k1_mm"), PCH)
            pool.wait_ge(sem("v1_mm"), 7)
            pool.memset(k2s[64:128, :], 0.0).then_inc(sem("k2s_const"), 1)
            pool.wait_ge(sem("k2s_const"), 1)
            pool.tensor_scalar(k2s[64:128, :], k2s[64:128, :], col(C_ONE1, 64, 128), None, ALU.add).then_inc(sem("k2s_const"), 1)
            pool.wait_ge(sem("k2s_const"), 2)

            pool.wait_ge(sem("ff_done"), 8)
            pool.memset(probs[:, 1, 0:P], 0.0).then_inc(sem("p1_zero"), 1)
            pool.wait_ge(sem("p1_zero"), 1)

            def normalise_s(h):
                pool.wait_ge(sem("s_recip"), 2 * h + 2 + 2)
                pool.wait_ge(sem("s_evac"), h + 1 + 1)
                o = o1[:, ds(h, 1), :].rearrange("p a b -> p (a b)")
                pool.tensor_tensor(o, o, recip[:, :], ALU.mult).then_inc(sem("s_o"), 1)
                pool.wait_ge(sem("s_o"), h + 1 + 1)

            def head_s(h, first=False):
                acc = accs[:, ds(h % 2, 1), :].rearrange("p a b -> p (a b)")
                pool.wait_ge(sem("ps_exp"), 8 * h + 1 + 3)
                pool.wait_ge(sem("s_sums"), h + 1)
                pool.tensor_tensor(acc, probs[:, 0, :], probs[:, 1, :], ALU.add).then_inc(sem("s_add"), 2)
                for t in range(2, NT):
                    pool.wait_ge(sem("ps_exp"), 8 * h + t + 3)
                    pool.wait_ge(sem("s_add"), 8 * h + t + 4)
                    part = accs[:, ds(h % 2, 1), P * t:T].rearrange("p a b -> p (a b)")
                    pool.tensor_tensor(part, part, p_slot(t)[:, P * t:T], ALU.add).then_inc(sem("s_add"), 1)
                    if t == 5 and not first:
                        pool.wait_ge(sem("s_add"), 8 * h + t + 1 + 4)
                        normalise_s(h - 1)

            head_s(0, first=True)
            with pool.Fori(1, H) as h:
                head_s(h)
            normalise_s(H - 1)

            for i in range(2 * H):
                pool.wait_ge(sem("qc_hi"), i + 1)
                lo = q1[64:128, i * HALF:(i + 1) * HALF]
                pool.tensor_tensor(lo, y_tmp[i % 2][64:128, :], lo, ALU.subtract).then_inc(sem("qc_split"), 1)
                pool.wait_ge(sem("qc_split"), i + 1)

            def add_g(h, n, u):
                pool.wait_ge(sem("p1_exp"), 51 * h + 3 * n + u + 3)
                pool.wait_ge(sem("c_add_g"), 33 * h + 2 * n + u - 1 + 2)
                pool.tensor_tensor(acc_g, acc_g, probs[:, u, :], ALU.add).then_inc(sem("c_add_g"), 1)

            with pool.Fori(0, H) as h:
                pool.wait_ge(sem("p1_exp"), 51 * h + 2 + 3)
                pool.wait_ge(sem("c_sums"), h + 1)
                pool.tensor_tensor(acc_g, probs[:, 1, :], probs[:, 2, :], ALU.add).then_inc(sem("c_add_g"), 2)
                with pool.Fori(1, KT // 3 - 1) as n:
                    add_g(h, n, 1)
                    add_g(h, n, 2)
                add_g(h, KT // 3 - 1, 1)

            for n in range(5):
                pool.wait_ge(sem("q_amax"), n + 1)
                pool.partition_all_reduce(y_tmp[0][:, 136 + n:137 + n], y_tmp[0][:, 128 + n:129 + n], P, RMAX)\
                    .then_inc(sem("q_gmax"), 1)


def laid_out(i):
    f = {k: np.ascontiguousarray(v) for k, v in i.items()}
    z = lambda *s: np.zeros(s, np.float32)
    o = {"x": f["x"].reshape(T, D)}
    ctx_rows = z(CTXP, D)
    ctx_rows[:CTX] = f["ctx_1024"][0]
    o["ctx"] = ctx_rows
    o["ctx_t"] = np.ascontiguousarray(ctx_rows.T)
    cols = z(P, 34)
    wk, wq, wo = z(P, G0, P), z(P, H, P), z(P, G0, P)
    wkt, wqt, wot = f["L0_xattn_Wk"].T, f["L0_xattn_Wq"].T, f["L0_xattn_Wo"].T
    for h in range(H):
        g, j = divmod(h, 4)
        s = slice(h * HD0, (h + 1) * HD0)
        for r in range(3):
            d = slice(32 * j + 8 * r, 32 * j + 8 * r + 8)
            wk[:, g, d] = wkt[:, s]
            wq[:, h, d] = wqt[:, s]
            cols[d, g] = f["L0_xattn_bk"][s]
            cols[d, 4 + h] = f["L0_xattn_bq"][s]
        cols[32 * j + ROW_SHIFT0:32 * j + ROW_SHIFT0 + 3, g] = 1
        cols[32 * j + ROW_PAD0, 4 + h] = 1
        wo[32 * j:32 * j + 8, g, :] = wot[s]
    r = np.arange(P) % 32
    cols[:, 20] = np.where(r < ROW_SHIFT0, np.float32(1 / np.sqrt(HD0)), 1)
    cols[:, 21] = (r >= 16) & (r < 24)
    cols[:, 22] = (r >= 8) & (r < 16)
    cols[:, 23] = np.where(r == ROW_PAD0, PAD_SCORE, 0)
    cols[ROW_SHIFT1:ROW_SHIFT1 + 3, 24] = 1
    cols[ROW_PAD1, 25] = PAD_SCORE
    cols[ROW_PAD1, 26] = 1
    cols[:, 27] = f["L1_xattn_ptb_gamma"]
    cols[:, 28] = f["L1_xattn_ca_ctx_gamma"]
    cols[:, 29] = f["L1_xattn_ca_gamma"]
    o["cols"] = cols
    o["wk0"], o["wq0"], o["wo0"] = wk, wq, wo
    o["wv0"] = np.ascontiguousarray(f["L0_xattn_Wv"].T)
    o["rows0"] = np.concatenate([f["L0_xattn_bv"], f["L0_xattn_bo"]])[None]
    o["wg0"] = f["L0_ffn_Wg"]
    o["moe_a"] = np.ascontiguousarray(f["L0_ffn_A"].transpose(1, 0, 2).reshape(D, E * R))
    o["moe_b"] = f["L0_ffn_B"].reshape(E * R, D)
    sel = z(P, P)
    for j in range(4):
        sel[32 * j + 8, 32 * j:32 * j + 32] = 1
    o["sel_sum"] = sel
    o["ident"] = np.eye(P, dtype=np.float32)
    o["ones"] = np.ones((P, P), np.float32)
    o["ident16"] = np.eye(P, dtype=np.float16)
    k, q = np.arange(P)[:, None], np.arange(P)[None]
    o["masks"] = np.concatenate([np.where(k > q, MASKED, 0), np.where(k < q, MASKED, 0)], 1).astype(np.float32)

    wf = f["L1_xattn_W_fused"]
    inner = H * HD1

    def twice(w):
        w = w.reshape(D, H, 1, HD1)
        return np.ascontiguousarray(np.broadcast_to(w, (D, H, 2, HD1)).reshape(D, H, P))

    def kkv(w):
        return np.concatenate([w[:, :HD1], w[:, :HD1], w[:, HD1:]], 1)

    def halves(w):
        m = z(P, H, 2 * D)
        for h in range(H):
            m[0:HD1, h, 0:D] = w[h * HD1:(h + 1) * HD1]
            m[HD1:P, h, D:] = w[h * HD1:(h + 1) * HD1]
        return m

    o["wq_s"] = twice(wf[:, :inner])
    o["wkv_s"] = kkv(wf[:, inner:inner + 2 * HD1])
    o["wff"] = np.ascontiguousarray(wf[:, inner + 2 * HD1:])
    o["wffo"] = np.ascontiguousarray(f["L1_xattn_W_ff_out"].reshape(FFI // P, P, D).transpose(1, 0, 2))
    o["wo_s"] = halves(f["L1_xattn_W_attn_out"])
    o["wq_c"] = twice(f["L1_xattn_W_q"])
    o["wkv_c"] = kkv(f["L1_xattn_W_kv"])
    o["wo_c"] = halves(f["L1_xattn_W_out"])
    rows = lambda w: w.reshape(3, P, D).transpose(1, 0, 2)
    o["qw"] = np.ascontiguousarray(np.stack([rows(f["L1_ffn_w_gate"]), rows(f["L1_ffn_w_up"]),
                                             f["L1_ffn_w_down"].reshape(D, 3, P)], 1))
    return {k: np.ascontiguousarray(v) for k, v in o.items()}


def kernel(**inputs):
    import concourse.bacc as bacc
    from concourse.bass_utils import run_bass_kernel_spmd

    arrays = laid_out(inputs)
    nc = bacc.Bacc("TRN2", target_bir_lowering=False, num_devices=1)
    args = {k: nc.dram_tensor("in_" + k, v.shape, mybir.dt.from_np(v.dtype), kind="ExternalInput").ap()
            for k, v in arrays.items()}
    out = nc.dram_tensor("out_x", (T, D), F32, kind="ExternalOutput").ap()
    build(nc, args, out)
    r = run_bass_kernel_spmd(nc, [{"in_" + k: v for k, v in arrays.items()}], core_ids=[0])
    return r.results[0]["out_x"].reshape(1, T, D)
```

```python
from contextlib import ExitStack

import numpy as np
import concourse.bass as bass
from concourse import mybir

F32 = mybir.dt.float32
F16 = mybir.dt.float16
BF16 = mybir.dt.bfloat16
ALU = mybir.AluOpType
ACT = mybir.ActivationFunctionType
AX = mybir.AxisListType
RMAX = bass.bass_isa.ReduceOp.max

P = 128
D = 128
T = 1024
NT = T // P
CTX = 6404
KT = -(-CTX // P)
CTXP = KT * P
HALF = 512
H = 16
HD0 = 8
HD1 = 64
G0 = H // 4
E, R = 8, 16
FFI = 512
QI = 384
BLK = 32
EPS = 1e-5
PAD_SCORE = -30000.0
MASKED = -1e30
ROUND = 1.5 * 2.0 ** 23
QMAX = 32767.0
NCH = -(-CTX // HALF)
CW = [min(HALF, CTX - c * HALF) for c in range(NCH)]
PCH = -(-CTXP // HALF)
PW = [min(HALF, CTXP - c * HALF) for c in range(PCH)]
ROW_SHIFT0, ROW_PAD0 = 24, 27
ROW_SHIFT1, ROW_PAD1 = 64, 67
CHUNKS0 = [range(0, 4), range(4, 9), range(9, 13)]
FIRST0 = [("k", 0, c) for c in range(PCH)] + [("q", h, f) for h in range(4) for f in range(2)]
_QS = [("q", h, f) for h in range(4, H) for f in range(2)]
OTHER0 = [item for c in range(PCH) for item in [("k", g, c) for g in range(1, G0)] + _QS[2 * c:2 * c + 2] + [("v", c, 0)]]
ITEMS0 = FIRST0 + OTHER0
NSPLIT = sum(kind != "v" for kind, _, _ in ITEMS0)
CHUNKS_S = [(t, c0, min(HALF, P * (t + 1) - c0)) for t in range(NT) for c0 in range(0, P * (t + 1), HALF)]
STEPS_S = [range(0, 2), range(2, 4), range(4, 6), range(6, 7), range(7, 8), range(8, 9), range(9, 11), range(11, 12)]
CHUNKS1 = [range(0, 3), range(3, 5), range(5, 7), range(7, 9), range(9, 11), range(11, 13)]
CHUNKS1_LAST = [range(0, 3), range(3, 7), range(7, 10), range(10, 13), (), ()]


class Chain:

    def __init__(self, eng, sem, base=0, per=None):
        self.eng, self.sem, self.base, self.n, self.per = eng, sem, base, 0, per

    def __call__(self, ins):
        self.n += 1
        ins.then_inc(self.sem, 1)
        self.eng.wait_ge(self.sem, self.base + self.n)

    def check(self):
        assert self.n == self.per, self.n


def build(nc, a, out):
    with ExitStack() as ctx:
        def sb(name, shape, dt=F32):
            return ctx.enter_context(nc.sbuf_tensor(name, shape, dt))

        def ps(name, shape):
            return ctx.enter_context(nc.psum_tensor(name, shape, F32))

        sems = {}

        def sem(name):
            if name not in sems:
                sems[name] = ctx.enter_context(nc.semaphore(name))
            return sems[name]

        arena_a = sb("arena_a", [P, G0 * CTXP // 2])
        arena_b = sb("arena_b", [P, H * T // 2])
        arena_c = sb("arena_c", [P, CTXP])
        arena_d = sb("arena_d", [P, 7680])
        arena_e = sb("arena_e", [P, H * HALF])
        probs = sb("probs", [P, 3, 2 * HALF])

        def view(arena, at, shape, dt=F32):
            n = int(np.prod(shape))
            words = n if dt == F32 else n // 2
            v = arena[:, at:at + words]
            if dt != F32:
                v = v.bitcast(dt)
            if len(shape) == 2:
                v = v.rearrange("p (a b) -> p a b", a=shape[0])
            if len(shape) == 3:
                v = v.rearrange("p (a b c) -> p a b c", a=shape[0], b=shape[1])
            return v

        k0 = view(arena_a, 0, [G0 * CTXP], F16)
        q0 = view(arena_b, 0, [H * T], F16)
        ctx_t = view(arena_c, 0, [CTXP])
        v0 = view(arena_d, 0, [KT, H * 9])
        o0 = view(arena_e, 0, [G0, T])
        wq0 = view(arena_e, 4096, [H, P])
        wk0 = view(arena_e, 6144, [G0, P])
        wv0 = view(arena_e, 6656, [P])
        wo0 = view(arena_e, 6784, [G0, P])
        wg0 = view(arena_e, 7296, [E])
        moe_a = view(arena_e, 7304, [P])
        moe_b = view(arena_e, 7432, [P])
        rows0 = view(arena_e, 7560, [2 * P])

        c_nat = view(arena_c, 0, [KT, D])
        c_stats = view(arena_e, 4096, [KT, 6])
        c_mv = view(arena_e, 4416, [KT, 2])
        c_sdev = view(arena_e, 4520, [KT])
        c_rstd = view(arena_e, 4580, [KT])
        c_t = view(arena_d, 0, [CTXP])
        k1 = view(arena_c, 0, [CTXP], F16)
        k2 = view(arena_c, CTXP // 2, [CTXP], F16)
        v1 = view(arena_a, H * T // 2, [KT, HD1])
        wkv_c = view(arena_e, 5000, [3 * HD1])

        q2 = view(arena_a, 0, [H * T], F16)
        q1 = view(arena_b, 0, [H * T], F16)
        o1 = view(arena_e, 0, [H // 2, T])
        wq1 = view(arena_e, 0, [H, P])
        wkv_s = view(arena_e, 2048, [3 * HD1])
        wff = view(arena_e, 2240, [2 * FFI])
        wffo = view(arena_e, 3264, [FFI // P, D])
        gated = view(arena_e, 3776, [FFI // P, T])
        k1s = view(arena_d, 0, [T], F16)
        k2s = view(arena_d, T // 2, [T], F16)
        v1s = view(arena_d, T, [NT, HD1])
        wproj = view(arena_d, 1536, [H // 2, D])
        o_raw = view(arena_d, 2560, [HALF])
        acc_v = view(arena_d, 5632, [2 * HALF])
        acc_g = view(arena_d, 6656, [2 * HALF])
        accs = view(arena_d, 5632, [2, 2 * HALF])
        probs_3 = view(arena_a, H * T // 2 + KT * HD1, [2 * HALF])

        qw = view(arena_d, 3072, [3, 3, D])
        qwt = view(arena_d, 4224, [3, 3, D])
        NB = 9 * D // BLK
        wscale = view(arena_d, 5376, [NB])
        winv = view(arena_d, 5376 + NB, [NB])
        up = view(arena_b, 0, [3, T])
        gate = view(arena_b, 3072, [3, T])
        sig = view(arena_c, 0, [3, T])
        tmp = view(arena_c, 3072, [3, T])

        x = sb("x", [P, NT, D])
        xn = sb("xn", [P, NT, D])
        xt = sb("xt", [P, T])
        ident = sb("ident", [P, P])
        ident16 = sb("ident16", [P, P], F16)
        identb = sb("identb", [P, P], BF16)
        mask_kq = sb("mask_kq", [P, P], BF16)
        mask_qk = sb("mask_qk", [P, P], BF16)
        zeros16 = sb("zeros16", [P, P], F16)
        sel_sum = sb("sel_sum", [P, P])
        ones = sb("ones", [P, P])
        cols = sb("cols", [P, 34])
        shift_rows = sb("shift_rows", [P, 4 * P], F16)
        v_stage = sb("v_stage", [P, 3, HD1])
        mpart = sb("mpart", [P, 16])
        mx = sb("mx", [P, 16])
        mrest = sb("mrest", [P, 2, 16])
        recip = sb("recip", [P, HALF])
        qb0s = sb("qb0s", [P, H])
        stats = probs[:, 2, 0:6 * KT].rearrange("p (t s) -> p t s", s=6)
        mv = probs[:, 2, 320:320 + 2 * KT].rearrange("p (t s) -> p t s", s=2)
        sdev = probs[:, 2, 430:430 + KT]
        rstd = probs[:, 2, 490:490 + KT]
        hm_tmp = [probs[:, 0, 512 + 256 * i:768 + 256 * i].bitcast(F16) for i in range(2)]
        k_tmp = [probs[0:64, 0, 512 * i:512 * i + 512] for i in range(2)]
        hn = probs[:, 0, :].rearrange("p (t d) -> p t d", t=NT)
        y_tmp = [probs[:, 1, 512 * i:512 * i + 512] for i in range(2)]

        kb0 = [cols[:, g:g + 1] for g in range(4)]
        qb0 = [cols[:, 4 + h:5 + h] for h in range(H)]
        C_QS, C_KLO, C_QLO, C_PAD0, C_GP, C_GC, C_GX = (20, 21, 22, 23, 27, 28, 29)

        def col(i, lo=0, hi=P):
            return cols[lo:hi, i:i + 1]

        ps_s = ps("ps_s", [P, 2, 2 * HALF])
        ps_o = ps("ps_o", [P, HALF])
        ps_m = ps("ps_m", [P, 2 * HALF])
        ps_t = ps("ps_t", [P, HALF])
        spare = [ps_m[:, 0:HALF], ps_m[:, HALF:], ps_o[:, :]]
        banks = [ps_s[:, i // 2, (i % 2) * HALF:(i % 2 + 1) * HALF] for i in range(4)]

        ps_flat = ps_s[:, :, :].rearrange("p a b -> p (a b)")

        def p_slot(t):
            return probs_3 if t % 4 == 3 else probs[:, t % 4, :]

        def mslot(c):
            return ps_m[:, (c % 2) * HALF:(c % 2 + 1) * HALF]

        def mslot3(c):
            return ps_t[:, :] if c % 3 == 2 else ps_m[:, 0:HALF] if c % 3 == 0 and c < NCH - 1 else ps_m[:, HALF:]

        ds = bass.ds

        def divide(eng, h, odd, done):
            for f in range(2):
                o = o1[64 * odd:64 * odd + 64, ds(h // 2, 1), f * HALF:(f + 1) * HALF].rearrange("p a b -> p (a b)")
                last = eng.tensor_tensor(o, o_raw[64 * f:64 * f + 64, :], recip[64 * f:64 * f + 64, :], ALU.mult)
                if f == 0 and eng is nc.gpsimd:
                    last.then_inc(sem("s_o_half"), 1)
                    eng.wait_ge(sem("s_o_half"), h + 1)
            last.then_inc(done, 1)

        def subtract_hi(eng, n, j):
            kind, i, c = ITEMS0[n]
            if kind == "k":
                at, w = i * CTXP + c * HALF, PW[c]
                dst = k0[:, at:at + w]
            else:
                at, w = i * T + c * HALF, HALF
                dst = q0[:, at:at + w]
            return eng.tensor_tensor(dst, y_tmp[j % 2][:, 0:w], hm_tmp[j % 2][:, 0:w], ALU.subtract)

        block = ctx.enter_context(nc.Block())

        @block.sync
        def _(sp):
            def load(dst, src, name, after=()):
                for s, v in after:
                    sp.wait_ge(sem(s), v)
                sp.dma_start(dst, src).then_inc(sem(name), 16)

            load(x[:, :, :], a["x"].rearrange("(t p) d -> p t d", p=P), "x_in")
            load(cols[:, :], a["cols"], "const_in")
            load(ident[:, :], a["ident"], "const_in")
            load(ones[:, :], a["ones"], "const_in")
            load(ident16[:, :], a["ident16"], "const_in")
            load(probs[:, 0, 0:2 * P], a["masks"], "masks_in")
            load(sel_sum[:, :], a["sel_sum"], "const_in")
            load(wk0, a["wk0"], "w0_in")
            load(wv0, a["wv0"], "w0_in")
            load(wq0, a["wq0"], "w0_in")
            load(wo0, a["wo0"], "w0_in")
            load(wg0, a["wg0"], "w0_in")
            load(moe_a, a["moe_a"], "w0_in")
            load(moe_b, a["moe_b"], "w0_in")
            load(rows0[0:1], a["rows0"], "w0_in")
            for i in range(4):
                lo, hi = i * CTXP // 4, (i + 1) * CTXP // 4
                load(ctx_t[:, lo:hi], a["ctx_t"][:, lo:hi], "ctx_in")
            load(c_nat, a["ctx"].rearrange("(t p) d -> p t d", p=P), "ctx1_in", [("item_mm", len(ITEMS0))])
            load(wkv_c, a["wkv_c"], "ctx1_in")
            load(k2[64:128, :], a["k2_rows"], "k2_in", [("ln_cx_mm", PCH)])
            load(wq1, a["wq_s"], "w1_in", [("proj0_mm", 1)])
            load(wkv_s, a["wkv_s"], "w1_in")
            load(wff, a["wff"], "w1_in")
            load(wffo, a["wffo"], "w1_in")
            load(k2s[64:128, :], a["k2_rows"][:, 0:T], "k2s_in", [("k1_mm", PCH), ("v1_mm", 7)])
            load(wproj, a["wo_s"], "w1_in")
            load(qw, a["qw"], "qw_in")
            load(wq1, a["wq_c"], "w2_in", [("sp_mm", 1)])
            load(wproj, a["wo_c"], "w2_in")
            for t in range(NT):
                sp.wait_ge(sem("y_out"), t + 1)
                sp.dma_start(out[t * P:(t + 1) * P, :], x[:, t, :]).then_inc(sem("stored"), 16)
            sp.wait_ge(sem("stored"), 16 * NT)

        @block.tensor
        def _(pe):
            def mm(o, l, r, start=True, stop=True):
                return pe.matmul(o, l, r, start=start, stop=stop, skip_group_check=True)

            def ln_transposes(name, src, nt):
                for i in range(0, nt, 4):
                    pe.wait_ge(sem(name + "_xn"), i // 4 + 1)
                    for t in range(i, min(i + 4, nt)):
                        last = pe.transpose(banks[i // 4 % 4][:, (t % 4) * P:(t % 4 + 1) * P], src[:, t, :], ident[:, :])
                    last.then_inc(sem(name + "_mm"), 1)

            pe.sem_inc(sem("o0_mm"), 3)
            pe.sem_inc(sem("os_mm"), 4)
            pe.sem_inc(sem("o1_mm"), 3)
            pe.sem_inc(sem("s_sums"), 2)
            pe.sem_inc(sem("c_sums"), 1)
            pe.wait_ge(sem("const_in"), 16 * 5)
            pe.wait_ge(sem("zeros"), 2)
            pe.wait_ge(sem("w0_in"), 16 * 8)
            ln_transposes("ln_a0", xn, NT)
            pe.wait_ge(sem("ctx_in"), 16 * 4)
            pe.wait_ge(sem("ln_a0_t"), 2)

            def operand0(n):
                kind, i, j = ITEMS0[n]
                if n >= 4:
                    pe.wait_ge(sem("item_read"), n - 3)
                bank = banks[n % 4]
                if kind == "k":
                    last = mm(bank[:, 0:PW[j]], wk0[:, i, :], ctx_t[:, j * HALF:j * HALF + PW[j]])
                elif kind == "q":
                    last = mm(bank, wq0[:, i, :], xt[:, j * HALF:(j + 1) * HALF])
                else:
                    for t in range(4 * i, min(4 * i + 4, KT)):
                        o = bank[:, (t % 4) * P:(t % 4 + 1) * P]
                        mm(o, ctx_t[:, t * P:(t + 1) * P], wv0, stop=False)
                        last = mm(o, ones[0:1, :], rows0[0:1, 0:P], start=False)
                last.then_inc(sem("item_mm"), 1)

            for n in range(len(FIRST0)):
                operand0(n)

            def q0_at(b):
                return (b // 2) * (4 * T) + (b % 2) * HALF

            def max_chunk0(b, n, c):
                m = 208 * b + 13 * n + c
                pe.wait_ge(sem("m0_red"), m + 2 if c in (1, NCH - 1) else m + 1)
                mm(mslot3(c)[:, 0:CW[c]], q0[:, ds(q0_at(b) + (n // 4) * T + (n % 4) * P, P)],
                   k0[:, ds((b // 2) * CTXP + c * HALF, CW[c])]).then_inc(sem("m0_mm"), 1)

            def shift0(b):
                pe.wait_ge(sem("m0_parts"), b + 1)
                for t in range(4):
                    last = mm(ps_t[:, t * P:(t + 1) * P], shift_rows[:, t * P:(t + 1) * P], ident16[:, :])
                last.then_inc(sem("m0_turned"), 1)

            def scores0(b, kt, hp):
                i = 102 * b + 2 * kt + hp
                pe.wait_ge(sem("p0_exp"), i + 1)
                for j in range(2):
                    last = mm(ps_s[:, hp, j * HALF:(j + 1) * HALF], k0[:, ds((b // 2) * CTXP + kt * P, P)],
                              q0[:, ds(q0_at(b) + (2 * hp + j) * T, HALF)])
                last.then_inc(sem("s0_mm"), 1)

            def pv0(b, kt, u, stop):
                pe.wait_ge(sem("v0_staged"), 51 * b + kt + 1)
                pe.wait_ge(sem("p0_exp"), 102 * b + 2 * kt + 4)
                for j in range(4):
                    last = mm(ps_o[32 * j:32 * j + 9, :], v_stage[:, u, 9 * j:9 * j + 9],
                              probs[:, (2 * u + j // 2) % 3, (j % 2) * HALF:(j % 2 + 1) * HALF], False, stop)
                last.then_inc(sem("o0_mm"), 1)

            def first_scores0(b, hp):
                pe.wait_ge(sem("q0_shifted"), 4 * b + 2 * hp + 2)
                scores0(b, 0, hp)

            def block0(b, more):
                def group(n, first, last):
                    for u in range(3):
                        kt = 3 * n + u
                        ch = list(CHUNKS0[u]) if more and not last else []
                        for hp in range(2):
                            if not (last and u == 2):
                                scores0(b, kt + 1, hp)
                            elif more:
                                first_scores0(b + 1, hp)
                            for c in ch[0:2] if hp == 0 else ch[2:-1]:
                                max_chunk0(b + 1, n, c)
                        if first and u == 0:
                            pe.wait_ge(sem("o0_evac"), b + 1)
                            mm(ps_o[:, :], zeros16[:, :], q0[:, 0:HALF], True, False)
                        pv0(b, kt, u, last and u == 2)
                        for c in ch[-1:]:
                            max_chunk0(b + 1, n, c)
                        if last and more and u == 0:
                            shift0(b + 1)

                group(0, True, False)
                if more:
                    with pe.Fori(1, 16) as n:
                        group(n, False, False)
                else:
                    with pe.Fori(1, 8) as n:
                        group(n, False, False)
                        sums0(n - 1, ps_m[:, ds(((n - 1) % 2) * HALF, HALF)])
                    with pe.Fori(8, 16) as n:
                        group(n, False, False)
                group(16, False, True)

            def sums0(b, bank):
                pe.wait_ge(sem("o0_norm"), b + 1)
                mm(bank, sel_sum[:, :], o0[:, ds(b // 2, 1), ds((b % 2) * HALF, HALF)].rearrange("p a b -> p (a b)"))\
                    .then_inc(sem("sum0_mm"), 1)

            pe.wait_ge(sem("k0_pad"), 1)
            pe.wait_ge(sem("item_split"), len(FIRST0))
            made, chunks = len(FIRST0), 0
            for n in range(16):
                for c in range(NCH):
                    max_chunk0(0, n, c)
                    chunks += 1
                    if made < len(ITEMS0) and (made - len(FIRST0)) * 16 * NCH < chunks * len(OTHER0):
                        operand0(made)
                        made += 1
            assert made == len(ITEMS0)
            shift0(0)
            pe.wait_ge(sem("item_split"), NSPLIT)
            pe.wait_ge(sem("item_read"), len(ITEMS0))
            pe.wait_ge(sem("k0_pad_others"), G0 - 1)
            first_scores0(0, 0)
            first_scores0(0, 1)
            with pe.Fori(0, 7) as b:
                block0(b, True)
            block0(7, False)

            pe.wait_ge(sem("o0_evac"), 9)
            mm(ps_t[:, :], sel_sum[:, :], o0[:, G0 - 1, HALF:]).then_inc(sem("sum0_mm"), 1)
            pe.wait_ge(sem("ln_cx_xn"), PCH)
            pe.wait_ge(sem("o0_norm"), 7 + 2)
            for i in range(PCH):
                if i >= 3:
                    pe.wait_ge(sem("ln_cx_t"), i - 2)
                for t in range(4 * i, min(4 * i + 4, KT)):
                    last = pe.transpose(spare[i % 3][:, (t % 4) * P:(t % 4 + 1) * P], c_nat[:, t, :], ident[:, :])
                last.then_inc(sem("ln_cx_mm"), 1)
            pe.wait_ge(sem("o0_norm"), 8 + 2)
            for t in range(NT):
                o = banks[t // 4][:, (t % 4) * P:(t % 4 + 1) * P]
                for g in range(G0):
                    mm(o, o0[:, g, t * P:(t + 1) * P], wo0[:, g, :], g == 0, False)
                last = mm(o, ones[0:1, :], rows0[0:1, P:2 * P], False)
            last.then_inc(sem("proj0_mm"), 1)

            def keys1(i):
                pe.wait_ge(sem("ln_cx_t"), PCH)
                if i >= 3:
                    pe.wait_ge(sem("k1_hi"), i - 2)
                mm(spare[i % 3][:, 0:PW[i]], wkv_c[:, 0:P], c_t[:, i * HALF:i * HALF + PW[i]]).then_inc(sem("k1_mm"), 1)

            for i in range(8):
                keys1(i)
            pe.wait_ge(sem("x1"), 1)
            ln_transposes("ln_f0", xn, NT)
            pe.wait_ge(sem("ln_f0_t"), 2)
            for t in range(NT):
                mm(ps_t[:, t * E:(t + 1) * E], xt[:, t * P:(t + 1) * P], wg0)
            for t in range(NT):
                last = mm(banks[t // 4][:, (t % 4) * P:(t % 4 + 1) * P], xt[:, t * P:(t + 1) * P], moe_a)
            last.then_inc(sem("moe_mm"), 1)
            for i in range(8, PCH):
                keys1(i)
            pe.wait_ge(sem("moe_hw"), 1)
            for t in range(NT):
                last = pe.transpose(banks[2 + t // 4][:, (t % 4) * P:(t % 4 + 1) * P], xn[:, t, :], ident[:, :])
            last.then_inc(sem("moe_tr"), 1)
            pe.wait_ge(sem("moe_ht"), 1)
            for t in range(NT):
                mm(banks[t // 4][:, (t % 4) * P:(t % 4 + 1) * P], xt[:, t * P:(t + 1) * P], moe_b).then_inc(sem("moe_out"), 1)

            for i in range(7):
                if i < 3:
                    pe.wait_ge(sem("k1_hi"), PCH)
                else:
                    pe.wait_ge(sem("v1_evac"), i - 2)
                for t in range(8 * i, min(8 * i + 8, KT)):
                    last = mm(spare[(i + 1) % 3][:, (t % 8) * HD1:(t % 8 + 1) * HD1], c_t[:, t * P:(t + 1) * P], wkv_c[:, P:P + HD1])
                last.then_inc(sem("v1_mm"), 1)
            pe.wait_ge(sem("v1_evac"), 7)
            pe.wait_ge(sem("x2"), 1)

            ln_transposes("ln_pb", hn, NT)
            pe.wait_ge(sem("ln_pb_t"), 2)
            pe.wait_ge(sem("w1_in"), 16 * 5)
            for i in range(8):
                if i >= 2:
                    pe.wait_ge(sem("ff_done"), i - 1)
                r, hf = i // 2, i % 2
                mm(banks[2 * (i % 2)], wff[:, r * P:(r + 1) * P], xt[:, hf * HALF:(hf + 1) * HALF])
                mm(banks[2 * (i % 2) + 1], wff[:, FFI + r * P:FFI + (r + 1) * P], xt[:, hf * HALF:(hf + 1) * HALF])\
                    .then_inc(sem("ff_mm"), 1)
            pe.wait_ge(sem("ff_done"), 8)
            for t in range(NT):
                for r in range(FFI // P):
                    last = mm(banks[t // 4][:, (t % 4) * P:(t % 4 + 1) * P], gated[:, r, t * P:(t + 1) * P], wffo[:, r, :],
                              r == 0, r == FFI // P - 1)
            last.then_inc(sem("ffo_mm"), 1)
            pe.wait_ge(sem("y_ff"), 1)
            for hf in range(2):
                mm(banks[hf], wkv_s[:, 0:P], xt[:, hf * HALF:(hf + 1) * HALF]).then_inc(sem("k1s_mm"), 1)
            for t in range(NT):
                last = mm(banks[2][:, t * HD1:(t + 1) * HD1], xt[:, t * P:(t + 1) * P], wkv_s[:, P:P + HD1])
            last.then_inc(sem("v1s_mm"), 1)
            pe.wait_ge(sem("k1s_split"), 2)
            pe.wait_ge(sem("v1s_evac"), 1)

            def query1(name, i, read):
                if i >= 4:
                    pe.wait_ge(sem(read), i - 3)
                mm(banks[i % 4], wq1[:, i // 2, :], xt[:, (i % 2) * HALF:(i % 2 + 1) * HALF]).then_inc(sem(name + "_mm"), 1)

            def max_chunk_s(h, n):
                t, c0, w = CHUNKS_S[n]
                pe.wait_ge(sem("sm_red"), 12 * h + n + 1)
                diagonal = c0 + w == P * (t + 1)
                last = mm(mslot(n)[:, 0:w], q1[:, ds(h * T + t * P, P)], k1s[:, c0:c0 + w], True, not diagonal)
                if diagonal:
                    last = mm(mslot(n)[:, w - P:w], identb[:, :], mask_qk[:, :], False, True)
                last.then_inc(sem("sm_mm"), 1)

            def shift1(k, h):
                pe.wait_ge(sem(k + "_parts"), h + 1)
                for t in range(NT):
                    at = 64 + 32 * (t // 4)
                    last = mm(ps_t[at:at + 32, (t % 4) * P:(t % 4 + 1) * P], shift_rows[:, t * 32:t * 32 + 32], ident16[:, :])
                last.then_inc(sem(k + "_turned"), 1)

            def scores_s(h, t):
                pe.wait_ge(sem("ps_exp"), 8 * h + t + 1)
                sl = ps_s[:, t % 2, :]
                parts = [(P * t, HALF), (HALF, T)] if t < 4 else [(P * t, T)]
                for lo, hi in parts:
                    mm(sl[:, lo:hi], k1s[:, t * P:(t + 1) * P], q1[:, ds(h * T + lo, hi - lo)], True, False)
                for lo, hi in parts:
                    mm(sl[:, lo:hi], k2s[:, t * P:(t + 1) * P], q2[:, ds(h * T + lo, hi - lo)], False, False)
                mm(sl[:, t * P:(t + 1) * P], identb[:, :], mask_kq[:, :], False, True).then_inc(sem("ss_mm"), 1)

            def pv_s(h, t):
                pe.wait_ge(sem("ps_exp"), 8 * h + t + 3)
                pr = p_slot(t).rearrange("p (i f c) -> p f i c", f=2, c=P)
                for f in range(2):
                    i = (t + 1 - f) // 2
                    if i < 4:
                        last = mm(ps_o[64 * f:64 * f + 64, i * P:HALF], v1s[:, t, :], pr[:, f, i:4], t == 0, t == 6 + f)
                last.then_inc(sem("os_mm"), 1)

            def sums_s(h, odd):
                pe.wait_ge(sem("s_add"), 8 * h + 8 + 4)
                for f in range(2):
                    last = mm(ps_t[64 * f:64 * f + 64, :], ones[:, 0:64],
                              accs[:, odd, :].rearrange("p (i f c) -> p f i c", f=2, c=P)[:, f], True, True)
                last.then_inc(sem("s_sums"), 1)

            def head_s(h, odd, first=False, maxima=True, more=True):
                for t in range(NT):
                    if t + 1 < NT:
                        scores_s(h, t + 1)
                    elif more:
                        pe.wait_ge(sem("s_shifted"), h + 2)
                        scores_s(h + 1, 0)
                    if maxima:
                        for n in STEPS_S[t]:
                            max_chunk_s(h + 2, n)
                    if t == 0:
                        pe.wait_ge(sem("s_evac"), h + 1)
                    pv_s(h, t)
                    if t == 0 and more:
                        pe.wait_ge(sem("s_shifted"), h + 1)
                        if not first:
                            pe.wait_ge(sem("s_recip"), 2 * h)
                        shift1("s", h + 1)
                    if t == 2 and not first:
                        pe.wait_ge(sem("s_shifted"), h + 2 if more else h + 1)
                        pe.wait_ge(sem("s_recip"), 2 * h)
                        sums_s(h - 1, 1 - odd)

            pe.wait_ge(sem("k2s_in"), 16)
            pe.wait_ge(sem("q2_zero"), 1)
            for i in range(4):
                query1("qs", i, "qs_split")
            for n in range(24):
                query1("qs", 4 + n, "qs_split")
                if n % 12 == 0:
                    pe.wait_ge(sem("qs_split"), 2 + n // 6)
                max_chunk_s(n // 12, n % 12)
                if n == 14:
                    shift1("s", 0)
            for i in range(28, 2 * H):
                query1("qs", i, "qs_split")
            pe.wait_ge(sem("qs_split"), 2 * H)
            pe.wait_ge(sem("s_shifted"), 1)
            scores_s(0, 0)
            head_s(0, 0, first=True)
            with pe.Fori(0, (H - 4) // 2) as n:
                head_s(2 * n + 1, 1)
                head_s(2 * n + 2, 0)
            head_s(H - 3, 1)
            head_s(H - 2, 0, maxima=False)
            head_s(H - 1, 1, maxima=False, more=False)
            pe.wait_ge(sem("s_recip"), 2 * H)
            sums_s(H - 1, 1)

            pe.wait_ge(sem("qw_deq"), 1)
            pe.wait_ge(sem("s_evac"), H + 1)
            for i in range(9):
                last = pe.transpose(ps_m[:, i * P:(i + 1) * P] if i < 8 else ps_o[:, 0:P], qw[:, i // 3, i % 3, :], ident[:, :])
            last.then_inc(sem("qw_mm"), 1)

            def project1(name, done, at):
                pe.wait_ge(sem(done), 16 + 1)
                for t in range(NT):
                    for p in range(H // 2):
                        last = mm(banks[t // 4][:, (t % 4) * P:(t % 4 + 1) * P], o1[:, p, at(t):at(t) + P], wproj[:, p, :],
                                  p == 0, p == H // 2 - 1)
                last.then_inc(sem(name), 1)

            project1("sp_mm", "s_o", lambda t: t % 2 * HALF + t // 2 * P)

            ln_transposes("ln_ca", hn, NT)
            pe.wait_ge(sem("ln_ca_t"), 2)
            pe.wait_ge(sem("w2_in"), 16 * 2)
            def max_chunk1(h, r, c):
                m = 104 * h + 13 * r + c
                pe.wait_ge(sem("m1_red"), m + 2 if c in (1, NCH - 1) else m + 1)
                mm(mslot3(c)[:, 0:CW[c]], q1[:, ds(h * T + r * P, P)], k1[:, c * HALF:c * HALF + CW[c]]).then_inc(sem("m1_mm"), 1)

            def scores1(h, kt):
                i = 51 * h + kt
                pe.wait_ge(sem("p1_exp"), i + 1)
                for n, (k, q) in enumerate(((k1, q1), (k2, q2))):
                    for hf in range(2):
                        last = mm(ps_flat[:, ds(((h + kt) % 2) * (2 * HALF) + hf * HALF, HALF)], k[:, ds(kt * P, P)],
                                  q[:, ds(h * T + hf * HALF, HALF)], n == 0, n == 1)
                last.then_inc(sem("s1_mm"), 1)

            def pv1(h, kt, slot, start, stop):
                i = 51 * h + kt
                pe.wait_ge(sem("v1_staged"), i + 1)
                pe.wait_ge(sem("p1_exp"), i + 3)
                for hf in range(2):
                    last = mm(ps_o[64 * hf:64 * hf + 64, :], v_stage[:, slot, :],
                              probs[:, slot, hf * HALF:(hf + 1) * HALF], start, stop)
                last.then_inc(sem("o1_mm"), 1)

            def sums_c(h):
                pe.wait_ge(sem("c_add_v"), 18 * h + 18 + 2)
                pe.wait_ge(sem("c_add_g"), 33 * h + 33 + 2)
                for i, acc in enumerate((acc_v, acc_g)):
                    for hf in range(2):
                        last = mm(ps_t[64 * hf:64 * hf + 64, :], ones[:, 0:64], acc[:, hf * HALF:(hf + 1) * HALF], i == 0, i == 1)
                last.then_inc(sem("c_sums"), 1)

            def head_c(h, first=False, more=True):
                for u in range(3):
                    scores1(h, u + 1)
                    if u == 0:
                        if not first:
                            sums_c(h - 1)
                        pe.wait_ge(sem("c_evac"), h + 1)
                    if u == 2 and more and not first:
                        pe.wait_ge(sem("c_recip"), 2 * h)
                    pv1(h, u, u, u == 0, False)

                def group(r, last):
                    for u in range(6):
                        kt = 3 + 6 * r + u
                        ch = list((CHUNKS1_LAST if last else CHUNKS1)[u]) if more else []
                        for c in ch[0:1]:
                            max_chunk1(h + 1, r, c)
                        if not (last and u == 5):
                            scores1(h, kt + 1)
                        for c in ch[1:]:
                            max_chunk1(h + 1, r, c)
                        pv1(h, kt, u % 3, False, last and u == 5)
                        if last and more and u == 4:
                            shift1("c", h + 1)

                with pe.Fori(0, 7) as r:
                    group(r, False)
                group(7, True)
                if more:
                    pe.wait_ge(sem("c_shifted"), h + 2)
                    scores1(h + 1, 0)

            pe.wait_ge(sem("qw_t"), 1)
            made = 0
            for n in range(NT * NCH):
                while made < 2 * H and made < 2 + n * 2 * H // (NT * NCH - 8):
                    query1("qc", made, "qc_read")
                    made += 1
                if n == 0:
                    pe.wait_ge(sem("qc_split"), 2)
                max_chunk1(0, n // NCH, n % NCH)
            assert made == 2 * H
            shift1("c", 0)
            pe.wait_ge(sem("qc_split"), 2 * H)
            pe.wait_ge(sem("c_shifted"), 1)
            pe.wait_ge(sem("k2_in"), 16)
            scores1(0, 0)
            head_c(0, first=True)
            with pe.Fori(1, H - 1) as h:
                head_c(h)
            head_c(H - 1, more=False)
            pe.wait_ge(sem("c_recip"), 2 * (H - 1))
            sums_c(H - 1)
            project1("cp_mm", "c_o", lambda t: t * P)

            ln_transposes("ln_f1", xn, NT)
            pe.wait_ge(sem("qx"), 1)
            for w in range(2):
                for i in range(6):
                    n = 6 * w + i
                    if n >= 4:
                        pe.wait_ge(sem("ug_evac"), n - 3)
                    mm(banks[n % 4], qwt[:, w, i // 2, :], xt[:, (i % 2) * HALF:(i % 2 + 1) * HALF]).then_inc(sem("ug_mm"), 1)
            pe.wait_ge(sem("ug_evac"), 12)
            pe.wait_ge(sem("o_q"), 1)
            for t in range(NT):
                for c in range(3):
                    last = mm(banks[t // 4][:, (t % 4) * P:(t % 4 + 1) * P], gate[:, c, t * P:(t + 1) * P], qwt[:, 2, c, :],
                              c == 0, c == 2)
                last.then_inc(sem("down_mm"), 1)

        @block.vector
        def _(dve):
            link = Chain(dve, sem("dve_link"))
            dve.sem_inc(sem("o0_norm"), 2)
            dve.sem_inc(sem("m0_red"), 3)
            dve.sem_inc(sem("m1_red"), 3)
            dve.sem_inc(sem("m0_unit"), 1)
            dve.sem_inc(sem("m1_unit"), 1)
            dve.sem_inc(sem("sm_red"), 2)
            dve.sem_inc(sem("s_recip"), 2)
            dve.sem_inc(sem("c_add_v"), 2)
            dve.sem_inc(sem("c_o"), 1)

            def flat(t3):
                return t3.rearrange("p a b -> p (a b)")

            def layernorm(name, src, dst, nt, stats=stats, mv=mv, sdev=sdev, rstd=rstd):
                for t in range(nt):
                    last = dve.bn_stats(stats[:, t, :], src[:, t, :])
                link(last)
                for t in range(nt):
                    last = dve.bn_aggr(mv[:, t, :], stats[:, t, :])
                link(last)
                dve.tensor_scalar(sdev[:, 0:nt], mv[:, 0:nt, 1], EPS, None, ALU.add).then_inc(sem(name + "_var"), 1)
                dve.wait_ge(sem(name + "_sd"), 1)
                link(dve.reciprocal(rstd[:, 0:nt], sdev[:, 0:nt]))
                for t in range(nt):
                    last = dve.tensor_scalar(dst[:, t, :], src[:, t, :], mv[:, t, 0:1], rstd[:, t:t + 1], ALU.subtract, ALU.mult)
                    if t % 4 == 3 or t == nt - 1:
                        last.then_inc(sem(name + "_xn"), 1)

            dve.wait_ge(sem("x_in"), 16)
            dve.wait_ge(sem("const_in"), 16 * 5)
            layernorm("ln_a0", x, xn, NT)
            dve.wait_ge(sem("masks_in"), 16)
            dve.tensor_copy(identb[:, :], ident[:, :])
            dve.tensor_copy(mask_kq[:, :], probs[:, 0, 0:P])
            link(dve.tensor_copy(mask_qk[:, :], probs[:, 0, P:2 * P]))
            dve.sem_inc(sem("masks"), 1)

            dve.wait_ge(sem("zeros"), 2)
            link(dve.tensor_scalar(qb0s[:, :], cols[:, 4:4 + H], col(C_QS), None, ALU.mult))
            dve.sem_inc(sem("qb0s"), 1)
            for n in range(len(FIRST0)):
                dve.wait_ge(sem("item_hi"), n + 1)
                subtract_hi(dve, n, n).then_inc(sem("item_split"), 1)
            dve.wait_ge(sem("item_split"), len(FIRST0))
            dve.tensor_scalar(k0[:, CTX:CTXP], zeros16[:, 0:CTXP - CTX], col(C_PAD0), None, ALU.add)\
                .then_inc(sem("k0_pad"), 1)

            rows4 = shift_rows[:, :].rearrange("p (t j r) -> p j t r", t=4, j=4)
            rows8 = shift_rows[:, 0:8 * 32].rearrange("p (t r) -> p t r", r=32)

            def negated_parts(link_sem, base, ready, part, mxv, rest):
                ch = Chain(dve, sem(link_sem), base, 4)
                ch(dve.tensor_scalar(part(0), mxv, -1.0, None, ALU.mult))
                ch(dve.scalar_tensor_tensor(out=rest(0), in0=mxv, scalar=-1.0, in1=part(0), op0=ALU.mult, op1=ALU.subtract))
                ch(dve.tensor_copy(part(1), rest(0)))
                ch(dve.tensor_tensor(rest(1), rest(0), part(1), ALU.subtract))
                dve.tensor_copy(part(2), rest(1)).then_inc(sem(ready), 1)
                ch.check()

            def unit0(b, n):
                dve.wait_ge(sem("m0_unit"), 16 * b + n + 1)
                for c in range(NCH):
                    dve.wait_ge(sem("m0_mm"), 208 * b + 13 * n + c + 1)
                    dve.tensor_reduce(mpart[:, c:c + 1], mslot3(c)[:, 0:CW[c]], AX.X, ALU.max).then_inc(sem("m0_red"), 1)
                dve.wait_ge(sem("m0_red"), 208 * b + 13 * n + NCH + 3)
                dve.tensor_reduce(mx[:, ds(n, 1)], mpart[:, 0:NCH], AX.X, ALU.max).then_inc(sem("m0_unit"), 1)

            def shift_block0(b):
                dve.wait_ge(sem("m0_unit"), 16 * b + 16 + 1)
                negated_parts("m0_link", 4 * b, "m0_parts",
                              lambda k: rows4[:, :, :, ROW_SHIFT0 + k],
                              mx[:, :].rearrange("p (j t) -> p j t", j=4),
                              lambda k: mrest[:, k, :].rearrange("p (j t) -> p j t", j=4))
                dve.wait_ge(sem("m0_turned"), b + 1)
                for j in range(4):
                    q = q0[32 * j:32 * j + 32, ds((b // 2) * (4 * T) + (b % 2) * HALF + j * T, HALF)]
                    dve.tensor_tensor(q, ps_t[32 * j:32 * j + 32, :], q, ALU.add).then_inc(sem("q0_shifted"), 1)

            with dve.Fori(0, 8) as b:
                with dve.Fori(0, 16) as n:
                    unit0(b, n)
                shift_block0(b)

            def normalise0(b, bank):
                dve.wait_ge(sem("sum0_mm"), b + 1)
                link(dve.reciprocal(recip[:, :], bank))
                o = o0[:, b // 2, (b % 2) * HALF:(b % 2 + 1) * HALF]
                link(dve.tensor_tensor(o, o, recip[:, :], ALU.mult))
                dve.sem_inc(sem("o0_norm"), 1)

            for b in range(7):
                normalise0(b, spare[b % 2])
            dve.wait_ge(sem("ctx1_in"), 32)
            layernorm("ln_cx", c_nat, c_nat, KT, c_stats, c_mv, c_sdev, c_rstd)

            normalise0(7, ps_t[:, :])
            dve.wait_ge(sem("proj0_mm"), 1)
            link(dve.tensor_tensor(flat(x[:, :, :]), ps_s[:, 0, :], flat(x[:, :, :]), ALU.add))
            dve.sem_inc(sem("x1"), 1)
            layernorm("ln_f0", x, xn, NT)

            dve.wait_ge(sem("moe_mm"), 1)
            lg = y_tmp[0][:, 0:64].rearrange("p (t e) -> p t e", e=E)
            ex = y_tmp[0][:, 64:128].rearrange("p (t e) -> p t e", e=E)
            rank = y_tmp[0][:, 128:192].rearrange("p (t e) -> p t e", e=E)
            m1 = y_tmp[0][:, 192:200]
            ssum = y_tmp[0][:, 200:208]
            ahead = y_tmp[1].rearrange("p (t e f) -> p t e f", e=E, f=E)
            link(dve.tensor_copy(flat(lg), ps_t[:, 0:NT * E]))
            link(dve.memset(y_tmp[1], 0.0))
            link(dve.tensor_reduce(m1, lg, AX.X, ALU.max))
            for f in range(E):
                one = lg[:, :, f:f + 1]
                if f + 1 < E:
                    last = dve.tensor_tensor(ahead[:, :, f + 1:E, f], one.broadcast_to([P, NT, E - f - 1]), lg[:, :, f + 1:E], ALU.is_ge)
                if f:
                    last = dve.tensor_tensor(ahead[:, :, 0:f, f], one.broadcast_to([P, NT, f]), lg[:, :, 0:f], ALU.is_gt)
            link(last)
            link(dve.tensor_reduce(rank, ahead, AX.X, ALU.add))
            link(dve.tensor_scalar(rank, rank, 1.5, None, ALU.is_lt))
            dve.tensor_tensor(ex, lg, m1.unsqueeze(2).broadcast_to([P, NT, E]), ALU.subtract).then_inc(sem("moe_d"), 1)
            dve.wait_ge(sem("moe_exp"), 1)
            link(dve.tensor_tensor(ex, ex, rank, ALU.mult))
            link(dve.tensor_reduce(ssum, ex, AX.X, ALU.add))
            link(dve.reciprocal(ssum, ssum))
            link(dve.tensor_tensor(ex, ex, ssum.unsqueeze(2).broadcast_to([P, NT, E]), ALU.mult))
            dve.tensor_tensor(flat(xn[:, :, :]).rearrange("p (a r) -> p a r", r=R), ps_s[:, 0, :].rearrange("p (a r) -> p a r", r=R),
                              flat(ex).unsqueeze(2).broadcast_to([P, NT * E, R]), ALU.mult).then_inc(sem("moe_hw"), 1)
            dve.wait_ge(sem("moe_out"), NT)
            link(dve.tensor_tensor(flat(x[:, :, :]), ps_s[:, 0, :], flat(x[:, :, :]), ALU.add))
            dve.sem_inc(sem("x2"), 1)

            layernorm("ln_a1", x, xn, NT)
            dve.wait_ge(sem("ln_a1_xn"), 2)
            dve.wait_ge(sem("k1_split"), PCH)
            layernorm("ln_pb", xn, hn, NT)

            dve.wait_ge(sem("ln_pb_t"), 2)
            for i in range(8):
                r, hf = i // 2, i % 2
                e = y_tmp[i % 2]
                g = gated[:, r, hf * HALF:(hf + 1) * HALF]
                dve.wait_ge(sem("ff_silu"), i + 1)
                dve.tensor_tensor(g, banks[2 * (i % 2)], e, ALU.mult).then_inc(sem("ff_done"), 1)
            dve.wait_ge(sem("ffo_mm"), 1)
            dve.tensor_tensor(flat(xn[:, :, :]), ps_s[:, 0, :], flat(xn[:, :, :]), ALU.add).then_inc(sem("y_ff"), 1)
            for i in range(2):
                dve.wait_ge(sem("k1s_hi"), i + 1)
                s = slice(i * HALF, (i + 1) * HALF)
                dve.tensor_tensor(k2s[0:64, s], banks[i][0:64, :], k1s[0:64, s], ALU.subtract).then_inc(sem("k1s_split"), 1)

            def split_query(i):
                dve.wait_ge(sem("qs_hi"), i + 1)
                lo = q1[64:128, i * HALF:(i + 1) * HALF]
                dve.scalar_tensor_tensor(out=lo, in0=banks[i % 4][64:128, :], scalar=HD1 ** -0.5, in1=lo,
                                         op0=ALU.mult, op1=ALU.subtract).then_inc(sem("qs_split"), 1)

            def reduce_s(h, n):
                t, c0, w = CHUNKS_S[n]
                dve.wait_ge(sem("sm_mm"), 12 * h + n + 1)
                at = t if c0 == 0 else 4 + t
                dve.tensor_reduce(mx[:, at:at + 1], mslot(n)[:, 0:w], AX.X, ALU.max).then_inc(sem("sm_red"), 1)

            def parts_s(h):
                dve.wait_ge(sem("sm_red"), 12 * h + 12 + 2)
                dve.tensor_tensor(mx[:, 4:8], mx[:, 4:8], mx[:, 8:12], ALU.max).then_inc(sem("s_unit"), 1)
                dve.wait_ge(sem("s_unit"), h + 1)
                negated_parts("s_link", 4 * h, "s_parts", lambda p: rows8[:, :, p], mx[:, 0:NT], lambda p: mrest[:, p, 0:NT])

            def recip_s(h, i):
                dve.wait_ge(sem("s_sums"), h + 1 + 2)
                dve.wait_ge(sem("s_o"), h + 1)
                s = slice(i * HALF // 2, (i + 1) * HALF // 2)
                dve.reciprocal(recip[:, s], ps_t[:, s]).then_inc(sem("s_recip"), 1)

            def head_s(h, first=False, maxima=True):
                for n in range(12):
                    if n in (6, 7) and not first:
                        recip_s(h - 1, n - 6)
                    if maxima:
                        reduce_s(h + 2, n)
                if maxima:
                    dve.wait_ge(sem("s_turned"), h + 2)
                    parts_s(h + 2)

            dve.wait_ge(sem("shift_zero"), 2)
            for i in range(4):
                split_query(i)
            for n in range(24):
                split_query(4 + n)
                reduce_s(n // 12, n % 12)
                if n == 11:
                    parts_s(0)
            dve.wait_ge(sem("s_turned"), 1)
            parts_s(1)
            for i in range(28, 2 * H):
                split_query(i)
            head_s(0, first=True)
            with dve.Fori(1, H - 2) as h:
                head_s(h)
            head_s(H - 2, maxima=False)

            dve.wait_ge(sem("qw_in"), 16)
            wb = qw.rearrange("p a b d -> p (a b d)").rearrange("p (n k) -> p n k", k=BLK)
            link(dve.tensor_reduce(wscale, wb, AX.X, ALU.max, apply_absolute_value=True))
            link(dve.tensor_scalar(wscale, wscale, 1.0 / 7.0, 1e-12, ALU.mult, ALU.max))
            link(dve.reciprocal(winv, wscale))
            link(dve.tensor_tensor(wb, wb, winv.unsqueeze(2).broadcast_to([P, NB, BLK]), ALU.mult))
            link(dve.tensor_scalar(wb, wb, ROUND, ROUND, ALU.add, ALU.subtract))
            link(dve.tensor_scalar(wb, wb, 7.0, -8.0, ALU.min, ALU.max))
            dve.tensor_tensor(wb, wb, wscale.unsqueeze(2).broadcast_to([P, NB, BLK]), ALU.mult).then_inc(sem("qw_deq"), 1)

            head_s(H - 1, maxima=False)
            recip_s(H - 1, 0)
            recip_s(H - 1, 1)

            dve.wait_ge(sem("sp_mm"), 1)
            link(dve.tensor_tensor(flat(xn[:, :, :]), ps_s[:, 0, :], flat(xn[:, :, :]), ALU.add))

            layernorm("ln_ca", xn, hn, NT)
            def reduce1(h, r, c):
                if c == 0:
                    dve.wait_ge(sem("m1_unit"), 8 * h + r + 1)
                dve.wait_ge(sem("m1_mm"), 104 * h + 13 * r + c + 1)
                dve.tensor_reduce(mpart[:, c:c + 1], mslot3(c)[:, 0:CW[c]], AX.X, ALU.max).then_inc(sem("m1_red"), 1)

            def unit1(h, r):
                dve.wait_ge(sem("m1_red"), 104 * h + 13 * r + NCH + 3)
                dve.tensor_reduce(mx[:, ds(r, 1)], mpart[:, 0:NCH], AX.X, ALU.max).then_inc(sem("m1_unit"), 1)

            def parts_c(h):
                dve.wait_ge(sem("m1_unit"), 8 * h + 8 + 1)
                negated_parts("c_link", 4 * h, "c_parts", lambda p: rows8[:, :, p], mx[:, 0:NT], lambda p: mrest[:, p, 0:NT])

            def add_v(h, n, slot=0):
                dve.wait_ge(sem("p1_exp"), 51 * h + 3 * n + 3 if slot == 0 else 51 * h + 50 + 3)
                dve.wait_ge(sem("c_add_v"), 18 * h + n + 2)
                dve.tensor_tensor(acc_v, acc_v, probs[:, slot, :], ALU.add).then_inc(sem("c_add_v"), 1)

            def normalise_c(h, odd):
                dve.wait_ge(sem("c_sums"), h + 2)
                dve.wait_ge(sem("c_o"), h + 1)
                for i in range(2):
                    s = slice(i * HALF // 2, (i + 1) * HALF // 2)
                    dve.reciprocal(recip[:, s], ps_t[:, s]).then_inc(sem("c_recip"), 1)
                dve.wait_ge(sem("c_recip"), 2 * h + 2)
                dve.wait_ge(sem("c_evac"), h + 1 + 1)
                divide(dve, h, odd, sem("c_o"))

            def head_c(h, odd, first=False, more=True):
                dve.wait_ge(sem("p1_exp"), 51 * h + 3)
                dve.wait_ge(sem("c_sums"), h + 1)
                dve.tensor_copy(acc_v, probs[:, 0, :]).then_inc(sem("c_add_v"), 1)
                if not first:
                    normalise_c(h - 1, 1 - odd)

                def group(r, last):
                    for u in range(6):
                        if more:
                            for c in (CHUNKS1_LAST if last else CHUNKS1)[u]:
                                reduce1(h + 1, r, c)
                            if u == (3 if last else 5):
                                unit1(h + 1, r)
                        if last and more and u == 3:
                            dve.wait_ge(sem("c_turned"), h + 1)
                            parts_c(h + 1)
                        if u % 3 == 0:
                            add_v(h, 1 + 2 * r + u // 3)
                    if last:
                        add_v(h, 17, 2)

                with dve.Fori(0, 7) as r:
                    group(r, False)
                group(7, True)

            with dve.Fori(0, NT) as r:
                for c in range(NCH):
                    reduce1(0, r, c)
                unit1(0, r)
            parts_c(0)
            head_c(0, 0, first=True)
            with dve.Fori(0, H // 2 - 1) as n:
                head_c(2 * n + 1, 1)
                head_c(2 * n + 2, 0)
            head_c(H - 1, 1, more=False)
            normalise_c(H - 1, 1)

            dve.wait_ge(sem("cp_mm"), 1)
            link(dve.tensor_tensor(flat(x[:, :, :]), ps_s[:, 0, :], flat(x[:, :, :]), ALU.add))

            layernorm("ln_f1", x, xn, NT)

            amax = [y_tmp[0][:, 128 + i:129 + i] for i in range(5)]
            gmax = [y_tmp[0][:, 136 + i:137 + i] for i in range(5)]
            scale = [y_tmp[0][:, 144 + i:145 + i] for i in range(5)]
            inv = [y_tmp[0][:, 152 + i:153 + i] for i in range(5)]

            chunk_max = y_tmp[0][:, 160:166]

            def quantise(n, z, done=None, parts=None):
                dve.tensor_reduce(amax[n], z if parts is None else parts, AX.X, ALU.max, apply_absolute_value=True)\
                    .then_inc(sem("q_amax"), 1)
                dve.wait_ge(sem("q_gmax"), n + 1)
                link(dve.tensor_scalar(scale[n], gmax[n], 1.0 / QMAX, 1e-12, ALU.mult, ALU.max))
                link(dve.reciprocal(inv[n], scale[n]))
                link(dve.tensor_scalar(z, z, inv[n], ROUND, ALU.mult, ALU.add))
                link(dve.tensor_scalar(z, z, ROUND, QMAX, ALU.subtract, ALU.min))
                last = dve.tensor_scalar(z, z, -QMAX - 1.0, scale[n], ALU.max, ALU.mult)
                if done:
                    last.then_inc(sem(done), 1)
                else:
                    link(last)

            upf, gatef, sigf, tmpf = (flat(v) for v in (up, gate, sig, tmp))
            dve.wait_ge(sem("ln_f1_t"), 2)
            quantise(0, xt[:, :], "qx")
            for i in range(6):
                dve.wait_ge(sem("ug_evac"), i + 1)
                last = dve.tensor_reduce(chunk_max[:, i:i + 1], gate[:, i // 2, (i % 2) * HALF:(i % 2 + 1) * HALF], AX.X, ALU.max,
                                         apply_absolute_value=True)
            link(last)
            quantise(1, gatef, "gate_q", chunk_max)
            dve.wait_ge(sem("ug_evac"), 12)
            quantise(2, upf)
            dve.wait_ge(sem("sigmoid"), 1)
            link(dve.tensor_scalar(sigf, sigf, 65536.0, ROUND, ALU.mult, ALU.add))
            link(dve.tensor_scalar(sigf, sigf, ROUND, 0.0, ALU.subtract, ALU.max))
            link(dve.tensor_scalar(sigf, sigf, 65535.0, 1.0 / 65536.0, ALU.min, ALU.mult))
            link(dve.tensor_tensor(tmpf, gatef, sigf, ALU.mult))
            quantise(3, tmpf)
            link(dve.tensor_tensor(gatef, tmpf, upf, ALU.mult))
            quantise(4, gatef, "o_q")
            for t in range(NT):
                dve.wait_ge(sem("down_mm"), 4 * (t // 4) + 4)
                dve.tensor_tensor(x[:, t, :], banks[t // 4][:, (t % 4) * P:(t % 4 + 1) * P], x[:, t, :], ALU.add)\
                    .then_inc(sem("y_out"), 1)

        @block.scalar
        def _(act):
            act.sem_inc(sem("p0_exp"), 2)
            act.sem_inc(sem("ps_exp"), 2)
            act.sem_inc(sem("s_evac"), 1)
            act.sem_inc(sem("c_evac"), 1)
            act.sem_inc(sem("p1_exp"), 2)
            act.sem_inc(sem("o0_evac"), 1)

            def sqrt(name, nt, sdev=sdev):
                act.wait_ge(sem(name + "_var"), 1)
                act.activation(sdev[:, 0:nt], sdev[:, 0:nt], ACT.Sqrt).then_inc(sem(name + "_sd"), 1)

            def columns(name, dst, nt, gamma=None):
                for i in range(0, nt, 4):
                    n = min(4, nt - i) * P
                    act.wait_ge(sem(name + "_mm"), i // 4 + 1)
                    act.activation(dst[:, i * P:i * P + n], banks[i // 4 % 4][:, 0:n], ACT.Copy,
                                   scale=1.0 if gamma is None else gamma).then_inc(sem(name + "_t"), 1)

            act.wait_ge(sem("const_in"), 16 * 5)
            sqrt("ln_a0", NT)
            act.wait_ge(sem("masks"), 1)
            act.wait_ge(sem("qb0s"), 1)
            act.wait_ge(sem("v0_ones"), 1)
            columns("ln_a0", xt, NT)
            v0h = v0.rearrange("p t (h c) -> p t h c", c=9)
            j = 0
            for n, (kind, i, c) in enumerate(ITEMS0):
                act.wait_ge(sem("item_mm"), n + 1)
                bank = banks[n % 4]
                if kind == "v":
                    for t in range(4 * i, min(4 * i + 4, KT)):
                        last = act.activation(v0h[:, t, :, 0:HD0],
                                              bank[:, (t % 4) * P:(t % 4 + 1) * P].rearrange("p (h c) -> p h c", c=HD0), ACT.Copy)
                    last.then_inc(sem("item_read"), 1)
                    continue
                if j >= 2:
                    act.wait_ge(sem("item_split"), j - 1)
                w = PW[c] if kind == "k" else HALF
                y = y_tmp[j % 2][:, 0:w]
                if kind == "k":
                    act.activation(y, bank[:, 0:w], ACT.Identity, bias=kb0[i]).then_inc(sem("item_read"), 1)
                else:
                    act.activation(y, bank, ACT.Identity, bias=qb0s[:, i:i + 1], scale=col(C_QS)).then_inc(sem("item_read"), 1)
                act.wait_ge(sem("item_read"), n + 1)
                act.activation(hm_tmp[j % 2][:, 0:w], y, ACT.Copy, scale=col(C_KLO if kind == "k" else C_QLO))\
                    .then_inc(sem("item_hi"), 1)
                j += 1

            act.preload_act_table(ACT.Exp)
            act.wait_ge(sem("item_read"), len(ITEMS0))
            act.wait_ge(sem("item_split"), NSPLIT)

            def exp0(b, n, u):
                kt = 3 * n + u
                i = 51 * b + kt
                act.wait_ge(sem("o0_mm"), i + 1)
                act.activation(v_stage[:, u, 0:36], v0[:, ds(kt, 1), ds((b // 2) * 36, 36)].rearrange("p a b -> p (a b)"),
                               ACT.Copy).then_inc(sem("v0_staged"), 1)
                for hp in range(2):
                    act.wait_ge(sem("s0_mm"), 2 * i + hp + 1)
                    act.wait_ge(sem("o0_mm"), i + 2 + hp)
                    act.activation(probs[:, (2 * u + hp) % 3, :], ps_s[:, hp, :], ACT.Exp).then_inc(sem("p0_exp"), 1)

            def block0(b, more):
                exp0(b, 0, 1)
                exp0(b, 0, 2)
                if more:
                    with act.Fori(1, KT // 3) as n:
                        for u in range(3):
                            exp0(b, n, u)
                else:
                    with act.Fori(1, 13) as n:
                        for u in range(3):
                            exp0(b, n, u)
                    sqrt("ln_cx", KT, c_sdev)
                    act.preload_act_table(ACT.Exp)
                    with act.Fori(13, KT // 3) as n:
                        for u in range(3):
                            exp0(b, n, u)
                if more:
                    exp0(b + 1, 0, 0)
                act.wait_ge(sem("o0_mm"), 51 * b + 51 + 3)
                act.activation(o0[:, ds(b // 2, 1), ds((b % 2) * HALF, HALF)].rearrange("p a b -> p (a b)"), ps_o[:, :], ACT.Copy)\
                    .then_inc(sem("o0_evac"), 1)

            exp0(0, 0, 0)
            with act.Fori(0, 7) as b:
                block0(b, True)
            block0(7, False)

            for i in range(PCH):
                act.wait_ge(sem("ln_cx_mm"), i + 1)
                act.activation(c_t[:, i * HALF:i * HALF + PW[i]], spare[i % 3][:, 0:PW[i]], ACT.Copy, scale=col(C_GC))\
                    .then_inc(sem("ln_cx_t"), 1)

            def hi_keys1(i):
                act.wait_ge(sem("k1_mm"), i + 1)
                if i >= 2:
                    act.wait_ge(sem("k1_split"), i - 1)
                act.activation(k_tmp[i % 2][:, 0:PW[i]], spare[i % 3][0:64, 0:PW[i]], ACT.Copy)
                act.activation(k1[:, i * HALF:i * HALF + PW[i]], spare[i % 3][:, 0:PW[i]], ACT.Copy).then_inc(sem("k1_hi"), 1)

            act.preload_act_table(ACT.Sqrt)
            for i in range(4):
                hi_keys1(i)
            sqrt("ln_f0", NT)
            for i in range(4, 8):
                hi_keys1(i)
            columns("ln_f0", xt, NT)
            act.preload_act_table(ACT.Exp)
            for i in range(8, 11):
                hi_keys1(i)
            ex = y_tmp[0][:, 64:128]
            act.wait_ge(sem("moe_d"), 1)
            act.activation(ex, ex, ACT.Exp).then_inc(sem("moe_exp"), 1)
            act.preload_act_table(ACT.Sqrt)
            for i in range(11, PCH):
                hi_keys1(i)
            act.wait_ge(sem("moe_tr"), 1)
            act.activation(xt[:, :], ps_s[:, 1, :], ACT.Copy).then_inc(sem("moe_ht"), 1)

            for i in range(7):
                if i == 2:
                    sqrt("ln_a1", NT)
                act.wait_ge(sem("v1_mm"), i + 1)
                n = min(8, KT - 8 * i)
                act.activation(v1[:, 8 * i:8 * i + n, :].rearrange("p a b -> p (a b)"), spare[(i + 1) % 3][:, 0:n * HD1], ACT.Copy)\
                    .then_inc(sem("v1_evac"), 1)
            sqrt("ln_pb", NT)
            act.preload_act_table(ACT.Silu)
            columns("ln_pb", xt, NT, col(C_GP))

            for i in range(8):
                act.wait_ge(sem("ff_mm"), i + 1)
                if i >= 2:
                    act.wait_ge(sem("ff_done"), i - 1)
                act.activation(y_tmp[i % 2], banks[2 * (i % 2) + 1], ACT.Silu).then_inc(sem("ff_silu"), 1)
            for i in range(2):
                act.wait_ge(sem("k1s_mm"), i + 1)
                act.activation(k1s[:, i * HALF:(i + 1) * HALF], banks[i], ACT.Copy).then_inc(sem("k1s_hi"), 1)
            act.wait_ge(sem("v1s_mm"), 1)
            act.activation(v1s.rearrange("p a b -> p (a b)"), banks[2], ACT.Copy).then_inc(sem("v1s_evac"), 1)

            def exp_s(h, t):
                i = 8 * h + t
                act.wait_ge(sem("ss_mm"), i + 1)
                act.wait_ge(sem("os_mm"), i + 1)
                act.wait_ge(sem("s_add"), i + 1)
                act.activation(p_slot(t)[:, P * t:T], ps_s[:, t % 2, P * t:T], ACT.Exp).then_inc(sem("ps_exp"), 1)

            def shift_copies(k, h):
                act.wait_ge(sem(k + "_turned"), h + 1)
                act.activation(q2[64:96, ds(h * T, HALF)], ps_t[64:96, :], ACT.Copy)
                act.activation(q2[64:96, ds(h * T + HALF, HALF)], ps_t[96:128, :], ACT.Copy).then_inc(sem(k + "_shifted"), 1)

            def head_s(h, more=True):
                for t in range(1, NT):
                    exp_s(h, t)
                    if t == 1 and more:
                        shift_copies("s", h + 1)
                if more:
                    exp_s(h + 1, 0)
                act.wait_ge(sem("os_mm"), 8 * h + 8 + 4)
                act.wait_ge(sem("s_o"), h + 1)
                act.activation(o_raw, ps_o[:, :], ACT.Copy).then_inc(sem("s_evac"), 1)

            for i in range(2 * H):
                act.wait_ge(sem("qs_mm"), i + 1)
                s = slice(i * HALF, (i + 1) * HALF)
                act.activation(q2[0:64, s], banks[i % 4][0:64, :], ACT.Copy, scale=HD1 ** -0.5)
                act.activation(q1[:, s], banks[i % 4], ACT.Copy, scale=HD1 ** -0.5).then_inc(sem("qs_hi"), 1)
                if i == 19:
                    shift_copies("s", 0)
            act.preload_act_table(ACT.Exp)
            exp_s(0, 0)
            with act.Fori(0, H - 1) as h:
                head_s(h)
            head_s(H - 1, more=False)

            act.wait_ge(sem("qw_mm"), 1)
            act.activation(qwt.rearrange("p a b d -> p (a b d)")[:, 0:8 * P], ps_m[:, :], ACT.Copy)
            act.activation(qwt[:, 2, 2, :], ps_o[:, 0:P], ACT.Copy).then_inc(sem("qw_t"), 1)
            act.preload_act_table(ACT.Sqrt)
            sqrt("ln_ca", NT)
            columns("ln_ca", xt, NT, col(C_GX))
            for i in range(2 * H):
                act.wait_ge(sem("qc_mm"), i + 1)
                s = slice(i * HALF, (i + 1) * HALF)
                if i >= 2:
                    act.wait_ge(sem("qc_split"), i - 1)
                act.activation(y_tmp[i % 2], banks[i % 4], ACT.Copy, scale=HD1 ** -0.5).then_inc(sem("qc_read"), 1)
                act.wait_ge(sem("qc_read"), i + 1)
                act.activation(q2[0:64, s], y_tmp[i % 2][0:64, :], ACT.Copy)
                act.activation(q1[:, s], y_tmp[i % 2], ACT.Copy).then_inc(sem("qc_hi"), 1)

            act.preload_act_table(ACT.Exp)

            def exp_c(h, n, u, first=False):
                i = 51 * h + 3 * n + u
                act.wait_ge(sem("o1_mm"), i + 1)
                act.activation(v_stage[:, u, :], v1[:, ds(3 * n + u, 1), :].rearrange("p a b -> p (a b)"), ACT.Copy)\
                    .then_inc(sem("v1_staged"), 1)
                act.wait_ge(sem("s1_mm"), i + 1)
                if u == 0 or first and u == 2:
                    act.wait_ge(sem("c_add_v"), 18 * h + n + 2)
                else:
                    act.wait_ge(sem("c_add_g"), 33 * h + (2 if first else 2 * n + u))
                act.activation(probs[:, u, :], ps_flat[:, ds(((h + n + u) % 2) * (2 * HALF), 2 * HALF)], ACT.Exp)\
                    .then_inc(sem("p1_exp"), 1)

            def head_c(h, more=True):
                for u in range(3):
                    exp_c(h, 0, u, first=True)
                with act.Fori(1, KT // 3) as n:
                    for u in range(3):
                        exp_c(h, n, u)
                if more:
                    shift_copies("c", h + 1)
                act.wait_ge(sem("o1_mm"), 51 * h + 51 + 3)
                act.wait_ge(sem("c_o"), h + 1)
                act.activation(o_raw, ps_o[:, :], ACT.Copy).then_inc(sem("c_evac"), 1)

            act.wait_ge(sem("qc_split"), 2 * H)
            shift_copies("c", 0)
            with act.Fori(0, H - 1) as h:
                head_c(h)
            head_c(H - 1, more=False)

            act.preload_act_table(ACT.Sqrt)
            sqrt("ln_f1", NT)
            columns("ln_f1", xt, NT)
            for n in range(12):
                i = n % 6
                dst = (gate, up)[n // 6]
                act.wait_ge(sem("ug_mm"), n + 1)
                act.activation(dst[:, i // 2, (i % 2) * HALF:(i % 2 + 1) * HALF], banks[n % 4], ACT.Copy).then_inc(sem("ug_evac"), 1)
            act.wait_ge(sem("gate_q"), 1)
            act.activation(sig.rearrange("p a b -> p (a b)"), gate.rearrange("p a b -> p (a b)"), ACT.Sigmoid)\
                .then_inc(sem("sigmoid"), 1)

        @block.gpsimd
        def _(pool):
            pool.sem_inc(sem("c_add_g"), 2)
            pool.sem_inc(sem("s_add"), 4)
            pool.sem_inc(sem("s_o"), 1)
            pool.memset(zeros16[:, :], 0.0).then_inc(sem("zeros"), 1)
            pool.wait_ge(sem("zeros"), 1)
            pool.memset(shift_rows[:, :], 0.0).then_inc(sem("zeros"), 1)
            pool.wait_ge(sem("zeros"), 2)
            pool.memset(v0.rearrange("p a b -> p (a b)"), 1.0).then_inc(sem("v0_ones"), 1)
            pool.wait_ge(sem("v0_ones"), 1)

            pool.wait_ge(sem("const_in"), 16 * 5)
            j = len(FIRST0)
            for n in range(len(FIRST0), len(ITEMS0)):
                if ITEMS0[n][0] != "v":
                    pool.wait_ge(sem("item_hi"), j + 1)
                    subtract_hi(pool, n, j).then_inc(sem("item_split"), 1)
                    j += 1
                    pool.wait_ge(sem("item_split"), j)
            for g in range(1, G0):
                pool.tensor_scalar(k0[:, g * CTXP + CTX:(g + 1) * CTXP], zeros16[:, 0:CTXP - CTX], col(C_PAD0), None, ALU.add)\
                    .then_inc(sem("k0_pad_others"), 1)
                pool.wait_ge(sem("k0_pad_others"), g)

            pool.wait_ge(sem("m0_turned"), 8)
            pool.memset(shift_rows[:, :], 0.0).then_inc(sem("shift_zero"), 1)
            pool.wait_ge(sem("shift_zero"), 1)
            pool.memset(shift_rows[:, 0:8 * 32].rearrange("p (t r) -> p t r", r=32)[:, :, 3], 1.0).then_inc(sem("shift_zero"), 1)
            pool.wait_ge(sem("shift_zero"), 2)
            pool.wait_ge(sem("o0_mm"), 51 * 8 + 3)
            pool.memset(q2[96:128, :], 0.0).then_inc(sem("q2_zero"), 1)
            pool.wait_ge(sem("q2_zero"), 1)
            for i in range(PCH):
                pool.wait_ge(sem("k1_hi"), i + 1)
                s = slice(i * HALF, i * HALF + PW[i])
                pool.tensor_tensor(k2[0:64, s], k_tmp[i % 2][:, 0:PW[i]], k1[0:64, s], ALU.subtract).then_inc(sem("k1_split"), 1)
                pool.wait_ge(sem("k1_split"), i + 1)

            pool.wait_ge(sem("ff_done"), 8)
            pool.memset(probs[:, 1, 0:P], 0.0).then_inc(sem("p1_zero"), 1)
            pool.wait_ge(sem("p1_zero"), 1)

            def normalise_s(h, odd):
                pool.wait_ge(sem("s_recip"), 2 * h + 2 + 2)
                pool.wait_ge(sem("s_evac"), h + 1 + 1)
                divide(pool, h, odd, sem("s_o"))
                pool.wait_ge(sem("s_o"), h + 1 + 1)

            def head_s(h, odd, first=False):
                acc = accs[:, ds(h % 2, 1), :].rearrange("p a b -> p (a b)")
                pool.wait_ge(sem("ps_exp"), 8 * h + 1 + 3)
                pool.wait_ge(sem("s_sums"), h + 1)
                pool.tensor_tensor(acc, probs[:, 0, :], probs[:, 1, :], ALU.add).then_inc(sem("s_add"), 2)
                for t in range(2, NT):
                    pool.wait_ge(sem("ps_exp"), 8 * h + t + 3)
                    pool.wait_ge(sem("s_add"), 8 * h + t + 4)
                    part = accs[:, ds(h % 2, 1), P * t:T].rearrange("p a b -> p (a b)")
                    pool.tensor_tensor(part, part, p_slot(t)[:, P * t:T], ALU.add).then_inc(sem("s_add"), 1)
                    if t == 5 and not first:
                        pool.wait_ge(sem("s_add"), 8 * h + t + 1 + 4)
                        normalise_s(h - 1, 1 - odd)

            head_s(0, 0, first=True)
            with pool.Fori(0, H // 2 - 1) as n:
                head_s(2 * n + 1, 1)
                head_s(2 * n + 2, 0)
            head_s(H - 1, 1)
            normalise_s(H - 1, 1)

            for i in range(2 * H):
                pool.wait_ge(sem("qc_hi"), i + 1)
                lo = q1[64:128, i * HALF:(i + 1) * HALF]
                pool.tensor_tensor(lo, y_tmp[i % 2][64:128, :], lo, ALU.subtract).then_inc(sem("qc_split"), 1)
                pool.wait_ge(sem("qc_split"), i + 1)

            def add_g(h, n, u):
                pool.wait_ge(sem("p1_exp"), 51 * h + 3 * n + u + 3)
                pool.wait_ge(sem("c_add_g"), 33 * h + 2 * n + u - 1 + 2)
                pool.tensor_tensor(acc_g, acc_g, probs[:, u, :], ALU.add).then_inc(sem("c_add_g"), 1)

            with pool.Fori(0, H) as h:
                pool.wait_ge(sem("p1_exp"), 51 * h + 2 + 3)
                pool.wait_ge(sem("c_sums"), h + 1)
                pool.tensor_tensor(acc_g, probs[:, 1, :], probs[:, 2, :], ALU.add).then_inc(sem("c_add_g"), 2)
                with pool.Fori(1, KT // 3 - 1) as n:
                    add_g(h, n, 1)
                    add_g(h, n, 2)
                add_g(h, KT // 3 - 1, 1)

            for n in range(5):
                pool.wait_ge(sem("q_amax"), n + 1)
                pool.partition_all_reduce(y_tmp[0][:, 136 + n:137 + n], y_tmp[0][:, 128 + n:129 + n], P, RMAX)\
                    .then_inc(sem("q_gmax"), 1)


def laid_out(i):
    f = {k: np.ascontiguousarray(v) for k, v in i.items()}
    z = lambda *s: np.zeros(s, np.float32)
    o = {"x": f["x"].reshape(T, D)}
    ctx_rows = z(CTXP, D)
    ctx_rows[:CTX] = f["ctx_1024"][0]
    o["ctx"] = ctx_rows
    o["ctx_t"] = np.ascontiguousarray(ctx_rows.T)
    cols = z(P, 34)
    wk, wq, wo = z(P, G0, P), z(P, H, P), z(P, G0, P)
    wkt, wqt, wot = f["L0_xattn_Wk"].T, f["L0_xattn_Wq"].T, f["L0_xattn_Wo"].T
    for h in range(H):
        g, j = divmod(h, 4)
        s = slice(h * HD0, (h + 1) * HD0)
        for r in range(3):
            d = slice(32 * j + 8 * r, 32 * j + 8 * r + 8)
            wk[:, g, d] = wkt[:, s]
            wq[:, h, d] = wqt[:, s]
            cols[d, g] = f["L0_xattn_bk"][s]
            cols[d, 4 + h] = f["L0_xattn_bq"][s]
        cols[32 * j + ROW_SHIFT0:32 * j + ROW_SHIFT0 + 3, g] = 1
        cols[32 * j + ROW_PAD0, 4 + h] = 1
        wo[32 * j:32 * j + 8, g, :] = wot[s]
    r = np.arange(P) % 32
    cols[:, 20] = np.where(r < ROW_SHIFT0, np.float32(1 / np.sqrt(HD0)), 1)
    cols[:, 21] = (r >= 16) & (r < 24)
    cols[:, 22] = (r >= 8) & (r < 16)
    cols[:, 23] = np.where(r == ROW_PAD0, PAD_SCORE, 0)
    k2_rows = np.zeros((HD1, CTXP), np.float16)
    k2_rows[0:3] = 1
    k2_rows[ROW_PAD1 - HD1, CTX:] = PAD_SCORE
    o["k2_rows"] = k2_rows
    cols[:, 27] = f["L1_xattn_ptb_gamma"]
    cols[:, 28] = f["L1_xattn_ca_ctx_gamma"]
    cols[:, 29] = f["L1_xattn_ca_gamma"]
    o["cols"] = cols
    o["wk0"], o["wq0"], o["wo0"] = wk, wq, wo
    o["wv0"] = np.ascontiguousarray(f["L0_xattn_Wv"].T)
    o["rows0"] = np.concatenate([f["L0_xattn_bv"], f["L0_xattn_bo"]])[None]
    o["wg0"] = f["L0_ffn_Wg"]
    o["moe_a"] = np.ascontiguousarray(f["L0_ffn_A"].transpose(1, 0, 2).reshape(D, E * R))
    o["moe_b"] = f["L0_ffn_B"].reshape(E * R, D)
    sel = z(P, P)
    for j in range(4):
        sel[32 * j + 8, 32 * j:32 * j + 32] = 1
    o["sel_sum"] = sel
    o["ident"] = np.eye(P, dtype=np.float32)
    o["ones"] = np.ones((P, P), np.float32)
    o["ident16"] = np.eye(P, dtype=np.float16)
    k, q = np.arange(P)[:, None], np.arange(P)[None]
    o["masks"] = np.concatenate([np.where(k > q, MASKED, 0), np.where(k < q, MASKED, 0)], 1).astype(np.float32)

    wf = f["L1_xattn_W_fused"]
    inner = H * HD1

    def twice(w):
        w = w.reshape(D, H, 1, HD1)
        return np.ascontiguousarray(np.broadcast_to(w, (D, H, 2, HD1)).reshape(D, H, P))

    def kkv(w):
        return np.concatenate([w[:, :HD1], w[:, :HD1], w[:, HD1:]], 1)

    def pairs(w):
        return w.reshape(H // 2, P, D).transpose(1, 0, 2)

    o["wq_s"] = twice(wf[:, :inner])
    o["wkv_s"] = kkv(wf[:, inner:inner + 2 * HD1])
    o["wff"] = np.ascontiguousarray(wf[:, inner + 2 * HD1:])
    o["wffo"] = np.ascontiguousarray(f["L1_xattn_W_ff_out"].reshape(FFI // P, P, D).transpose(1, 0, 2))
    o["wo_s"] = pairs(f["L1_xattn_W_attn_out"])
    o["wq_c"] = twice(f["L1_xattn_W_q"])
    o["wkv_c"] = kkv(f["L1_xattn_W_kv"])
    o["wo_c"] = pairs(f["L1_xattn_W_out"])
    rows = lambda w: w.reshape(3, P, D).transpose(1, 0, 2)
    o["qw"] = np.ascontiguousarray(np.stack([rows(f["L1_ffn_w_gate"]), rows(f["L1_ffn_w_up"]),
                                             f["L1_ffn_w_down"].reshape(D, 3, P)], 1))
    return {k: np.ascontiguousarray(v) for k, v in o.items()}


def kernel(**inputs):
    import concourse.bacc as bacc
    from concourse.bass_utils import run_bass_kernel_spmd

    arrays = laid_out(inputs)
    nc = bacc.Bacc("TRN2", target_bir_lowering=False, num_devices=1)
    args = {k: nc.dram_tensor("in_" + k, v.shape, mybir.dt.from_np(v.dtype), kind="ExternalInput").ap()
            for k, v in arrays.items()}
    out = nc.dram_tensor("out_x", (T, D), F32, kind="ExternalOutput").ap()
    build(nc, args, out)
    r = run_bass_kernel_spmd(nc, [{"in_" + k: v for k, v in arrays.items()}], core_ids=[0])
    return r.results[0]["out_x"].reshape(1, T, D)
```
